# Optimizing a Trainium2 kernel written in Bass

```python
import numpy as np
import jax
import jax.numpy as jnp

def _softmax(x, axis=-1):
    return jax.nn.softmax(x, axis=axis)

def _gelu(x):
    return jax.nn.gelu(x, approximate=True)

def _silu(x):
    return jax.nn.silu(x)

def _sigmoid(x):
    return jax.nn.sigmoid(x)

def _layernorm(x, axis=-1, eps=1e-05):
    m = jnp.mean(x, axis=axis, keepdims=True)
    v = jnp.var(x, axis=axis, keepdims=True)
    return (x - m) / jnp.sqrt(v + eps)

def _scatter_add(tgt, idx, src, axis=0):
    return tgt.at[idx].add(src)

def _segment_sum(src, seg, n):
    return jax.ops.segment_sum(src, seg, n)
kernel_name = 'mk_flamingo_gated_d4_seqx_r8_b9ae39'

def setup_inputs(seed: int=0):
    np.random.seed(seed)
    _w = jnp.asarray

    def _rec_inputs():
        import jax
        import jax.numpy as jnp
        _rk = jax.random.key(seed)
        x = -0.0003929 + 0.9999 * jax.random.normal(jax.random.fold_in(_rk, 1), (8, 56, 128), jnp.float32)
        _lenS = 56 - jax.random.randint(jax.random.fold_in(_rk, 7), (8,), 0, max(1, 56 // 4) + 1, jnp.int32)
        _lenS2 = 1500 - jax.random.randint(jax.random.fold_in(_rk, 8), (8,), 0, max(1, 1500 // 4) + 1, jnp.int32)
        _ctx_1024P = jax.random.normal(jax.random.fold_in(_rk, 11), (8, 16, 128), jnp.float32)
        _ctx_1024c = jax.random.dirichlet(jax.random.fold_in(_rk, 511), 0.3 * jnp.ones((16,), jnp.float32), (8, 1500))
        _ctx_1024t = jnp.einsum('bsk,bkd->bsd', _ctx_1024c, _ctx_1024P)
        _ctx_1024t = _ctx_1024t * jax.lax.rsqrt(jnp.mean(jnp.square(_ctx_1024t)) + 1e-12) * 0.953939
        ctx_1024 = 2.81802e-05 + 1.00001 * (_ctx_1024t + 0.3 * jax.random.normal(jax.random.fold_in(_rk, 611), (8, 1500, 128), jnp.float32))
        _validS = jnp.arange(56)[None, :] < _lenS[:, None]
        _validS2 = jnp.arange(1500)[None, :] < _lenS2[:, None]
        _causal = jnp.tril(jnp.ones((56, 56), dtype=bool))
        mask_BxS2_ff1 = jnp.where(jnp.ones((8, 1500), dtype=bool), 1.0, 0.0).astype(jnp.float32)
        mask_BxS2_bk0 = jnp.logical_not(jnp.broadcast_to(_validS2[:, :], (8, 1500)))
        _g = jax.random.normal(jax.random.fold_in(_rk, 9001), (2, 4), jnp.float32)
        _g = jnp.sign(_g) * jnp.maximum(jnp.abs(_g), 1.0) + (_g == 0) * 1.0
        g_xattn = _g[0]
        g_ffn = _g[1]
        return (x, ctx_1024, mask_BxS2_ff1, mask_BxS2_bk0, g_xattn, g_ffn)
    x, ctx_1024, mask_BxS2_ff1, mask_BxS2_bk0, g_xattn, g_ffn = _rec_inputs()

    def _L0_xattn_setup():
        import jax, jax.numpy as jnp
        import numpy as np
        D_MODEL = 128
        HEADS = 16
        DEPTH = D_MODEL // HEADS
        B, S = (4, 512)
        EPS_K = 1e-06
        EPS_LN = 1e-06

        def _layernorm(x, g, b):
            m = jnp.mean(x, axis=-1, keepdims=True)
            var = jnp.var(x, axis=-1, keepdims=True)
            return (x - m) * jax.lax.rsqrt(var + EPS_LN) * g + b

        def _split_heads(x):
            bsz, sl, _ = x.shape
            return x.reshape(bsz, sl, HEADS, DEPTH).transpose(0, 2, 1, 3)
        key = jax.random.key(seed)
        ks = jax.random.split(key, 8)
        lecun = 1.0 / np.sqrt(D_MODEL)
        glorot = np.sqrt(2.0 / (D_MODEL + D_MODEL))
        return {'q': jax.random.normal(ks[0], (B, S, D_MODEL), jnp.float32), 'k': jax.random.normal(ks[1], (B, S, D_MODEL), jnp.float32), 'v': jax.random.normal(ks[2], (B, S, D_MODEL), jnp.float32), 'mask': jnp.ones((B, S), jnp.float32), 'wq': jax.random.normal(ks[3], (D_MODEL, D_MODEL), jnp.float32) * lecun, 'wk': jax.random.normal(ks[4], (D_MODEL, D_MODEL), jnp.float32) * lecun, 'wv': jax.random.normal(ks[5], (D_MODEL, D_MODEL), jnp.float32) * lecun, 'ln_gamma': jnp.ones((D_MODEL,), jnp.float32), 'ln_beta': jnp.zeros((D_MODEL,), jnp.float32), 'dense_w': jax.random.normal(ks[6], (D_MODEL, D_MODEL), jnp.float32) * glorot, 'dense_b': jnp.zeros((D_MODEL,), jnp.float32)}
    _L0_xattn_all = _L0_xattn_setup()
    _L0_xattn_in = {k: v for k, v in _L0_xattn_all.items() if k in ('wq', 'wk', 'wv', 'ln_gamma', 'ln_beta', 'dense_w', 'dense_b')}
    del _L0_xattn_all

    def _L0_ffn_setup():
        import jax, jax.numpy as jnp
        import numpy as np
        HIDDEN = 128
        INNER = 512

        def _weight_quant(w):
            scale = 1.0 / jnp.clip(jnp.mean(jnp.abs(w)), 1e-05)
            wq = jnp.clip(jnp.round(w * scale), -1.0, 1.0) / scale
            return w + jax.lax.stop_gradient(wq - w)

        def _act_quant(x):
            scale = 127.0 / jnp.clip(jnp.max(jnp.abs(x), axis=-1, keepdims=True), 1e-05)
            xq = jnp.clip(jnp.round(x * scale), -128.0, 127.0) / scale
            return x + jax.lax.stop_gradient(xq - x)

        def _bitlinear(x, w):
            return jnp.einsum('bsi,oi->bso', _act_quant(x), _weight_quant(w))
        key = jax.random.key(seed)
        k0, k1, k2, k3 = jax.random.split(key, 4)
        x = jax.random.normal(k0, (4, 256, HIDDEN), dtype=jnp.float32)
        w_gate = jax.random.normal(k1, (INNER, HIDDEN), dtype=jnp.float32) / np.sqrt(HIDDEN)
        w_up = jax.random.normal(k2, (INNER, HIDDEN), dtype=jnp.float32) / np.sqrt(HIDDEN)
        w_down = jax.random.normal(k3, (HIDDEN, INNER), dtype=jnp.float32) / np.sqrt(INNER)
        return {'x': x, 'w_gate': w_gate, 'w_up': w_up, 'w_down': w_down}
    _L0_ffn_all = _L0_ffn_setup()
    _L0_ffn_in = {k: v for k, v in _L0_ffn_all.items() if k in ('w_gate', 'w_up', 'w_down')}
    del _L0_ffn_all

    def _L1_xattn_setup():
        import jax, jax.numpy as jnp
        import numpy as np
        EMBED_DIM = 128
        NUM_HEADS = 16
        HEAD_DIM = EMBED_DIM // NUM_HEADS
        WINDOW = 64

        def apply_rope(x):
            B, H, S, d = x.shape
            half = d // 2
            pos = jnp.arange(S, dtype=x.dtype)
            freqs = 1.0 / 10000.0 ** (jnp.arange(half, dtype=x.dtype) / half)
            ang = pos[:, None] * freqs[None, :]
            cos, sin = (jnp.cos(ang), jnp.sin(ang))
            x1, x2 = (x[..., :half], x[..., half:])
            return jnp.concatenate([x1 * cos - x2 * sin, x1 * sin + x2 * cos], axis=-1)

        def _forward(query, key, value, q_w, q_b, k_w, k_b, v_w, v_b, o_w, o_b):
            B, S_q, D = query.shape
            S_k = key.shape[1]
            H, d, W = (NUM_HEADS, HEAD_DIM, WINDOW)
            q = (query @ q_w.T + q_b).reshape(B, S_q, H, d).transpose(0, 2, 1, 3)
            k = (key @ k_w.T + k_b).reshape(B, S_k, H, d).transpose(0, 2, 1, 3)
            v = (value @ v_w.T + v_b).reshape(B, S_k, H, d).transpose(0, 2, 1, 3)
            q = apply_rope(q) * d ** (-0.5)
            k = apply_rope(k)
            q_pos = jnp.arange(S_q)[:, None]
            offsets = jnp.arange(-W, 1)[None, :]
            idx = q_pos + offsets
            local_mask = (idx < 0) | (idx >= S_k)
            gidx = jnp.clip(idx, 0, S_k - 1)
            k_win = k[:, :, gidx, :]
            v_win = v[:, :, gidx, :]
            scores = jnp.einsum('bhqd,bhqwd->bhqw', q, k_win)
            mask = local_mask[None, None, :, :]
            scores = jnp.where(mask, -jnp.inf, scores)
            m = jnp.max(scores, axis=-1, keepdims=True)
            m = jnp.where(jnp.isfinite(m), m, 0.0)
            e = jnp.exp(scores - m)
            denom = jnp.sum(e, axis=-1, keepdims=True)
            probs = jnp.where(denom > 0, e / jnp.where(denom > 0, denom, 1.0), 0.0)
            ctx = jnp.einsum('bhqw,bhqwd->bhqd', probs, v_win)
            ctx = ctx.transpose(0, 2, 1, 3).reshape(B, S_q, D)
            return ctx @ o_w.T + o_b
        key = jax.random.key(seed)
        ks = jax.random.split(key, 12)
        B, S, D = (1, 256, EMBED_DIM)
        scale = 1.0 / np.sqrt(D)
        inp = {'query': jax.random.normal(ks[0], (B, S, D), jnp.float32), 'key': jax.random.normal(ks[1], (B, S, D), jnp.float32), 'value': jax.random.normal(ks[2], (B, S, D), jnp.float32), 'q_w': jax.random.normal(ks[3], (D, D), jnp.float32) * scale, 'q_b': jax.random.normal(ks[4], (D,), jnp.float32) * 0.01, 'k_w': jax.random.normal(ks[5], (D, D), jnp.float32) * scale, 'k_b': jax.random.normal(ks[6], (D,), jnp.float32) * 0.01, 'v_w': jax.random.normal(ks[7], (D, D), jnp.float32) * scale, 'v_b': jax.random.normal(ks[8], (D,), jnp.float32) * 0.01, 'o_w': jax.random.normal(ks[9], (D, D), jnp.float32) * scale, 'o_b': jax.random.normal(ks[10], (D,), jnp.float32) * 0.01}
        return inp
    _L1_xattn_all = _L1_xattn_setup()
    _L1_xattn_in = {k: v for k, v in _L1_xattn_all.items() if k in ('q_w', 'q_b', 'k_w', 'k_b', 'v_w', 'v_b', 'o_w', 'o_b')}
    del _L1_xattn_all

    def _L1_ffn_setup():
        import jax, jax.numpy as jnp
        import numpy as np
        D_MODEL = 128
        N_EXPERTS = 16
        TOP_K = 2
        EXPERT_DIM = 128
        SHARED_DIM = 256
        B, T = (2, 128)
        key = jax.random.key(seed)
        ks = jax.random.split(key, 7)
        std = 0.02
        return {'x': jax.random.normal(ks[0], (B, T, D_MODEL), dtype=jnp.float32), 'router_w': jax.random.normal(ks[1], (N_EXPERTS, D_MODEL), dtype=jnp.float32) * std, 'gate_up_w': jax.random.normal(ks[2], (N_EXPERTS, D_MODEL, 2 * EXPERT_DIM), dtype=jnp.float32) * std, 'down_w': jax.random.normal(ks[3], (N_EXPERTS, EXPERT_DIM, D_MODEL), dtype=jnp.float32) * std, 'shared_gate_w': jax.random.normal(ks[4], (SHARED_DIM, D_MODEL), dtype=jnp.float32) * std, 'shared_up_w': jax.random.normal(ks[5], (SHARED_DIM, D_MODEL), dtype=jnp.float32) * std, 'shared_down_w': jax.random.normal(ks[6], (D_MODEL, SHARED_DIM), dtype=jnp.float32) * std}
    _L1_ffn_all = _L1_ffn_setup()
    _L1_ffn_in = {k: v for k, v in _L1_ffn_all.items() if k in ('router_w', 'gate_up_w', 'down_w', 'shared_gate_w', 'shared_up_w', 'shared_down_w')}
    del _L1_ffn_all

    def _L2_xattn_setup():
        import jax, jax.numpy as jnp
        import numpy as np
        DIM, DIM_HEAD, HEADS, SCALE = (128, 64, 8, 8.0)
        INNER = DIM_HEAD * HEADS
        LN_EPS = 1e-05
        L2_EPS = 1e-12

        def layer_norm(x, w, b):
            mu = jnp.mean(x, axis=-1, keepdims=True)
            var = jnp.mean(jnp.square(x - mu), axis=-1, keepdims=True)
            return (x - mu) * jax.lax.rsqrt(var + LN_EPS) * w + b

        def l2norm(t):
            n = jnp.sqrt(jnp.sum(jnp.square(t), axis=-1, keepdims=True))
            return t / jnp.maximum(n, L2_EPS)
        key = jax.random.key(seed)
        ks = jax.random.split(key, 8)
        b, n, m = (8, 1024, 64)
        x = jax.random.normal(ks[0], (b, n, DIM), dtype=jnp.float32)
        latents = jax.random.normal(ks[1], (b, m, DIM), dtype=jnp.float32)
        mask = jax.random.randint(ks[2], (b, n), 0, 2) > 0
        Wq = jax.random.normal(ks[3], (DIM, INNER), dtype=jnp.float32) * DIM ** (-0.5)
        Wkv = jax.random.normal(ks[4], (DIM, 2 * INNER), dtype=jnp.float32) * DIM ** (-0.5)
        Wo = jax.random.normal(ks[5], (INNER, DIM), dtype=jnp.float32) * INNER ** (-0.5)
        return {'x': x, 'latents': latents, 'mask': mask, 'ln_x_w': jnp.ones((DIM,)), 'ln_x_b': jnp.zeros((DIM,)), 'ln_l_w': jnp.ones((DIM,)), 'ln_l_b': jnp.zeros((DIM,)), 'Wq': Wq, 'Wkv': Wkv, 'q_scale': jnp.ones((DIM_HEAD,)), 'k_scale': jnp.ones((DIM_HEAD,)), 'Wo': Wo, 'ln_o_w': jnp.ones((DIM,)), 'ln_o_b': jnp.zeros((DIM,))}
    _L2_xattn_all = _L2_xattn_setup()
    _L2_xattn_in = {k: v for k, v in _L2_xattn_all.items() if k in ('ln_x_w', 'ln_x_b', 'ln_l_w', 'ln_l_b', 'Wq', 'Wkv', 'q_scale', 'k_scale', 'Wo', 'ln_o_w', 'ln_o_b')}
    del _L2_xattn_all

    def _L2_ffn_setup():
        import jax, jax.numpy as jnp
        import numpy as np
        EPS = 1e-05

        def act_quant(x):
            scale = 127.0 / jnp.clip(jnp.max(jnp.abs(x), axis=-1, keepdims=True), EPS, None)
            xq = jnp.clip(jnp.round(x * scale), -128.0, 127.0)
            return (xq, scale)

        def weight_quant(w):
            scale = 1.0 / jnp.clip(jnp.mean(jnp.abs(w)), EPS, None)
            wq = jnp.clip(jnp.round(w * scale), -1.0, 1.0)
            return (wq, scale)

        def qlinear(x, w, b):
            xq, sx = act_quant(x)
            wq, sw = weight_quant(w)
            y = jnp.einsum('bsd,hd->bsh', xq, wq) / (sx * sw)
            return y + b

        def layernorm(x, gamma, beta):
            mu = jnp.mean(x, axis=-1, keepdims=True)
            var = jnp.mean(jnp.square(x - mu), axis=-1, keepdims=True)
            return (x - mu) * jax.lax.rsqrt(var + EPS) * gamma + beta
        key = jax.random.key(seed)
        ks = jax.random.split(key, 6)
        dim, hidden = (128, 512)
        B, S = (4, 256)
        x = jax.random.normal(ks[0], (B, S, dim), dtype=jnp.float32)
        w1 = jax.random.normal(ks[1], (hidden, dim), dtype=jnp.float32) * (1.0 / np.sqrt(dim))
        b1 = jnp.zeros((hidden,), dtype=jnp.float32)
        w2 = jax.random.normal(ks[2], (dim, hidden), dtype=jnp.float32) * (1.0 / np.sqrt(hidden))
        b2 = jnp.zeros((dim,), dtype=jnp.float32)
        gamma = jnp.ones((dim,), dtype=jnp.float32)
        beta = jnp.zeros((dim,), dtype=jnp.float32)
        return {'x': x, 'w1': w1, 'b1': b1, 'w2': w2, 'b2': b2, 'gamma': gamma, 'beta': beta}
    _L2_ffn_all = _L2_ffn_setup()
    _L2_ffn_in = {k: v for k, v in _L2_ffn_all.items() if k in ('w1', 'b1', 'w2', 'b2', 'gamma', 'beta')}
    del _L2_ffn_all

    def _L3_xattn_setup():
        import jax, jax.numpy as jnp
        import numpy as np
        EMBED = 128
        HEADS = 16
        HEAD_DIM = EMBED // HEADS
        key = jax.random.key(seed)
        ks = jax.random.split(key, 8)
        B, S, D = (4, 256, EMBED)
        s = 1.0 / np.sqrt(D)
        return {'values': jax.random.normal(ks[0], (B, S, D), jnp.float32), 'keys': jax.random.normal(ks[1], (B, S, D), jnp.float32), 'query': jax.random.normal(ks[2], (B, S, D), jnp.float32), 'Wv': jax.random.normal(ks[3], (D, D), jnp.float32) * s, 'Wk': jax.random.normal(ks[4], (D, D), jnp.float32) * s, 'Wq': jax.random.normal(ks[5], (D, D), jnp.float32) * s, 'Wo': jax.random.normal(ks[6], (D, D), jnp.float32) * s, 'bo': jax.random.normal(ks[7], (D,), jnp.float32) * 0.01}
    _L3_xattn_all = _L3_xattn_setup()
    _L3_xattn_in = {k: v for k, v in _L3_xattn_all.items() if k in ('Wv', 'Wk', 'Wq', 'Wo', 'bo')}
    del _L3_xattn_all

    def _L3_ffn_setup():
        import jax, jax.numpy as jnp
        import numpy as np
        H = 128
        F = 512
        E = 8
        TOP_K = 2
        B, S = (1, 256)
        key = jax.random.key(seed)
        k0, k1, k2, k3 = jax.random.split(key, 4)
        hidden_states = jax.random.normal(k0, (B, S, H), dtype=jnp.float32)
        gate_w = jax.random.normal(k1, (E, H), dtype=jnp.float32) * 0.02
        gate_up_w = jax.random.normal(k2, (E, 2 * F, H), dtype=jnp.float32) * 0.02
        down_w = jax.random.normal(k3, (E, H, F), dtype=jnp.float32) * 0.02
        return {'hidden_states': hidden_states, 'gate_w': gate_w, 'gate_up_w': gate_up_w, 'down_w': down_w}
    _L3_ffn_all = _L3_ffn_setup()
    _L3_ffn_in = {k: v for k, v in _L3_ffn_all.items() if k in ('gate_w', 'gate_up_w', 'down_w')}
    del _L3_ffn_all
    return {'x': x, 'ctx_1024': ctx_1024, 'mask_BxS2_ff1': mask_BxS2_ff1, 'mask_BxS2_bk0': mask_BxS2_bk0, 'g_xattn': g_xattn, 'g_ffn': g_ffn, 'L0_xattn_wq': _L0_xattn_in['wq'], 'L0_xattn_wk': _L0_xattn_in['wk'], 'L0_xattn_wv': _L0_xattn_in['wv'], 'L0_xattn_ln_gamma': _L0_xattn_in['ln_gamma'], 'L0_xattn_ln_beta': _L0_xattn_in['ln_beta'], 'L0_xattn_dense_w': _L0_xattn_in['dense_w'], 'L0_xattn_dense_b': _L0_xattn_in['dense_b'], 'L0_ffn_w_gate': _L0_ffn_in['w_gate'], 'L0_ffn_w_up': _L0_ffn_in['w_up'], 'L0_ffn_w_down': _L0_ffn_in['w_down'], 'L1_xattn_q_w': _L1_xattn_in['q_w'], 'L1_xattn_q_b': _L1_xattn_in['q_b'], 'L1_xattn_k_w': _L1_xattn_in['k_w'], 'L1_xattn_k_b': _L1_xattn_in['k_b'], 'L1_xattn_v_w': _L1_xattn_in['v_w'], 'L1_xattn_v_b': _L1_xattn_in['v_b'], 'L1_xattn_o_w': _L1_xattn_in['o_w'], 'L1_xattn_o_b': _L1_xattn_in['o_b'], 'L1_ffn_router_w': _L1_ffn_in['router_w'], 'L1_ffn_gate_up_w': _L1_ffn_in['gate_up_w'], 'L1_ffn_down_w': _L1_ffn_in['down_w'], 'L1_ffn_shared_gate_w': _L1_ffn_in['shared_gate_w'], 'L1_ffn_shared_up_w': _L1_ffn_in['shared_up_w'], 'L1_ffn_shared_down_w': _L1_ffn_in['shared_down_w'], 'L2_xattn_ln_x_w': _L2_xattn_in['ln_x_w'], 'L2_xattn_ln_x_b': _L2_xattn_in['ln_x_b'], 'L2_xattn_ln_l_w': _L2_xattn_in['ln_l_w'], 'L2_xattn_ln_l_b': _L2_xattn_in['ln_l_b'], 'L2_xattn_Wq': _L2_xattn_in['Wq'], 'L2_xattn_Wkv': _L2_xattn_in['Wkv'], 'L2_xattn_q_scale': _L2_xattn_in['q_scale'], 'L2_xattn_k_scale': _L2_xattn_in['k_scale'], 'L2_xattn_Wo': _L2_xattn_in['Wo'], 'L2_xattn_ln_o_w': _L2_xattn_in['ln_o_w'], 'L2_xattn_ln_o_b': _L2_xattn_in['ln_o_b'], 'L2_ffn_w1': _L2_ffn_in['w1'], 'L2_ffn_b1': _L2_ffn_in['b1'], 'L2_ffn_w2': _L2_ffn_in['w2'], 'L2_ffn_b2': _L2_ffn_in['b2'], 'L2_ffn_gamma': _L2_ffn_in['gamma'], 'L2_ffn_beta': _L2_ffn_in['beta'], 'L3_xattn_Wv': _L3_xattn_in['Wv'], 'L3_xattn_Wk': _L3_xattn_in['Wk'], 'L3_xattn_Wq': _L3_xattn_in['Wq'], 'L3_xattn_Wo': _L3_xattn_in['Wo'], 'L3_xattn_bo': _L3_xattn_in['bo'], 'L3_ffn_gate_w': _L3_ffn_in['gate_w'], 'L3_ffn_gate_up_w': _L3_ffn_in['gate_up_w'], 'L3_ffn_down_w': _L3_ffn_in['down_w']}

def reference(x, ctx_1024, mask_BxS2_ff1, mask_BxS2_bk0, g_xattn, g_ffn, L0_xattn_wq, L0_xattn_wk, L0_xattn_wv, L0_xattn_ln_gamma, L0_xattn_ln_beta, L0_xattn_dense_w, L0_xattn_dense_b, L0_ffn_w_gate, L0_ffn_w_up, L0_ffn_w_down, L1_xattn_q_w, L1_xattn_q_b, L1_xattn_k_w, L1_xattn_k_b, L1_xattn_v_w, L1_xattn_v_b, L1_xattn_o_w, L1_xattn_o_b, L1_ffn_router_w, L1_ffn_gate_up_w, L1_ffn_down_w, L1_ffn_shared_gate_w, L1_ffn_shared_up_w, L1_ffn_shared_down_w, L2_xattn_ln_x_w, L2_xattn_ln_x_b, L2_xattn_ln_l_w, L2_xattn_ln_l_b, L2_xattn_Wq, L2_xattn_Wkv, L2_xattn_q_scale, L2_xattn_k_scale, L2_xattn_Wo, L2_xattn_ln_o_w, L2_xattn_ln_o_b, L2_ffn_w1, L2_ffn_b1, L2_ffn_w2, L2_ffn_b2, L2_ffn_gamma, L2_ffn_beta, L3_xattn_Wv, L3_xattn_Wk, L3_xattn_Wq, L3_xattn_Wo, L3_xattn_bo, L3_ffn_gate_w, L3_ffn_gate_up_w, L3_ffn_down_w):
    import jax
    import jax.numpy as jnp

    def _L0_xattn_ref(q, k, v, mask, wq, wk, wv, ln_gamma, ln_beta, dense_w, dense_b):
        import jax, jax.numpy as jnp
        import numpy as np
        D_MODEL = 128
        HEADS = 16
        DEPTH = D_MODEL // HEADS
        B, S = (4, 512)
        EPS_K = 1e-06
        EPS_LN = 1e-06

        def _layernorm(x, g, b):
            m = jnp.mean(x, axis=-1, keepdims=True)
            var = jnp.var(x, axis=-1, keepdims=True)
            return (x - m) * jax.lax.rsqrt(var + EPS_LN) * g + b

        def _split_heads(x):
            bsz, sl, _ = x.shape
            return x.reshape(bsz, sl, HEADS, DEPTH).transpose(0, 2, 1, 3)
        bsz = q.shape[0]
        em = mask[:, None, :, None]
        qh = _split_heads(_layernorm(q @ wq, ln_gamma, ln_beta))
        kh = _split_heads(_layernorm(k @ wk, ln_gamma, ln_beta))
        vh = _split_heads(_layernorm(v @ wv, ln_gamma, ln_beta))
        q_prime = jax.nn.relu(qh) + EPS_K
        k_prime = (jax.nn.relu(kh) + EPS_K) * em
        vh = vh * em
        kv = jnp.einsum('bhnd,bhne->bhde', k_prime, vh)
        z = 1.0 / (jnp.einsum('bhnd,bhd->bhn', q_prime, k_prime.sum(axis=-2)) + EPS_K)
        att = jnp.einsum('bhnd,bhde,bhn->bhne', q_prime, kv, z)
        att = att.reshape(bsz, -1, D_MODEL)
        out = att @ dense_w + dense_b
        return _layernorm(out, ln_gamma, ln_beta)

    def _L0_ffn_ref(x, w_gate, w_up, w_down):
        import jax, jax.numpy as jnp
        import numpy as np
        HIDDEN = 128
        INNER = 512

        def _weight_quant(w):
            scale = 1.0 / jnp.clip(jnp.mean(jnp.abs(w)), 1e-05)
            wq = jnp.clip(jnp.round(w * scale), -1.0, 1.0) / scale
            return w + jax.lax.stop_gradient(wq - w)

        def _act_quant(x):
            scale = 127.0 / jnp.clip(jnp.max(jnp.abs(x), axis=-1, keepdims=True), 1e-05)
            xq = jnp.clip(jnp.round(x * scale), -128.0, 127.0) / scale
            return x + jax.lax.stop_gradient(xq - x)

        def _bitlinear(x, w):
            return jnp.einsum('bsi,oi->bso', _act_quant(x), _weight_quant(w))
        gate = jax.nn.silu(_bitlinear(x, w_gate))
        up = _bitlinear(x, w_up)
        return _bitlinear(gate * up, w_down)

    def _L1_xattn_ref(query, key, value, q_w, q_b, k_w, k_b, v_w, v_b, o_w, o_b):
        import jax, jax.numpy as jnp
        import numpy as np
        EMBED_DIM = 128
        NUM_HEADS = 16
        HEAD_DIM = EMBED_DIM // NUM_HEADS
        WINDOW = 64

        def apply_rope(x):
            B, H, S, d = x.shape
            half = d // 2
            pos = jnp.arange(S, dtype=x.dtype)
            freqs = 1.0 / 10000.0 ** (jnp.arange(half, dtype=x.dtype) / half)
            ang = pos[:, None] * freqs[None, :]
            cos, sin = (jnp.cos(ang), jnp.sin(ang))
            x1, x2 = (x[..., :half], x[..., half:])
            return jnp.concatenate([x1 * cos - x2 * sin, x1 * sin + x2 * cos], axis=-1)

        def _forward(query, key, value, q_w, q_b, k_w, k_b, v_w, v_b, o_w, o_b):
            B, S_q, D = query.shape
            S_k = key.shape[1]
            H, d, W = (NUM_HEADS, HEAD_DIM, WINDOW)
            q = (query @ q_w.T + q_b).reshape(B, S_q, H, d).transpose(0, 2, 1, 3)
            k = (key @ k_w.T + k_b).reshape(B, S_k, H, d).transpose(0, 2, 1, 3)
            v = (value @ v_w.T + v_b).reshape(B, S_k, H, d).transpose(0, 2, 1, 3)
            q = apply_rope(q) * d ** (-0.5)
            k = apply_rope(k)
            q_pos = jnp.arange(S_q)[:, None]
            offsets = jnp.arange(-W, 1)[None, :]
            idx = q_pos + offsets
            local_mask = (idx < 0) | (idx >= S_k)
            gidx = jnp.clip(idx, 0, S_k - 1)
            k_win = k[:, :, gidx, :]
            v_win = v[:, :, gidx, :]
            scores = jnp.einsum('bhqd,bhqwd->bhqw', q, k_win)
            mask = local_mask[None, None, :, :]
            scores = jnp.where(mask, -jnp.inf, scores)
            m = jnp.max(scores, axis=-1, keepdims=True)
            m = jnp.where(jnp.isfinite(m), m, 0.0)
            e = jnp.exp(scores - m)
            denom = jnp.sum(e, axis=-1, keepdims=True)
            probs = jnp.where(denom > 0, e / jnp.where(denom > 0, denom, 1.0), 0.0)
            ctx = jnp.einsum('bhqw,bhqwd->bhqd', probs, v_win)
            ctx = ctx.transpose(0, 2, 1, 3).reshape(B, S_q, D)
            return ctx @ o_w.T + o_b
        return _forward(query, key, value, q_w, q_b, k_w, k_b, v_w, v_b, o_w, o_b)

    def _L1_ffn_ref(x, router_w, gate_up_w, down_w, shared_gate_w, shared_up_w, shared_down_w):
        import jax, jax.numpy as jnp
        import numpy as np
        D_MODEL = 128
        N_EXPERTS = 16
        TOP_K = 2
        EXPERT_DIM = 128
        SHARED_DIM = 256
        B, T = (2, 128)
        Bb, Tt, C = x.shape
        N = Bb * Tt
        E = gate_up_w.shape[0]
        logits = jnp.einsum('btc,ec->bte', x, router_w)
        top_vals, top_idx = jax.lax.top_k(logits, TOP_K)
        gates = jax.nn.sigmoid(top_vals)
        xf = x.reshape(N, C)
        sel = top_idx.reshape(N, TOP_K)
        gw = gates.reshape(N, TOP_K)
        w_full = jnp.zeros((N, E), dtype=x.dtype).at[jnp.arange(N)[:, None], sel].add(gw)
        gu = jnp.einsum('nc,ech->neh', xf, gate_up_w)
        gate, up = jnp.split(gu, 2, axis=-1)
        h = jax.nn.silu(gate) * up
        out_all = jnp.einsum('neh,ehc->nec', h, down_w)
        moe = jnp.einsum('ne,nec->nc', w_full, out_all).reshape(Bb, Tt, C)
        sg = jnp.einsum('btc,sc->bts', x, shared_gate_w)
        su = jnp.einsum('btc,sc->bts', x, shared_up_w)
        shared = jnp.einsum('bts,cs->btc', jax.nn.silu(sg) * su, shared_down_w)
        return moe + shared

    def _L2_xattn_ref(x, latents, mask, ln_x_w, ln_x_b, ln_l_w, ln_l_b, Wq, Wkv, q_scale, k_scale, Wo, ln_o_w, ln_o_b):
        import jax, jax.numpy as jnp
        import numpy as np
        DIM, DIM_HEAD, HEADS, SCALE = (128, 64, 8, 8.0)
        INNER = DIM_HEAD * HEADS
        LN_EPS = 1e-05
        L2_EPS = 1e-12

        def layer_norm(x, w, b):
            mu = jnp.mean(x, axis=-1, keepdims=True)
            var = jnp.mean(jnp.square(x - mu), axis=-1, keepdims=True)
            return (x - mu) * jax.lax.rsqrt(var + LN_EPS) * w + b

        def l2norm(t):
            n = jnp.sqrt(jnp.sum(jnp.square(t), axis=-1, keepdims=True))
            return t / jnp.maximum(n, L2_EPS)
        b, n, _ = x.shape
        m = latents.shape[1]
        x = layer_norm(x, ln_x_w, ln_x_b)
        latents = layer_norm(latents, ln_l_w, ln_l_b)
        q = latents @ Wq
        kv_input = jnp.concatenate([x, latents], axis=1)
        kv = kv_input @ Wkv
        k, v = jnp.split(kv, 2, axis=-1)

        def to_heads(t):
            return t.reshape(t.shape[0], t.shape[1], HEADS, DIM_HEAD).transpose(0, 2, 1, 3)
        q, k, v = map(to_heads, (q, k, v))
        q = l2norm(q) * q_scale
        k = l2norm(k) * k_scale
        sim = jnp.einsum('bhid,bhjd->bhij', q, k) * SCALE
        full_mask = jnp.concatenate([mask, jnp.ones((b, m), dtype=bool)], axis=1)[:, None, None, :]
        max_neg = -jnp.finfo(sim.dtype).max
        sim = jnp.where(full_mask, sim, max_neg)
        attn = jax.nn.softmax(sim.astype(jnp.float32), axis=-1).astype(sim.dtype)
        out = jnp.einsum('bhij,bhjd->bhid', attn, v)
        out = out.transpose(0, 2, 1, 3).reshape(b, m, INNER)
        return layer_norm(out @ Wo, ln_o_w, ln_o_b)

    def _L2_ffn_ref(x, w1, b1, w2, b2, gamma, beta):
        import jax, jax.numpy as jnp
        import numpy as np
        EPS = 1e-05

        def act_quant(x):
            scale = 127.0 / jnp.clip(jnp.max(jnp.abs(x), axis=-1, keepdims=True), EPS, None)
            xq = jnp.clip(jnp.round(x * scale), -128.0, 127.0)
            return (xq, scale)

        def weight_quant(w):
            scale = 1.0 / jnp.clip(jnp.mean(jnp.abs(w)), EPS, None)
            wq = jnp.clip(jnp.round(w * scale), -1.0, 1.0)
            return (wq, scale)

        def qlinear(x, w, b):
            xq, sx = act_quant(x)
            wq, sw = weight_quant(w)
            y = jnp.einsum('bsd,hd->bsh', xq, wq) / (sx * sw)
            return y + b

        def layernorm(x, gamma, beta):
            mu = jnp.mean(x, axis=-1, keepdims=True)
            var = jnp.mean(jnp.square(x - mu), axis=-1, keepdims=True)
            return (x - mu) * jax.lax.rsqrt(var + EPS) * gamma + beta
        h = layernorm(x, gamma, beta)
        h = qlinear(h, w1, b1)
        h = jax.nn.gelu(h, approximate=False)
        out = qlinear(h, w2, b2)
        return out

    def _L3_xattn_ref(values, keys, query, Wv, Wk, Wq, Wo, bo):
        import jax, jax.numpy as jnp
        import numpy as np
        EMBED = 128
        HEADS = 16
        HEAD_DIM = EMBED // HEADS
        N, Lq, D = query.shape
        Lk = keys.shape[1]
        Lv = values.shape[1]
        v = (values @ Wv.T).reshape(N, Lv, HEADS, HEAD_DIM)
        k = (keys @ Wk.T).reshape(N, Lk, HEADS, HEAD_DIM)
        q = (query @ Wq.T).reshape(N, Lq, HEADS, HEAD_DIM)
        energy = jnp.einsum('nqhd,nkhd->nhqk', q, k)
        attn = jax.nn.softmax(energy / jnp.sqrt(jnp.float32(D)), axis=3)
        out = jnp.einsum('nhql,nlhd->nqhd', attn, v).reshape(N, Lq, D)
        return out @ Wo.T + bo

    def _L3_ffn_ref(hidden_states, gate_w, gate_up_w, down_w):
        import jax, jax.numpy as jnp
        import numpy as np
        H = 128
        F = 512
        E = 8
        TOP_K = 2
        B, S = (1, 256)
        b, s, h = hidden_states.shape
        x = hidden_states.reshape(-1, h)
        router_logits = x @ gate_w.T
        probs = jax.nn.softmax(router_logits.astype(jnp.float32), axis=-1)
        topw, sel = jax.lax.top_k(probs, TOP_K)
        topw = topw / jnp.sum(topw, axis=-1, keepdims=True)
        topw = topw.astype(x.dtype)
        combine = jnp.sum(jax.nn.one_hot(sel, E, dtype=x.dtype) * topw[..., None], axis=1)
        gu = jnp.einsum('th,efh->etf', x, gate_up_w)
        gate, up = (gu[..., :F], gu[..., F:])
        hact = up * jax.nn.gelu(gate, approximate=False)
        expert_out = jnp.einsum('etf,ehf->eth', hact, down_w)
        out = jnp.einsum('eth,te->th', expert_out, combine)
        return out.reshape(b, s, h)
    x = x + jnp.tanh(g_xattn[0]) * _L0_xattn_ref(_layernorm(x, axis=-1), ctx_1024, ctx_1024, mask_BxS2_ff1, L0_xattn_wq, L0_xattn_wk, L0_xattn_wv, L0_xattn_ln_gamma, L0_xattn_ln_beta, L0_xattn_dense_w, L0_xattn_dense_b)
    x = x + jnp.tanh(g_ffn[0]) * _L0_ffn_ref(_layernorm(x, axis=-1), L0_ffn_w_gate, L0_ffn_w_up, L0_ffn_w_down)
    x = x + jnp.tanh(g_xattn[1]) * _L1_xattn_ref(_layernorm(x, axis=-1), ctx_1024, ctx_1024, L1_xattn_q_w, L1_xattn_q_b, L1_xattn_k_w, L1_xattn_k_b, L1_xattn_v_w, L1_xattn_v_b, L1_xattn_o_w, L1_xattn_o_b)
    x = x + jnp.tanh(g_ffn[1]) * _L1_ffn_ref(_layernorm(x, axis=-1), L1_ffn_router_w, L1_ffn_gate_up_w, L1_ffn_down_w, L1_ffn_shared_gate_w, L1_ffn_shared_up_w, L1_ffn_shared_down_w)
    x = x + jnp.tanh(g_xattn[2]) * _L2_xattn_ref(ctx_1024, _layernorm(x, axis=-1), mask_BxS2_bk0, L2_xattn_ln_x_w, L2_xattn_ln_x_b, L2_xattn_ln_l_w, L2_xattn_ln_l_b, L2_xattn_Wq, L2_xattn_Wkv, L2_xattn_q_scale, L2_xattn_k_scale, L2_xattn_Wo, L2_xattn_ln_o_w, L2_xattn_ln_o_b)
    x = x + jnp.tanh(g_ffn[2]) * _L2_ffn_ref(_layernorm(x, axis=-1), L2_ffn_w1, L2_ffn_b1, L2_ffn_w2, L2_ffn_b2, L2_ffn_gamma, L2_ffn_beta)
    x = x + jnp.tanh(g_xattn[3]) * _L3_xattn_ref(ctx_1024, ctx_1024, _layernorm(x, axis=-1), L3_xattn_Wv, L3_xattn_Wk, L3_xattn_Wq, L3_xattn_Wo, L3_xattn_bo)
    x = x + jnp.tanh(g_ffn[3]) * _L3_ffn_ref(_layernorm(x, axis=-1), L3_ffn_gate_w, L3_ffn_gate_up_w, L3_ffn_down_w)
    return x

_drawn_inputs = setup_inputs


def setup_inputs(seed=0):
    import zlib

    import numpy as np

    out = dict(_drawn_inputs(seed))
    spreads = {'L0_xattn_ln_gamma': (1.0, 0.2),
     'L0_xattn_ln_beta': (0.0, 0.1),
     'L0_xattn_dense_b': (0.0, 0.1),
     'L2_xattn_ln_x_w': (1.0, 0.2),
     'L2_xattn_ln_x_b': (0.0, 0.1),
     'L2_xattn_ln_l_w': (1.0, 0.2),
     'L2_xattn_ln_l_b': (0.0, 0.4),
     'L2_xattn_q_scale': (1.0, 0.2),
     'L2_xattn_k_scale': (1.0, 0.2),
     'L2_xattn_ln_o_w': (1.0, 0.2),
     'L2_xattn_ln_o_b': (0.0, 0.427),
     'L2_ffn_b1': (0.0, 0.427),
     'L2_ffn_b2': (0.0, 0.1),
     'L2_ffn_gamma': (1.0, 0.595),
     'L2_ffn_beta': (0.0, 0.655)}
    factors = {'g_ffn': 8.0,
     'L1_xattn_q_b': 8.0,
     'L1_xattn_k_b': 8.0,
     'L1_xattn_v_b': 7.703,
     'L1_xattn_o_b': 7.242,
     'L1_ffn_router_w': 8.0,
     'L1_ffn_gate_up_w': 8.0,
     'L1_ffn_down_w': 8.0,
     'L1_ffn_shared_gate_w': 8.0,
     'L1_ffn_shared_up_w': 8.0,
     'L1_ffn_shared_down_w': 8.0,
     'L3_xattn_bo': 41.587,
     'L3_ffn_gate_w': 8.0,
     'L3_ffn_gate_up_w': 8.0,
     'L3_ffn_down_w': 8.0,
     'L3_xattn_Wk': 4.554,
     'L3_xattn_Wq': 5.604}
    for name, (base, spread) in spreads.items():
        noise = np.random.default_rng([zlib.crc32(name.encode()), seed]).standard_normal(out[name].shape)
        drawn = base * np.exp(spread * noise) if base else spread * noise
        out[name] = jnp.asarray(drawn.astype(out[name].dtype))
    for name, factor in factors.items():
        out[name] = (out[name] * factor).astype(out[name].dtype)
    return out
```

```python
from contextlib import ExitStack, contextmanager

import numpy as np

import concourse.bass as bass
from concourse import mybir

F32 = mybir.dt.float32
F16 = mybir.dt.float16
BF16 = mybir.dt.bfloat16
U8 = mybir.dt.uint8
ALU = mybir.AluOpType
ACT = mybir.ActivationFunctionType
AX = mybir.AxisListType

D = 128
B = 8
S = 56
N = B * S
NT = 4
TT = N // NT
C = 1500
KT = 12
KP = C // KT
CL = C + S
H16, HD16 = 16, 8
H8, HD8 = 8, 64
I2 = H8 * HD8
FF = 512
E1 = 18
E3 = 8
MAGIC = 12582912.0
NEG = -1e30

CST = {}
_at = 0
for _name, _n in (("ident", D), ("blk", D), ("causal", S), ("cosq", N), ("sinq", N), ("cosk", N), ("sink", N),
                  ("rot", D), ("mean", D), ("hmask", 16), ("numA", 3 * D), ("denA", 3 * D),
                  ("numB", 2 * D), ("denB", 2 * D), ("rank", 16), ("gmask", 4)):
    CST[_name] = (_at, _at + _n)
    _at += _n
CST_N = _at


def constants():
    c = np.zeros((D, CST_N), np.float32)

    def put(name, a):
        a = np.asarray(a, np.float32)
        c[:a.shape[0], CST[name][0]:CST[name][1]] = a.reshape(a.shape[0], -1)

    f = np.arange(D)
    put("ident", np.eye(D))
    put("blk", f[:, None] // HD16 == f[None, :] // HD16)
    causal = np.where(np.arange(S)[None, :] > np.arange(64)[:, None], NEG, 0.0)
    put("causal", np.concatenate([causal, causal]))
    half = HD16 // 2
    freqs = np.float32(1.0) / np.float32(10000.0) ** (np.arange(half, dtype=np.float32) / np.float32(half))
    ang = np.tile(np.arange(S, dtype=np.float32), B)[None, :] * freqs[f % half][:, None]
    cos, sin = np.cos(ang), np.sin(ang)
    put("cosk", cos)
    put("sink", sin)
    put("cosq", cos * np.float32(HD16 ** -0.5))
    put("sinq", sin * np.float32(HD16 ** -0.5))
    rot = np.zeros((D, D))
    for i in f:
        if i % HD16 < half:
            rot[i + half, i] = -1.0
        else:
            rot[i - half, i] = 1.0
    put("rot", rot)
    put("mean", np.ones((D, D)))
    put("hmask", f[:, None] // HD16 == np.arange(16)[None, :])
    num_a, den_a = np.zeros((D, 3, D)), np.zeros((D, 3, D))
    num_b, den_b = np.zeros((D, 2, D)), np.zeros((D, 2, D))
    for g in range(4):
        for h in range(3):
            for d in range(HD16):
                num_a[32 * g + 8 * h + d, h, (3 * g + h) * 8 + d] = 1.0
                den_a[32 * g + 24, h, (3 * g + h) * 8 + d] = 1.0
    for g in range(2):
        for h in range(2):
            for d in range(HD16):
                num_b[32 * g + 8 * h + d, h, (12 + 2 * g + h) * 8 + d] = 1.0
                den_b[32 * g + 16, h, (12 + 2 * g + h) * 8 + d] = 1.0
    put("numA", num_a)
    put("denA", den_a)
    put("numB", num_b)
    put("denB", den_b)
    put("rank", np.tile(16.0 - np.arange(16), (D, 1)))
    put("gmask", f[:, None] // 32 == np.arange(4)[None, :])
    sel = np.zeros((D, 2, 4, D), np.float16)
    for g in range(4):
        for hh in range(4):
            for d in range(HD16):
                src = (4 * g + hh) * 8 + d
                sel[src, 0, g, 32 * hh + 8 + d] = 1.0
                sel[src, 0, g, 32 * hh + 16 + d] = 1.0
                sel[src, 1, g, 32 * hh + 24 + d] = 1.0
    return c, sel


N_LOADS = 20
L1_LOADS = 5
PRODUCT = {"ffn0_in": 10, "latent_qk": 23, "queries2": 25}
OPERAND = {"kvt": 2, "k": 13, "latentsT": 21}


V128 = ["L0_g", "L0_b", "L0_db", "L1_vb", "L1_ob", "L2_xw", "L2_xb", "L2_lw", "L2_lb", "L2_ow", "L2_ob",
        "L2f_b2", "L2f_g", "L2f_be", "L3_bo"]
V64 = ["qs", "ks"]



class Chain:

    def __init__(self, eng, sem):
        self.eng, self.sem, self.n, self.turns = eng, sem, 0, None

    def step(self, ins):
        ins.then_inc(self.sem, 1)
        self.n += 1

    def sync(self):
        self.eng.wait_ge(self.sem, self.n if self.turns is None else self.turns + self.n)

    def link(self, ins):
        self.step(ins)
        self.sync()

    @contextmanager
    def loop(self, i, per_turn, turns):
        before = self.n
        self.turns = i * per_turn
        yield
        assert self.n - before == per_turn, self.n - before
        self.turns = None
        self.n = before + per_turn * turns


class Count:

    def __init__(self, eng, sem):
        self.eng, self.sem, self.n = eng, sem, 0

    def next(self, k=1):
        self.n += k
        self.eng.wait_ge(self.sem, self.n)


def build(nc, io, out):
    ctx = ExitStack()
    with ctx:
        def sb(name, shape, dt=F32):
            return ctx.enter_context(nc.sbuf_tensor(name, shape, dt))[tuple(slice(0, n) for n in shape)]

        def sem(name):
            return ctx.enter_context(nc.semaphore(name))

        d_cln = nc.dram_tensor("d_cln", (B, KP, KT * D), F32).ap()
        d_clnT = nc.dram_tensor("d_clnT", (B, D, C), F32).ap()
        d_k3 = nc.dram_tensor("d_k3", (B, 4, 4, 24, C), F16).ap()
        d_v3 = nc.dram_tensor("d_v3", (B, KP, KT * 192), F32).ap()
        d_att = nc.dram_tensor("d_att", (B, H16, S, HD16), F32).ap()
        d_lat = nc.dram_tensor("d_lat", (N, D), F32).ap()
        d_latT = nc.dram_tensor("d_latT", (D, N), F32).ap()
        d_rl = nc.dram_tensor("d_rl", (N, H8), F32).ap()

        ps = ctx.enter_context(nc.psum_tensor("ps", [128, 8, 512], F32))

        cst = sb("cst", [D, CST_N])
        sel = sb("sel", [D, 2, 4, D], F16)
        vec = sb("vec", [D, len(V128), D])
        qks = sb("qks", [D, 2, HD8])
        b1v = sb("b1v", [D, FF])
        gates = sb("gates", [D, 8])
        tg = sb("tg", [D, 8])
        colv = sb("colv", [D, 2])
        ident_h = sb("ident_h", [D, D], BF16)
        em = sb("em", [KP, B, KT])
        em2 = sb("em2", [KP, B, KT])
        kmask = sb("kmask", [KP, B, KT], U8)
        kbias = sb("kbias", [KP, B, KT])
        lbias = sb("lbias", [D, 1])
        w_l0 = sb("w_l0", [D, 2, D])
        w_q0 = sb("w_q0", [D, D])
        w_d0 = sb("w_d0", [D, D])
        w_k2 = sb("w_k2", [D, I2])
        w_k3 = sb("w_k3", [D, D])
        w_v3 = sb("w_v3", [D, D])
        w_q3 = sb("w_q3", [D, D])
        w_o3 = sb("w_o3", [D, D])
        w_r3 = sb("w_r3", [D, E3])
        wquant = sb("wquant", [D, 5, FF], BF16)
        mw = sb("mw", [D, 5])
        wscale = sb("wscale", [D, 5])
        gm4 = sb("gm4", [D, 4], F16)
        x = sb("x", [TT, NT, D])
        kv_all = sb("kv_all", [D, B, D + 2])
        rn = sb("rn", [KP, B, KT, H8])
        wgu = [sb(f"wgu{i}", [D, 2 * FF]) for i in range(2)]
        wdn = [sb(f"wdn{i}", [D, 4, D]) for i in range(2)]

        def cs(name, rows=D):
            a, b = CST[name]
            return cst[0:rows, a:b]

        def spread(name, rows=TT, n=NT):
            return vec[0:rows, V128.index(name), :].unsqueeze(1).broadcast_to([rows, n, D])

        ARENA = 34500
        arena = sb("arena", [D, ARENA])
        at = [0]

        def carve(shape, dt=F32):
            n = int(np.prod(shape[1:]))
            words = n if dt == F32 else (n + 1) // 2
            a = arena[0:shape[0], at[0]:at[0] + words]
            at[0] += words
            assert at[0] <= ARENA, at[0]
            if dt != F32:
                a = a.bitcast(dt)
            if len(shape) == 2:
                return a
            names = "abcd"[:len(shape) - 1]
            return a.rearrange("p (" + " ".join(names) + ") -> p " + " ".join(names),
                               **dict(zip(names[1:], shape[2:])))

        c_in = [carve([KP, KT, D]) for _ in range(2)]
        cln = [carve([KP, KT, D]) for _ in range(2)]
        cT = [carve([D, KT, KP]) for _ in range(2)]
        clnT = [carve([D, KT, KP]) for _ in range(2)]
        kraw = carve([KP, KT, D])
        sq0 = carve([KP, KT, 2, D])
        kn = carve([KP, KT, D])
        kpr = carve([KP, KT, D])
        rhs0 = carve([KP, KT, D + 2])
        k_hi = [carve([D, C], F16) for _ in range(2)]
        k_lo = [carve([D, C], F16) for _ in range(2)]
        v3 = [carve([KP, KT, 192]) for _ in range(2)]
        sqk = carve([KP, 2, I2])
        stat = carve([KP, KT, 6])
        sm = carve([KP, 16, 24])
        wraw = carve([D, 5, FF])

        at[0] = 0
        z = carve([TT, NT, D])
        y = carve([TT, NT, D])
        y2 = carve([TT, NT, D])
        xT = carve([D, N])
        xT2 = carve([D, N])
        xT3 = carve([D, N])
        big = carve([TT, NT, FF])
        big2 = carve([TT, NT, FF])
        big3 = carve([TT, NT, FF])
        zq = carve([TT, NT, D], BF16)
        zqT = carve([D, N], BF16)
        hq = carve([TT, NT, FF], BF16)
        hqT = carve([D, 4, N], BF16)
        lnst = carve([TT, NT, 6])
        lnmv = carve([TT, NT, 2])
        lnve = carve([TT, NT])
        lnrs = carve([TT, NT])
        nhalf = carve([D, 32])
        acol = carve([TT, 6, NT])
        qss = carve([TT, 3, NT * H8])
        exs = [carve([D, N]) for _ in range(2)]
        core_end = at[0]
        kvm = carve([D, B, D])
        kvt = carve([D, B, D])
        ksm = carve([D, B, 16])
        at0 = carve([S, B, D])
        rd0 = carve([S, B, 16])
        c56 = carve([TT, NT, D])
        c56T = carve([D, N])
        k1T = carve([D, N])
        q1T = carve([D, N])
        v1 = carve([S, B, D])
        w_l1 = carve([D, 4, D])
        w_col1 = carve([D, 2])
        kblk = carve([D, 2, 16, S])
        qst = carve([D, 2, 64])
        v1s = carve([S, 2, D])
        sc1 = carve([D, 16, S])
        pr1 = carve([D, 16, S])
        pT1 = carve([S, 16, D])
        m1 = carve([D, 3, 16])
        o1 = carve([D, D])
        w_r1 = carve([D, 16])
        sm16 = carve([TT, 8, NT, 16])
        wts = carve([TT, NT, E1])
        at[0] = core_end
        clnT_s = [carve([D, CL]) for _ in range(2)]
        cln_s = [carve([KP, KT + 1, D + 1]) for _ in range(2)]
        qtT = carve([D, H8, N])
        ctxT = carve([D, H8, N])
        m2 = carve([D, H8, D])
        w_kT2 = carve([D, 4, D])
        w_vT2 = carve([D, 4, D])
        w_o2 = carve([D, 4, D])
        w_q2 = carve([D, I2])
        sscl = [carve([KP, N]) for _ in range(2)]
        pexp = [carve([KP, N]) for _ in range(2)]
        onrm = carve([TT, 4, D])
        rden = carve([TT, 4])
        rnl = carve([S, B, H8])
        qT2 = carve([D, 4, N])
        at[0] = core_end
        kst = [carve([D, 4, C], F16) for _ in range(2)]
        v3s = [carve([KP, KT, 192]) for _ in range(2)]
        q3 = carve([D, 4, N], F16)
        q_hi = carve([D, N], F16)
        q_lo = carve([D, N], F16)
        qst3 = [carve([D, 4, 4, S], F16) for _ in range(2)]
        p3 = [carve([KP, 16, S]) for _ in range(2)]
        oA = carve([D, B, 3, S])
        oB = carve([64, B, 2, S])
        mx3 = carve([TT, 8, 3])
        m3 = carve([TT, 8])
        diag3 = carve([TT, 8, TT])
        sm8 = carve([TT, 8, NT, 8])
        wt3 = carve([TT, NT, 8])
        at[0] = core_end
        h3 = [carve([D, 4, N]) for _ in range(2)]

        ld_c = [sem(f"context_loaded{i}") for i in range(2)]
        ld_w = sem("weights_loaded")
        ld_x = sem("x_loaded")
        st = [sem(f"context_results_stored{i}") for i in range(2)]
        a_full, a_free = sem("act_banks_full"), sem("act_banks_free")
        d_full, d_free = sem("dve_banks_full"), sem("dve_banks_free")
        wsum_in, wsum = sem("weight_sums_ready"), sem("weight_sums_summed")
        w_ready = sem("weights_ready")
        c_var, c_sd = sem("context_variance"), sem("context_deviation")
        c_hat, c_lned = sem("context_normalised"), sem("context_affine")
        l0_var, l0_sd = sem("l0_variance"), sem("l0_deviation")
        l0_kn, l0_kaff = sem("l0_keys_normalised"), sem("l0_keys_affine")
        l0_w, l0_rhs = sem("l0_value_weights"), sem("l0_rhs_ready")
        l0_kp = sem("l0_kprime_ready")
        k_hi_ready = sem("l3_k_hi_ready")
        sq_used = sem("l2_squares_used")
        acc_full, acc_used = sem("kv_sums_full"), sem("kv_sums_used")
        rn_sq, rn_sd = sem("l2_key_squares"), sem("l2_key_norms")
        dve_s, pool_s, act_s = sem("dve_steps"), sem("pool_steps"), sem("act_steps")
        pe_passed = sem("tensor_waits_passed")
        operand, product = sem("operand_ready"), sem("product_ready")
        to_act, from_act = sem("act_input_ready"), sem("act_output_ready")
        ln_var, ln_rstd = sem("variance_ready"), sem("rstd_ready")
        ctx_done = sem("context_pass_done")
        l0_att = sem("l0_attention_ready")
        l0_st, l0_ld = sem("l0_attention_stored"), sem("l0_attention_loaded")
        l1_ld = sem("l1_loaded")
        l1_kq, l1_s, l1_m = sem("l1_operands"), sem("l1_scores"), sem("l1_shifted")
        l1_p, l1_t, l1_pt = sem("l1_probs"), sem("l1_probs_transposed"), sem("l1_probsT_ready")
        l1_o, l1_on, l1_ot = sem("l1_out"), sem("l1_out_normalised"), sem("l1_out_transposed")
        l1_done = sem("l1_pair_done")
        ex_ld = [sem(f"expert_loaded{i}") for i in range(2)]
        ex_gu, ex_act, ex_h = sem("expert_gate_up"), sem("expert_activated"), sem("expert_hidden")
        ex_dn, ex_w, ex_acc = sem("expert_down"), sem("expert_weighted"), sem("expert_added")
        ld_m = sem("layer_weights_loaded")
        st_m = sem("latents_stored")
        l2_ld = [sem(f"l2_loaded{i}") for i in range(2)]
        l2_s, l2_sc, l2_p, l2_pv = sem("l2_sim"), sem("l2_scaled"), sem("l2_probs"), sem("l2_pv_tile")
        l2_on, l2_t, l2_done = sem("l2_out_normalised"), sem("l2_out_transposed"), sem("l2_batch_done")
        l3_ld = [sem(f"l3_loaded{i}") for i in range(2)]
        l3_q, l3_mx, l3_mxd = sem("l3_queries_ready"), sem("l3_max_sim"), sem("l3_max_done")
        l3_dg, l3_sh, l3_row = sem("l3_diag_ready"), sem("l3_shift_row"), sem("l3_shift_copied")
        l3_s, l3_p, l3_pv, l3_o = sem("l3_sim"), sem("l3_probs"), sem("l3_pv_tile"), sem("l3_out_copied")
        st_out = sem("out_stored")
        lat_ready, l3_free, out_ready = sem("latents_ready"), sem("l2_memory_free"), sem("out_ready")

        block = ctx.enter_context(nc.Block())

        def batch(t, b):
            names = "abcd"[:len(t.shape) - 2]
            return t[bass.ds(b, 1)].rearrange("o p " + " ".join(names) + " -> (o p) " + " ".join(names))

        k3_in = d_k3.rearrange("n g e (s d) c -> n s (g e) d c", s=3)

        @block.sync
        def _(sp):
            def load_context(b, p):
                src = io["ctx"][bass.ds(b, 1)].rearrange("o (p j) d -> (o p) j d", j=KT)
                sp.dma_start(c_in[p][0:112], src[0:112]).then_inc(ld_c[p], 16)
                sp.dma_start(c_in[p][112:KP], src[112:KP]).then_inc(ld_c[p], 16)

            load_context(0, 0)
            loads = [(cst[:, :], io["cst"]), (w_l0[:, 0, :], io["L0_wk"]), (w_l0[:, 1, :], io["L0_wv"]),
                     (vec[:, :, :], io["vec"].unsqueeze(0).broadcast_to([D, len(V128), D])),
                     (wraw, io["wquant"]), (w_k2[:, :], io["L2_wk"]), (w_k3[:, :], io["L3_wkT"]),
                     (w_v3[:, :], io["L3_wvT"]), (sel[:, :, :, :], io["sel"]),
                     (em[:, :, :], io["mask"].rearrange("b (p j) -> p b j", j=KT)),
                     (kmask[:, :, :], io["kmask"].rearrange("b (p j) -> p b j", j=KT)),
                     (w_q0[:, :], io["L0_wq"]), (w_d0[:, :], io["L0_wd"]),
                     (w_r3[:, :], io["L3_router"]), (w_q3[:, :], io["L3_wqT"]), (w_o3[:, :], io["L3_woT"]),
                     (qks[:, :, :], io["qks"].unsqueeze(0).broadcast_to([D, 2, HD8])),
                     (b1v[:, :], io["b1"].unsqueeze(0).broadcast_to([D, FF])),
                     (gates[:, :], io["gates"].unsqueeze(0).broadcast_to([D, 8])),
                     (x[:, :, :], io["x"].rearrange("(t p) d -> p t d", p=TT))]
            for dst, src in loads:
                sp.dma_start(dst, src).then_inc(ld_w, 16)
            load_context(1, 1)

            def store_results(b, p):
                sp.wait_ge(c_lned, b + 1)
                sp.dma_start(batch(d_cln, b), cln[p].rearrange("p j d -> p (j d)")).then_inc(st[p], 16)
                sp.wait_ge(d_free, 9 * b + 3 + 3)
                for s, part in enumerate((k_hi[p], k_lo[p], k_hi[p])):
                    sp.dma_start(k3_in[bass.ds(b, 1), s].rearrange("o h d c -> (o h) d c"), part).then_inc(st[p], 16)
                sp.wait_ge(d_free, 9 * b + 3 + 6)
                sp.dma_start(batch(d_v3, b), v3[p].rearrange("p j d -> p (j d)")).then_inc(st[p], 16)
                sp.wait_ge(d_free, 9 * b + 3 + 9)
                sp.dma_start(batch(d_clnT, b), clnT[p].rearrange("p j d -> p (j d)")).then_inc(st[p], 16)

            with sp.Fori(0, B // 2 - 1) as i:
                for p in range(2):
                    b = 2 * i + p
                    store_results(b, p)
                    sp.wait_ge(d_full, 9 * b + 9)
                    sp.wait_ge(l0_rhs, b + 1)
                    load_context(b + 2, p)
            for b in (B - 2, B - 1):
                store_results(b, b % 2)
            for p in range(2):
                sp.wait_ge(st[p], 96 * (B // 2 + 1))

            sp.wait_ge(ctx_done, 1)
            for e in range(2):
                sp.dma_start(c56[S * e:S * e + S], io["ctx"].rearrange("(t e) s d -> e s t d", e=2)[e, 0:S])\
                    .then_inc(l1_ld, 16)
            sp.dma_start(w_l1, io["L1_w"]).then_inc(l1_ld, 16)
            sp.dma_start(w_col1, io["L1_cols"]).then_inc(l1_ld, 16)
            sp.dma_start(w_r1, io["L1_router"]).then_inc(l1_ld, 16)

            def load_expert1(e, p):
                sp.dma_start(wgu[p][:, 0:2 * D], batch(io["L1_gu"], e)).then_inc(ex_ld[p], 16)
                sp.dma_start(wdn[p][:, 0, :], batch(io["L1_dn"], e)).then_inc(ex_ld[p], 16)

            load_expert1(0, 0)
            load_expert1(1, 1)

            sp.wait_ge(l0_att, 1)
            sp.dma_start(d_att.rearrange("b h n e -> n (b h) e"), at0.rearrange("n b (h e) -> n (b h) e", h=H16))\
                .then_inc(l0_st, 16)
            sp.wait_ge(l0_st, 16)
            sp.dma_start(y2, d_att.rearrange("b h n e -> (b h n e)").rearrange("(t p d) -> p t d", p=TT, d=D))\
                .then_inc(l0_ld, 16)

            with sp.Fori(0, E1 // 2 - 1) as i:
                for p in range(2):
                    e = 2 * i + p
                    sp.wait_ge(ex_dn, e + 1)
                    load_expert1(e + 2, p)

            sp.wait_ge(ex_acc, E1 + 2)
            sp.dma_start(w_kT2, io["L2_wkT"]).then_inc(ld_m, 16)
            sp.dma_start(w_vT2, io["L2_wvT"]).then_inc(ld_m, 16)
            sp.dma_start(w_o2, io["L2_wo"]).then_inc(ld_m, 16)
            sp.dma_start(w_q2, io["L2_wq"]).then_inc(ld_m, 16)
            sp.wait_ge(lat_ready, 1)
            sp.dma_start(d_lat.rearrange("(t p) d -> p t d", p=TT), y).then_inc(st_m, 16)
            sp.wait_ge(lat_ready, 2)
            sp.dma_start(d_latT, xT).then_inc(st_m, 16)
            sp.wait_ge(lat_ready, 3)
            sp.dma_start(d_rl.rearrange("(t p) h -> p t h", p=TT), qss[:, 2, :].rearrange("p (t h) -> p t h", t=NT))\
                .then_inc(st_m, 16)
            sp.wait_ge(st_m, 48)
            sp.dma_start(rnl, d_rl.rearrange("(b q) h -> q b h", b=B)).then_inc(ld_m, 16)

            def load_keys2(b, p):
                sp.dma_start(clnT_s[p][:, 0:C], batch(d_clnT, b)).then_inc(l2_ld[p], 16)
                sp.dma_start(clnT_s[p][:, C:CL], d_latT[:, bass.ds(b * S, S)]).then_inc(l2_ld[p], 16)
                src = batch(d_cln, b).rearrange("p (j d) -> p j d", j=KT)
                sp.dma_start(cln_s[p][0:112, 0:KT, 0:D], src[0:112]).then_inc(l2_ld[p], 16)
                sp.dma_start(cln_s[p][112:KP, 0:KT, 0:D], src[112:KP]).then_inc(l2_ld[p], 16)
                sp.dma_start(cln_s[p][0:S, KT, 0:D], d_lat[bass.ds(b * S, S), :]).then_inc(l2_ld[p], 16)

            load_keys2(0, 0)
            load_keys2(1, 1)
            with sp.Fori(0, B // 2 - 1) as i:
                for p in range(2):
                    b = 2 * i + p
                    sp.wait_ge(l2_pv, (KT + 1) * (b + 1) + 2)
                    load_keys2(b + 2, p)

            def load_keys3(b, p):
                src = d_k3[bass.ds(b, 1)].rearrange("o g e r c -> (o e) r g c")
                for hh in range(4):
                    sp.dma_start(kst[p][32 * hh + 8:32 * hh + 32], src[hh]).then_inc(l3_ld[p], 16)
                src = batch(d_v3, b).rearrange("p (j d) -> p j d", j=KT)
                sp.dma_start(v3s[p][0:112], src[0:112]).then_inc(l3_ld[p], 16)
                sp.dma_start(v3s[p][112:KP], src[112:KP]).then_inc(l3_ld[p], 16)

            sp.wait_ge(l3_free, 1)
            load_keys3(0, 0)
            load_keys3(1, 1)
            with sp.Fori(0, B // 2 - 1) as i:
                for p in range(2):
                    b = 2 * i + p
                    sp.wait_ge(l3_pv, KT * (b + 1) + 2)
                    load_keys3(b + 2, p)

            def load_expert3(e, p):
                sp.dma_start(wgu[p][:, :], batch(io["L3_gu"], e)).then_inc(ex_ld[p], 16)
                sp.dma_start(wdn[p][:, :, :], batch(io["L3_dn"], e)).then_inc(ex_ld[p], 16)

            load_expert3(0, 0)
            load_expert3(1, 1)
            with sp.Fori(0, E3 // 2 - 1) as i:
                for p in range(2):
                    e = 2 * i + p
                    sp.wait_ge(ex_dn, E1 + e + 1)
                    load_expert3(e + 2, p)
            sp.wait_ge(out_ready, 1)
            sp.dma_start(out.rearrange("(t p) d -> p t d", p=TT), x[:, :, :]).then_inc(st_out, 16)
            sp.wait_ge(st_out, 16)


        @block.tensor
        def _(pe):
            op = Count(pe, operand)
            ident = cs("ident")

            def transposes(src, k):
                for t in range(NT):
                    last = pe.transpose(ps[0:D, k, TT * t:TT * t + TT], src[:, t, :], ident[0:TT, 0:TT])
                last.then_inc(product, 1)

            def by_tokens(srcT, w, k, cols=D):
                for t in range(NT):
                    mm = pe.matmul(ps[0:TT, k, cols * t:cols * t + cols], srcT[:, TT * t:TT * t + TT], w,
                                   start=True, stop=True)
                mm.then_inc(product, 1)

            pe.wait_ge(ld_w, N_LOADS * 16)
            pe.wait_ge(wsum_in, 1)
            pe.matmul(ps[0:D, 7, 0:5], cs("mean"), mw[:, :], start=True, stop=True).then_inc(wsum, 1)
            pe.wait_ge(w_ready, 1)

            A, DV = (0, 1, 2), (3, 4, 5)
            with pe.Fori(0, B // 2) as i:
                for p in range(2):
                    b = 2 * i + p
                    use_a, use_d = [0], [0]

                    def bank_a():
                        n = use_a[0]
                        use_a[0] += 1
                        pe.wait_ge(a_free, 21 * b + n + 1)
                        return A[(21 * p + n) % 3]

                    def bank_d():
                        n = use_d[0]
                        use_d[0] += 1
                        pe.wait_ge(d_free, 9 * b + n + 1)
                        return DV[n % 3]

                    pe.wait_ge(ld_c[p], 32 * (i + 1))
                    for u in range(3):
                        k = bank_a()
                        for j in range(4):
                            mm = pe.transpose(ps[0:D, k, KP * j:KP * j + KP], c_in[p][:, 4 * u + j, :],
                                              ident[0:KP, 0:KP])
                        mm.then_inc(a_full, 1)
                    for u in range(6):
                        if u % 2 == 0:
                            pe.wait_ge(a_free, 21 * b + 3 + u // 2 + 1)
                        k = bank_a()
                        for j in range(2):
                            mm = pe.matmul(ps[0:KP, k, 256 * j:256 * j + 256], cT[p][:, 2 * u + j, :],
                                           w_l0[:, :, :].rearrange("p a n -> p (a n)"), start=True, stop=True)
                        mm.then_inc(a_full, 1)
                    for u in range(3):
                        k = bank_d()
                        pe.matmul(ps[0:D, k, 0:4 * KP], w_k3[:, :],
                                  cT[p][:, 4 * u:4 * u + 4, :].rearrange("p j n -> p (j n)"),
                                  start=True, stop=True).then_inc(d_full, 1)
                    for u in range(3):
                        k = bank_d()
                        for j in range(4):
                            mm = pe.matmul(ps[0:KP, k, D * j:D * j + D], cT[p][:, 4 * u + j, :], w_v3[:, :],
                                           start=True, stop=True)
                        mm.then_inc(d_full, 1)
                    pe.wait_ge(c_lned, b + 1)
                    for u in range(3):
                        k = bank_d()
                        for j in range(4):
                            mm = pe.transpose(ps[0:D, k, KP * j:KP * j + KP], cln[p][:, 4 * u + j, :],
                                              ident[0:KP, 0:KP])
                        mm.then_inc(d_full, 1)
                    for j in range(KT):
                        if j % 4 == 0:
                            pe.wait_ge(d_free, 9 * b + 3 + 6 + j // 4 + 1)
                        k = bank_a()
                        pe.matmul(ps[0:KP, k, :], clnT[p][:, j, :], w_k2[:, :], start=True, stop=True)\
                            .then_inc(a_full, 1)
                    pe.wait_ge(l0_kp, b + 1)
                    pe.wait_ge(l0_rhs, b + 1)
                    pe.wait_ge(acc_used, b + 1)
                    for j in range(KT):
                        mm = pe.matmul(ps[0:D, 6 + p, 0:D + 2], kpr[:, j, :], rhs0[:, j, :],
                                       start=(j == 0), stop=(j == KT - 1))
                    mm.then_inc(acc_full, 1)

            op.next()
            for b in range(B):
                mm = pe.transpose(ps[0:D, b // 4, D * (b % 4):D * (b % 4) + D], kv_all[:, b, 0:D], ident)
            mm.then_inc(product, 1)
            op.next()
            for b in range(B):
                mm = pe.matmul(ps[0:D, 2 + b // 4, D * (b % 4):D * (b % 4) + D], kvt[:, b, :], w_l0[:, 1, :],
                               start=True, stop=True)
            mm.then_inc(product, 1)
            op.next()
            transposes(z, 4)
            op.next()
            by_tokens(xT, w_q0[:, :], 5)
            op.next()
            transposes(y2, 4)
            op.next()
            for b in range(B):
                pe.matmul(ps[0:S, 6 + b // 4, D * (b % 4):D * (b % 4) + D], xT[:, S * b:S * b + S], kvm[:, b, :],
                          start=True, stop=True)
                mm = pe.matmul(ps[0:S, 5, 16 * b:16 * b + 16], xT[:, S * b:S * b + S], ksm[:, b, :],
                               start=True, stop=True)
            mm.then_inc(product, 1)
            pe.wait_ge(l0_ld, 16)
            transposes(y2, 4)
            op.next()
            by_tokens(xT2, w_d0[:, :], 0)

            def quantised_ffn(first, n_first, second):
                op.next()
                zps = ps[0:D, 0, 0:256].bitcast(BF16)
                for t in range(NT):
                    mm = pe.transpose(zps[:, TT * t:TT * t + TT], zq[:, t, :], ident_h[0:TT, 0:TT])
                mm.then_inc(product, 1)
                op.next()
                for t in range(NT):
                    for m in range(n_first):
                        mm = pe.matmul(ps[0:TT, t + 4 * m, :], zqT[:, TT * t:TT * t + TT], wquant[:, first + m, :],
                                       start=True, stop=True)
                mm.then_inc(product, 1)
                op.next()
                for c in range(4):
                    hps = ps[0:D, c // 2, 256 * (c % 2):256 * (c % 2) + 256].bitcast(BF16)
                    for t in range(NT):
                        mm = pe.transpose(hps[:, TT * t:TT * t + TT], hq[:, t, D * c:D * c + D],
                                          ident_h[0:TT, 0:TT])
                mm.then_inc(product, 1)
                op.next()
                for t in range(NT):
                    for c in range(4):
                        mm = pe.matmul(ps[0:TT, 2, D * t:D * t + D], hqT[:, c, TT * t:TT * t + TT],
                                       wquant[:, second, D * c:D * c + D], start=(c == 0), stop=(c == 3))
                mm.then_inc(product, 1)

            quantised_ffn(0, 2, 2)

            pe.wait_ge(l1_ld, L1_LOADS * 16)
            transposes(c56, 0)
            op.next()
            pe.matmul(ps[0:D, 1, 0:N], w_l1[:, 1, :], c56T, start=True, stop=True).then_inc(product, 1)
            op.next()
            pe.matmul(ps[0:D, 2, 0:N], cs("rot"), k1T, start=True, stop=True)
            for b in range(B):
                mm = pe.matmul(ps[0:S, 3 + b // 4, D * (b % 4):D * (b % 4) + D], c56T[:, S * b:S * b + S],
                               w_l1[:, 2, :], start=True, stop=True)
            mm.then_inc(product, 1)
            op.next()
            transposes(z, 0)
            op.next()
            pe.matmul(ps[0:D, 1, 0:N], w_l1[:, 0, :], xT, start=True, stop=True).then_inc(product, 1)
            op.next()
            pe.matmul(ps[0:D, 2, 0:N], cs("rot"), q1T, start=True, stop=True).then_inc(product, 1)
            with pe.Fori(0, NT) as i:
                pe.wait_ge(l1_kq, i + 1)
                for e in range(2):
                    for half in range(2):
                        mm = pe.matmul(ps[64 * e:64 * e + 64, half, 0:8 * S], qst[:, e, :],
                                       kblk[:, e, 8 * half:8 * half + 8, :].rearrange("p h s -> p (h s)"),
                                       start=True, stop=True)
                mm.then_inc(l1_s, 1)
                pe.wait_ge(l1_p, i + 1)
                pe.nop().then_inc(pe_passed, 1)
                for h in range(16):
                    mm = pe.transpose(ps[0:S, 2 + h // 4, D * (h % 4):D * (h % 4) + D], pr1[:, h, :], ident)
                mm.then_inc(l1_t, 1)
                pe.wait_ge(l1_pt, i + 1)
                pe.nop().then_inc(pe_passed, 1)
                for e in range(2):
                    for h in range(16):
                        mm = pe.matmul(ps[64 * e:64 * e + 64, 6, 8 * h:8 * h + 8], pT1[:, h, 64 * e:64 * e + 64],
                                       v1s[:, e, 8 * h:8 * h + 8], start=True, stop=True)
                mm.then_inc(l1_o, 1)
                pe.wait_ge(l1_on, i + 1)
                pe.transpose(ps[0:D, 7, 0:D], o1, ident).then_inc(l1_ot, 1)
            op.next()
            by_tokens(xT2, w_l1[:, 3, :], 0)

            op.next()
            transposes(z, 0)
            op.next()
            by_tokens(xT, w_r1, 1, cols=16)

            def gate_up1(e, p):
                for m in range(2):
                    mm = pe.matmul(ps[0:D, 2 + 2 * p + m, 0:N], wgu[p][:, D * m:D * m + D], xT, start=True, stop=True)
                mm.then_inc(ex_gu, 1)

            def down1(e, p):
                pe.wait_ge(ex_h, e + 2)
                for t in range(NT):
                    mm = pe.matmul(ps[0:TT, 6 + p, D * t:D * t + D], (xT2, xT3)[p][:, TT * t:TT * t + TT],
                                   wdn[p][:, 0, :], start=True, stop=True)
                mm.then_inc(ex_dn, 1)

            pe.wait_ge(ex_ld[0], 32)
            gate_up1(0, 0)
            with pe.Fori(0, E1 // 2 - 1) as i:
                for p in range(2):
                    e = 2 * i + p
                    pe.wait_ge(ex_ld[1 - p], 32 * (i + 1 + p))
                    pe.wait_ge(ex_h, e + 1)
                    gate_up1(e + 1, 1 - p)
                    pe.wait_ge(ex_w, e + 1)
                    down1(e, p)
            pe.wait_ge(ex_ld[1], 32 * (E1 // 2))
            pe.wait_ge(ex_h, E1 - 1)
            gate_up1(E1 - 1, 1)
            pe.wait_ge(ex_w, E1 - 1)
            down1(E1 - 2, 0)
            pe.wait_ge(ex_w, E1)
            down1(E1 - 1, 1)

            pe.wait_ge(ld_m, 4 * 16)
            op.next()
            for h in range(H8):
                r, c = 64 * (h % 2), h // 2
                pe.matmul(ps[0:D, 2 + h % 2, D * c:D * c + D], w_vT2[r:r + 64, c, :], w_o2[r:r + 64, c, :],
                          start=True, stop=True)
            transposes(y, 0)
            op.next()
            for t in range(NT):
                pe.matmul(ps[0:TT, t, :], xT[:, TT * t:TT * t + TT], w_q2, start=True, stop=True)
                mm = pe.matmul(ps[0:TT, 4 + t, :], xT[:, TT * t:TT * t + TT], w_k2[:, :], start=True, stop=True)
            mm.then_inc(product, 1)
            op.next()
            for c in range(4):
                for t in range(NT):
                    mm = pe.transpose(ps[0:D, c, TT * t:TT * t + TT], big[:, t, D * c:D * c + D],
                                      ident[0:TT, 0:TT])
            mm.then_inc(product, 1)
            op.next()
            for h in range(H8):
                r, c = 64 * (h % 2), h // 2
                mm = pe.matmul(ps[0:D, (4 + h) % 8, 0:N], w_kT2[r:r + 64, c, :], qT2[r:r + 64, c, :],
                               start=True, stop=True)
            mm.then_inc(product, 1)
            op.next()

            def sim2(b, p, t, i):
                rows, cols = (KP, KP * t) if t < KT else (S, C)
                pe.wait_ge(l2_sc, (KT + 1) * b + t + 1)
                if t == KT:
                    pe.nop().then_inc(pe_passed, 1)
                pe.matmul(ps[0:rows, (t + p) % 2, 0:N].rearrange("p (h q) -> p h q", h=H8),
                          clnT_s[p][:, cols:cols + rows], qtT[:, :, bass.ds(b * S, S)],
                          start=True, stop=True).then_inc(l2_s, 1)

            def pv2(b, p, t):
                rows = KP if t < KT else S
                pe.wait_ge(l2_p, (KT + 1) * b + t + 3)
                for c in range(4):
                    dst = ps[0:TT, 4 + 2 * p, 129 * c:129 * c + 129] if c < 3 else ps[0:TT, 5 + 2 * p, 0:129]
                    mm = pe.matmul(dst, pexp[(t + p) % 2][0:rows, TT * c:TT * c + TT], cln_s[p][0:rows, t, :],
                                   start=(t == 0 and c in (0, 3)), stop=(t == KT), skip_group_check=True)
                mm.then_inc(l2_pv, 1)

            with pe.Fori(0, B // 2) as i:
                for p in range(2):
                    b = 2 * i + p
                    pe.wait_ge(l2_ld[p], 80 * (i + 1))
                    sim2(b, p, 0, i)
                    sim2(b, p, 1, i)
                    for t in range(KT + 1):
                        if t + 2 <= KT:
                            sim2(b, p, t + 2, i)
                        pv2(b, p, t)
                    pe.wait_ge(l2_on, b + 1)
                    for c in range(4):
                        mm = pe.transpose(ps[0:D, 2, TT * c:TT * c + TT], onrm[:, c, :], ident[0:TT, 0:TT])
                    mm.then_inc(l2_t, 1)
            pe.wait_ge(l2_done, B)
            for t in range(NT):
                for h in range(H8):
                    mm = pe.matmul(ps[0:TT, 0, D * t:D * t + D], ctxT[:, h, TT * t:TT * t + TT], m2[:, h, :],
                                   start=(h == 0), stop=(h == H8 - 1))
            mm.then_inc(product, 1)

            quantised_ffn(3, 1, 4)

            op.next()
            transposes(z, 0)
            op.next()
            pe.matmul(ps[0:D, 1, 0:N], w_q3[:, :], xT, start=True, stop=True).then_inc(product, 1)
            op.next()
            for g in range(4):
                pe.matmul(ps[0:D, g, 0:N], sel[:, 0, g, :], q_hi, start=True, stop=False)
                mm = pe.matmul(ps[0:D, g, 0:N], sel[:, 1, g, :], q_lo, start=False, stop=True)
            mm.then_inc(product, 1)

            def max_sim(bn, pn, u):
                pair, third = u // 3, u % 3
                pe.wait_ge(l3_mxd, 24 * bn + u + 1)
                pe.matmul(ps[0:TT, 4 + u % 2, 0:500],
                          qst3[pn][:, pair // 2, 2 * (pair % 2):2 * (pair % 2) + 2, :].rearrange("p h q -> p (h q)"),
                          kst[pn][:, pair // 2, 500 * third:500 * third + 500],
                          start=True, stop=True).then_inc(l3_mx, 1)

            def shift_row(bn):
                pe.wait_ge(l3_dg, bn + 1)
                for half in range(2):
                    if half:
                        pe.wait_ge(l3_row, 2 * bn + 1)
                    mm = pe.matmul(ps[0:1, 7, 0:4 * TT], cs("mean")[0:TT, 0:1],
                                   diag3[:, 4 * half:4 * half + 4, :].rearrange("p a n -> p (a n)"),
                                   start=True, stop=True)
                    mm.then_inc(l3_sh, 1)

            def sim3(b, p, t):
                pe.wait_ge(l3_p, KT * b + t + 1)
                for g in range(4):
                    mm = pe.matmul(ps[0:KP, 2 * (t % 2) + g // 2, 224 * (g % 2):224 * (g % 2) + 224],
                                   kst[p][:, g, KP * t:KP * t + KP],
                                   qst3[p][:, g, :, :].rearrange("p h q -> p (h q)"), start=True, stop=True)
                mm.then_inc(l3_s, 1)

            def pv3(b, p, t):
                pe.wait_ge(l3_p, KT * b + t + 3)
                if t == 0:
                    pe.wait_ge(l3_o, b + 1)
                for g in range(4):
                    pe.matmul(ps[32 * g:32 * g + 32, 6, 0:168], v3s[p][:, t, 32 * g:32 * g + 32],
                              p3[t % 2][:, 3 * g:3 * g + 3, :].rearrange("p h q -> p (h q)"),
                              start=(t == 0), stop=(t == KT - 1), skip_group_check=True)
                for g in range(2):
                    mm = pe.matmul(ps[32 * g:32 * g + 32, 6, 168:280], v3s[p][:, t, 128 + 32 * g:160 + 32 * g],
                                   p3[t % 2][:, 12 + 2 * g:14 + 2 * g, :].rearrange("p h q -> p (h q)"),
                                   start=False, stop=(t == KT - 1), skip_group_check=True)
                mm.then_inc(l3_pv, 1)

            def batch3(b, p, bn, i, more=True):
                pe.wait_ge(l3_row, 2 * b + 2)
                if more:
                    pe.wait_ge(l3_ld[1 - p], 96 * (i + 1 + p))
                    pe.wait_ge(l3_q, bn + 1)
                sim3(b, p, 0)
                for t in range(KT):
                    if t + 1 < KT:
                        sim3(b, p, t + 1)
                    if more:
                        max_sim(bn, 1 - p, 2 * t)
                        max_sim(bn, 1 - p, 2 * t + 1)
                    pv3(b, p, t)
                if more:
                    shift_row(bn)

            pe.wait_ge(l3_ld[0], 96)
            pe.wait_ge(l3_q, 1)
            for u in range(24):
                max_sim(0, 0, u)
            shift_row(0)
            with pe.Fori(0, B // 2 - 1) as i:
                for p in range(2):
                    batch3(2 * i + p, p, 2 * i + p + 1, i)
            batch3(B - 2, 0, B - 1, B // 2 - 1)
            batch3(B - 1, 1, None, None, more=False)
            pe.wait_ge(l3_o, B + 1)
            for k, names in enumerate((("numA", "numB"), ("denA", "denB"))):
                parts = [(cs(names[0])[:, D * h:D * h + D], oA[:, :, h, :]) for h in range(3)]
                parts += [(cs(names[1], 64)[:, D * h:D * h + D], oB[:, :, h, :]) for h in range(2)]
                for n, (w, o) in enumerate(parts):
                    mm = pe.matmul(ps[0:D, k, 0:N].rearrange("p (b q) -> p b q", b=B), w, o,
                                   start=(n == 0), stop=(n == 4))
            mm.then_inc(product, 1)
            op.next()
            by_tokens(xT2, w_o3[:, :], 2)

            op.next()
            transposes(z, 0)
            op.next()
            by_tokens(xT, w_r3[:, :], 1, cols=E3)

            def gate_up3(e, p, c):
                for m in range(2):
                    mm = pe.matmul(ps[0:D, 2 + 2 * (c % 2) + m, 0:N], wgu[p][:, FF * m + D * c:FF * m + D * c + D],
                                   xT, start=True, stop=True)
                mm.then_inc(ex_gu, 1)

            def down3(e, p):
                pe.wait_ge(ex_h, E1 + 4 * e + 5)
                pe.wait_ge(ex_w, E1 + e + 1)
                for t in range(NT):
                    for c in range(4):
                        mm = pe.matmul(ps[0:TT, 6 + p, D * t:D * t + D], h3[p][:, c, TT * t:TT * t + TT],
                                       wdn[p][:, c, :], start=(c == 0), stop=(c == 3))
                mm.then_inc(ex_dn, 1)

            def expert3(e, p, i, first=False):
                pe.wait_ge(ex_ld[p], 32 * (E1 // 2) + 32 * (i + 1))
                for c in range(4):
                    pe.wait_ge(ex_h, E1 + 4 * e + c)
                    gate_up3(e, p, c)
                    if c == 1 and not first:
                        down3(e - 1, 1 - p)

            expert3(0, 0, 0, first=True)
            expert3(1, 1, 0)
            with pe.Fori(1, E3 // 2) as i:
                for p in range(2):
                    expert3(2 * i + p, p, i)
            down3(E3 - 1, 1)

        @block.scalar
        def _(act):
            act.nop().then_inc(a_free, 3)
            act.nop().then_inc(l2_p, 2)
            act.nop().then_inc(l3_p, 2)
            act.wait_ge(ld_w, N_LOADS * 16)
            act.activation(tg[:, :], gates[:, :], ACT.Tanh).then_inc(from_act, 1)

            with act.Fori(0, B // 2) as i:
                for p in range(2):
                    b = 2 * i + p
                    use = [0]

                    def bank_a():
                        n = use[0]
                        use[0] += 1
                        act.wait_ge(a_full, 21 * b + n + 1)
                        return (21 * p + n) % 3

                    for u in range(3):
                        k = bank_a()
                        act.copy(cT[p][:, 4 * u:4 * u + 4, :].rearrange("p j n -> p (j n)"), ps[0:D, k, 0:4 * KP])\
                            .then_inc(a_free, 1)
                    act.wait_ge(l0_kn, b + 1)
                    for u in range(6):
                        k = bank_a()
                        src = ps[0:KP, k, :].rearrange("p (j a n) -> p j a n", j=2, a=2)
                        act.activation(sq0[:, 2 * u:2 * u + 2].rearrange("p j a n -> p (j a n)"), ps[0:KP, k, :],
                                       ACT.Square)
                        act.copy(kraw[:, 2 * u:2 * u + 2, :], src[:, :, 0, :]).then_inc(a_free, 1)
                        if u == 1:
                            act.wait_ge(c_var, b + 1)
                            act.activation(sm[:, 5, 0:KT], sm[:, 4, 0:KT], ACT.Sqrt).then_inc(c_sd, 1)
                    act.wait_ge(st[p], 96 * (i + 1))
                    for u in range(3):
                        act.wait_ge(d_full, 9 * b + u + 1)
                        act.copy(k_hi[p][:, 500 * u:500 * u + 500], ps[0:D, 3 + u, 0:500]).then_inc(k_hi_ready, 1)
                    act.wait_ge(l0_var, b + 1)
                    act.activation(sm[:, 8, :], sm[:, 7, :], ACT.Sqrt).then_inc(l0_sd, 1)
                    for j in range(KT):
                        k = bank_a()
                        act.wait_ge(sq_used, KT * b + j + 1)
                        act.activation(sqk[:, j % 2, :], ps[0:KP, k, :], ACT.Square).then_inc(a_free, 1)
            act.wait_ge(rn_sq, 1)
            rn_flat = rn[:, :, :, :].rearrange("p b t h -> p (b t h)")
            act.activation(rn_flat, rn_flat, ACT.Sqrt).then_inc(rn_sd, 1)

            act.wait_ge(product, PRODUCT["ffn0_in"])
            for t in range(NT):
                act.activation(big[:, t, :], ps[0:TT, t, :], ACT.Silu, scale=acol[:, 2, t:t + 1]).then_inc(from_act, 1)

            with act.Fori(0, NT) as i:
                act.wait_ge(l1_m, i + 1)
                act.activation(pr1, sc1, ACT.Exp).then_inc(l1_p, 1)
                act.wait_ge(l1_t, i + 1)
                act.copy(pT1.rearrange("p (k h) n -> p k (h n)", k=4), ps[0:S, 2:6, :]).then_inc(l1_pt, 1)
            act.wait_ge(to_act, 1)
            act.activation(sm16[:, 6], sm16[:, 0], ACT.Sigmoid).then_inc(from_act, 1)
            with act.Fori(0, E1 // 2) as i:
                for p in range(2):
                    act.wait_ge(ex_gu, 2 * i + p + 1)
                    act.activation(exs[p], ps[0:D, 2 + 2 * p, 0:N], ACT.Silu).then_inc(ex_act, 1)

            act.wait_ge(product, PRODUCT["latent_qk"])
            for t in range(NT):
                act.activation(big2[:, t, :], ps[0:TT, t, :], ACT.Square).then_inc(from_act, 1)
            for t in range(NT):
                act.activation(big3[:, t, :], ps[0:TT, 4 + t, :], ACT.Square).then_inc(from_act, 1)
            act.wait_ge(product, PRODUCT["queries2"])
            for h in range(0, H8, 2):
                act.copy(qtT[:, h, :], ps[0:D, (4 + h) % 8, 0:N]).then_inc(from_act, 1)
            with act.Fori(0, B // 2) as i:
                for p in range(2):
                    b = 2 * i + p
                    for t in range(KT + 1):
                        n = (KT + 1) * b + t
                        rows = KP if t < KT else S
                        act.wait_ge(l2_sc, n + 3)
                        act.wait_ge(l2_pv, n + 1)
                        bias = kbias[:, bass.ds(b, 1), t] if t < KT else lbias[0:S, :]
                        act.activation(pexp[(t + p) % 2][0:rows], sscl[(t + p) % 2][0:rows], ACT.Exp, bias=bias)\
                            .then_inc(l2_p, 1)

            for t in range(NT):
                act.wait_ge(to_act, 2 + t)
                act.activation(big2[:, t, :], big[:, t, :], ACT.Gelu).then_inc(from_act, 1)

            with act.Fori(0, B // 2) as i:
                for p in range(2):
                    b = 2 * i + p
                    for t in range(KT):
                        n = KT * b + t
                        act.wait_ge(l3_s, n + 1)
                        act.wait_ge(l3_pv, n + 1)
                        act.activation(p3[t % 2].rearrange("p (k h) q -> p k (h q)", k=2),
                                       ps[0:KP, 2 * (t % 2):2 * (t % 2) + 2, 0:8 * S], ACT.Exp).then_inc(l3_p, 1)
            act.wait_ge(to_act, 6)
            act.activation(sm8[:, 0], sm8[:, 7], ACT.Exp).then_inc(from_act, 1)
            with act.Fori(0, E3 // 2) as i:
                for p in range(2):
                    for c in range(4):
                        act.wait_ge(ex_gu, E1 + 8 * i + 4 * p + c + 1)
                        act.activation(exs[c % 2], ps[0:D, 2 + 2 * (c % 2), 0:N], ACT.Gelu).then_inc(ex_act, 1)

        @block.gpsimd
        def _(pool):
            for p in range(2):
                pool.nop().then_inc(st[p], 96)
            pool.nop().then_inc(ex_acc, 2)
            ch = Chain(pool, pool_s)
            pool.wait_ge(ld_w, N_LOADS * 16)

            with pool.Fori(0, B // 2) as i, ch.loop(i, 2 * 4, B // 2):
                for p in range(2):
                    b = 2 * i + p
                    pool.wait_ge(c_hat, b + 1)
                    ch.link(pool.tensor_tensor(cln[p], cln[p], spread("L2_xw", KP, KT), ALU.mult))
                    pool.tensor_tensor(cln[p], cln[p], spread("L2_xb", KP, KT), ALU.add).then_inc(c_lned, 1)
                    pool.wait_ge(l0_w, b + 1)
                    pool.wait_ge(acc_used, b + 2)
                    ch.step(pool.tensor_copy(rhs0[:, :, D:D + 1], em[:, bass.ds(b, 1), :].rearrange("p o j -> p (o j)")
                                             .unsqueeze(2)))
                    ch.step(pool.tensor_copy(rhs0[:, :, D + 1:D + 2], em2[:, bass.ds(b, 1), :]
                                             .rearrange("p o j -> p (o j)").unsqueeze(2)))
                    pool.tensor_tensor(rhs0[:, :, 0:D], c_in[p], sm[:, 11, 0:KT].unsqueeze(2)
                                       .broadcast_to([KP, KT, D]), ALU.mult).then_inc(l0_rhs, 1)
                    pool.wait_ge(l0_kn, b + 2)
                    ch.link(pool.tensor_tensor(kn, kn, spread("L0_g", KP, KT), ALU.mult))
                    pool.tensor_tensor(kn, kn, spread("L0_b", KP, KT), ALU.add).then_inc(l0_kaff, 1)

            rs = [0]

            def rsqrt(n=1):
                for _ in range(n):
                    rs[0] += 1
                    pool.wait_ge(ln_var, rs[0])
                    pool.tensor_tensor(lnrs, lnve, nhalf[0:TT, 0:NT], ALU.pow).then_inc(ln_rstd, 1)

            rsqrt(3)
            rsqrt()
            rsqrt()

            def add_expert(e, p):
                pool.wait_ge(ex_w, e + 3)
                pool.tensor_tensor(y2, y2, big[:, :, D * p:D * p + D], ALU.add).then_inc(ex_acc, 1)

            rsqrt()
            ch.link(pool.memset(y2, 0.0))
            with pool.Fori(0, E1 // 2) as i:
                for p in range(2):
                    e = 2 * i + p
                    pool.wait_ge(ex_acc, e + 2)
                    add_expert(e, p)
            rsqrt(2)
            for k in range(2):
                rs[0] += 1
                pool.wait_ge(ln_var, rs[0])
                pool.tensor_tensor(qss[:, 2, :], qss[:, k, :], nhalf[0:TT, :], ALU.pow).then_inc(ln_rstd, 1)
            rsqrt()
            rsqrt(2)
            rsqrt()

            def queries(bv, p):
                pool.tensor_tensor(qst3[p], q3[:, :, bass.ds(bv * S, S)].unsqueeze(2).broadcast_to([D, 4, 4, S]),
                                   gm4.unsqueeze(1).unsqueeze(3).broadcast_to([D, 4, 4, S]), ALU.mult)\
                    .then_inc(l3_q, 1)

            pool.wait_ge(l3_free, 2)
            queries(0, 0)
            queries(1, 1)
            with pool.Fori(0, B // 2 - 1) as i:
                for p in range(2):
                    b = 2 * i + p
                    pool.wait_ge(l3_pv, KT * (b + 1) + 2)
                    queries(b + 2, p)

            rsqrt()
            ch.link(pool.memset(y2, 0.0))
            with pool.Fori(0, E3 // 2) as i:
                for p in range(2):
                    e = E1 + 2 * i + p
                    pool.wait_ge(ex_acc, e + 2)
                    add_expert(e, p)

        @block.vector
        def _(dve):
            ch = Chain(dve, dve_s)
            product_in, act_in = Count(dve, product), Count(dve, from_act)
            rstd_in = Count(dve, ln_rstd)
            ident = cs("ident")

            def tt(out, a, b, op):
                return dve.tensor_tensor(out, a, b, op)

            def over(col, shape):
                return col.unsqueeze(2).broadcast_to(shape)

            def signal(s, after=None):
                ch.sync()
                if after:
                    dve.wait_ge(operand, after)
                dve.nop().then_inc(s, 1)

            def layernorm(src, dst, eps, gain=None, bias=None):
                for t in range(NT):
                    ch.step(dve.bn_stats(lnst[:, t, :], src[:, t, :]))
                ch.sync()
                for t in range(NT):
                    ch.step(dve.bn_aggr(lnmv[:, t, :], lnst[:, t, :]))
                ch.sync()
                dve.tensor_scalar(lnve, lnmv[:, :, 1], eps, None, ALU.add).then_inc(ln_var, 1)
                rstd_in.next()
                for t in range(NT):
                    ch.step(dve.tensor_scalar(dst[:, t, :], src[:, t, :], lnmv[:, t, 0:1], lnrs[:, t:t + 1],
                                              ALU.subtract, ALU.mult))
                ch.sync()
                if gain:
                    ch.link(tt(dst, dst, spread(gain), ALU.mult))
                    ch.link(tt(dst, dst, spread(bias), ALU.add))

            def residual(k, src):
                ch.link(dve.scalar_tensor_tensor(x[:, :, :], src, tg[0:TT, k:k + 1], x[:, :, :],
                                                 ALU.mult, ALU.add))

            def turned(dst, k):
                product_in.next()
                dve.tensor_copy(dst, ps[0:D, k, 0:N]).then_inc(operand, 1)

            def quantise(src, tmp, dst, scales):
                width = src.shape[2]
                ch.link(dve.tensor_reduce(acol[:, 0, :], src, AX.X, ALU.max, apply_absolute_value=True))
                ch.link(dve.tensor_scalar(acol[:, 0, :], acol[:, 0, :], 1e-5, None, ALU.max))
                ch.link(dve.reciprocal(acol[:, 1, :], acol[:, 0, :]))
                ch.link(dve.tensor_scalar(acol[:, 1, :], acol[:, 1, :], 127.0, None, ALU.mult))
                for row, m in scales:
                    ch.step(dve.tensor_scalar(acol[:, row, :], acol[:, 0, :], 1.0 / 127.0, mw[0:TT, m:m + 1],
                                              ALU.mult, ALU.mult))
                ch.link(tt(tmp, src, over(acol[:, 1, :], [TT, NT, width]), ALU.mult))
                ch.link(dve.tensor_scalar(tmp, tmp, MAGIC, MAGIC, ALU.add, ALU.subtract))
                dve.tensor_scalar(dst, tmp, -128.0, 127.0, ALU.max, ALU.min).then_inc(operand, 1)

            dve.nop().then_inc(d_free, 3)
            dve.nop().then_inc(sq_used, 2)
            dve.nop().then_inc(acc_used, 2)
            dve.nop().then_inc(l0_kn, 1)
            dve.nop().then_inc(l2_sc, 2)
            dve.nop().then_inc(l2_pv, 2)
            dve.nop().then_inc(l3_mxd, 2)
            dve.nop().then_inc(l3_pv, 2)
            dve.nop().then_inc(l3_o, 1)
            dve.nop().then_inc(ex_h, 1)
            dve.nop().then_inc(ex_w, 2)
            for p in range(2):
                ch.step(dve.memset(v3[p], 0.0))
            ch.sync()
            for p in range(2):
                blocks = v3[p].rearrange("p j (g c) -> p j g c", c=32)
                ch.step(dve.memset(blocks[:, :, 0:4, 24:25], 1.0))
                ch.step(dve.memset(blocks[:, :, 4:6, 16:17], 1.0))
            dve.wait_ge(ld_w, N_LOADS * 16)
            dve.tensor_reduce(mw[:, :], wraw, AX.X, ALU.add, apply_absolute_value=True).then_inc(wsum_in, 1)
            ch.link(dve.tensor_reduce(colv[:, :], w_l0[:, :, :], AX.X, ALU.add))
            ch.link(dve.tensor_scalar(colv[:, :], colv[:, :], 1.0 / D, None, ALU.mult))
            ch.step(tt(w_l0[:, :, :], w_l0[:, :, :], over(colv[:, :], [D, 2, D]), ALU.subtract))
            ch.step(dve.tensor_copy(ident_h[:, :], ident))
            ch.step(dve.tensor_copy(gm4[:, :], cs("gmask")))
            ch.step(tt(em2, em, em, ALU.mult))
            ch.link(tt(qks[:, 0, :], qks[:, 0, :], qks[:, 1, :], ALU.mult))
            ch.link(dve.tensor_scalar(qks[:, 0, :], qks[:, 0, :], 8.0, None, ALU.mult))
            ch.link(dve.tensor_reduce(lbias[:, :], qks[:, 0, :], AX.X, ALU.max, apply_absolute_value=True))
            ch.link(dve.tensor_scalar(lbias[:, :], lbias[:, :], -1.0, None, ALU.mult))
            ch.link(dve.tensor_copy(kbias[:, :, :], kmask[:, :, :]))
            ch.link(dve.tensor_scalar(kbias[:, :, :], kbias[:, :, :], -1.0, -NEG, ALU.add, ALU.mult))
            ch.link(dve.tensor_scalar(kbias[:, :, :], kbias[:, :, :], lbias[0:KP, 0:1], None, ALU.add))
            dve.wait_ge(wsum, 1)
            ch.link(dve.tensor_scalar(mw[:, :], ps[0:D, 7, 0:5], 1.0 / (D * FF), 1e-5, ALU.mult, ALU.max))
            ch.link(dve.reciprocal(wscale[:, :], mw[:, :]))
            for m in range(5):
                ch.step(dve.tensor_scalar(wraw[:, m, :], wraw[:, m, :], wscale[:, m:m + 1], MAGIC,
                                          ALU.mult, ALU.add))
            ch.sync()
            ch.link(dve.tensor_scalar(wraw, wraw, MAGIC, -1.0, ALU.subtract, ALU.max))
            dve.tensor_scalar(wquant[:, :, :], wraw, 1.0, None, ALU.min).then_inc(w_ready, 1)

            with dve.Fori(0, B // 2) as i, ch.loop(i, 2 * 32, B // 2):
                for p in range(2):
                    b = 2 * i + p
                    dve.wait_ge(ld_c[p], 32 * (i + 1))
                    for j in range(KT):
                        ch.step(dve.bn_stats(stat[:, j, :], c_in[p][:, j, :]))
                    ch.sync()
                    n = KT
                    ch.step(tt(sm[:, 0, 0:n], stat[:, :, 1], stat[:, :, 4], ALU.add))
                    ch.step(tt(sm[:, 1, 0:n], stat[:, :, 1], stat[:, :, 4], ALU.subtract))
                    ch.link(tt(sm[:, 2, 0:n], stat[:, :, 2], stat[:, :, 5], ALU.add))
                    ch.step(dve.tensor_scalar(sm[:, 2, 0:n], sm[:, 2, 0:n], 1.0 / D, 1e-5, ALU.mult, ALU.add))
                    ch.step(dve.tensor_scalar(sm[:, 3, 0:n], sm[:, 0, 0:n], 0.5, None, ALU.mult))
                    ch.link(tt(sm[:, 1, 0:n], sm[:, 1, 0:n], sm[:, 1, 0:n], ALU.mult))
                    dve.scalar_tensor_tensor(sm[:, 4, 0:n], sm[:, 1, 0:n], 0.25, sm[:, 2, 0:n],
                                             ALU.mult, ALU.add).then_inc(c_var, 1)
                    dve.wait_ge(c_sd, b + 1)
                    ch.link(dve.reciprocal(sm[:, 6, 0:n], sm[:, 5, 0:n]))
                    dve.wait_ge(st[p], 96 * (i + 1))
                    for j in range(KT):
                        ins = dve.tensor_scalar(cln[p][:, j, :], c_in[p][:, j, :], sm[:, 3, j:j + 1],
                                                sm[:, 6, j:j + 1], ALU.subtract, ALU.mult)
                        if j < KT - 1:
                            ch.step(ins)
                    ins.then_inc(c_hat, 1)
                    dve.wait_ge(a_free, 21 * b + 3 + 9)
                    ch.link(dve.tensor_reduce(sm[:, 10, :].rearrange("p (j a) -> p j a", a=2), sq0, AX.X, ALU.add))
                    dve.tensor_scalar(sm[:, 7, :], sm[:, 10, :], 1.0 / D, 1e-6, ALU.mult, ALU.add)\
                        .then_inc(l0_var, 1)
                    for u in range(3):
                        dve.wait_ge(k_hi_ready, 3 * b + u + 1)
                        tt(k_lo[p][:, 500 * u:500 * u + 500], ps[0:D, 3 + u, 0:500],
                           k_hi[p][:, 500 * u:500 * u + 500], ALU.subtract).then_inc(d_free, 1)
                    dve.wait_ge(l0_sd, b + 1)
                    ch.link(dve.reciprocal(sm[:, 9, :], sm[:, 8, :]))
                    r = sm[:, 9, :].rearrange("p (j a) -> p j a", a=2)
                    tt(sm[:, 11, 0:n], r[:, :, 1], em2[:, bass.ds(b, 1), :].rearrange("p o j -> p (o j)"), ALU.mult)\
                        .then_inc(l0_w, 1)
                    tt(kn, kraw, r[:, :, 0:1].broadcast_to([KP, KT, D]), ALU.mult).then_inc(l0_kn, 1)
                    for u in range(3):
                        dve.wait_ge(d_full, 9 * b + 3 + u + 1)
                        src = ps[0:KP, 3 + u, :].rearrange("p (j n) -> p j n", j=4)
                        dst = v3[p][:, 4 * u:4 * u + 4, :]
                        dve.tensor_copy(dst[:, :, 0:128].rearrange("p j (g c) -> p j g c", c=32)[:, :, :, 0:24],
                                        src[:, :, 0:96].rearrange("p j (g c) -> p j g c", c=24))
                        dve.tensor_copy(dst[:, :, 128:192].rearrange("p j (g c) -> p j g c", c=32)[:, :, :, 0:16],
                                        src[:, :, 96:128].rearrange("p j (g c) -> p j g c", c=16))\
                            .then_inc(d_free, 1)
                    for u in range(3):
                        dve.wait_ge(d_full, 9 * b + 6 + u + 1)
                        dve.tensor_copy(clnT[p][:, 4 * u:4 * u + 4, :].rearrange("p j n -> p (j n)"),
                                        ps[0:D, 3 + u, 0:4 * KP]).then_inc(d_free, 1)
                    for j in range(KT):
                        if j == 2:
                            dve.wait_ge(l0_kaff, b + 1)
                            dve.tensor_scalar(kpr, kn, 0.0, 1e-6, ALU.max, ALU.add).then_inc(l0_kp, 1)
                        dve.wait_ge(a_free, 21 * b + 3 + 9 + j + 1)
                        dve.tensor_reduce(rn[:, bass.ds(b, 1), j, :].rearrange("p o h -> p (o h)"),
                                          sqk[:, j % 2, :].rearrange("p (h d) -> p h d", h=H8), AX.X, ALU.add)\
                            .then_inc(sq_used, 1)
                    dve.wait_ge(acc_full, b + 1)
                    dve.tensor_copy(kv_all[:, bass.ds(b, 1), :].rearrange("p o n -> p (o n)"),
                                    ps[0:D, 6 + p, 0:D + 2]).then_inc(acc_used, 1)
            dve.wait_ge(acc_used, B + 2)
            dve.wait_ge(sq_used, KT * B + 2)
            rn_flat = rn[:, :, :, :].rearrange("p b t h -> p (b t h)")
            dve.tensor_scalar(rn_flat, rn_flat, 1e-24, None, ALU.max).then_inc(rn_sq, 1)
            dve.nop().then_inc(ctx_done, 1)
            dve.nop().then_inc(operand, 1)

            for p in range(2):
                dve.wait_ge(st[p], 96 * (B // 2 + 1))
            ch.link(dve.memset(nhalf, -0.5))
            layernorm(x, z, 1e-5)
            product_in.next()
            dve.tensor_copy(kvt.rearrange("p b n -> p (b n)"), ps[0:D, 0:2, :].rearrange("p k n -> p (k n)"))\
                .then_inc(operand, 1)
            signal(operand, after=OPERAND["kvt"])
            dve.wait_ge(rn_sd, 1)
            ch.link(dve.reciprocal(rn_flat, rn_flat))
            product_in.next()
            ch.link(tt(kvm, ps[0:D, 2:4, :].rearrange("p k (b n) -> p (k b) n", b=4), spread("L0_g", D, B), ALU.mult))
            for b in range(B):
                ch.step(dve.scalar_tensor_tensor(kvm[:, b, :], spread("L0_b", D, 1)[:, 0, :], kv_all[:, b, D + 1:D + 2],
                                                 kvm[:, b, :], ALU.mult, ALU.add))
            ch.sync()
            blk = cs("blk").unsqueeze(1).broadcast_to([D, B, D])
            ch.step(tt(kvm, kvm, blk, ALU.mult))
            ch.step(tt(ksm, cs("hmask").unsqueeze(1).broadcast_to([D, B, 16]),
                       kv_all[:, :, D:D + 1].broadcast_to([D, B, 16]), ALU.mult))
            turned(xT, 4)
            product_in.next()
            ch.link(dve.tensor_copy(y.rearrange("p t n -> p (t n)"), ps[0:TT, 5, :]))
            layernorm(y, y2, 1e-6, "L0_g", "L0_b")
            dve.tensor_scalar(y2, y2, 0.0, 1e-6, ALU.max, ALU.add).then_inc(operand, 1)
            turned(xT, 4)
            product_in.next()
            ch.link(dve.tensor_scalar(rd0, ps[0:S, 5, 0:D].rearrange("p (b h) -> p b h", b=B), 1e-6, None, ALU.add))
            ch.link(dve.reciprocal(rd0, rd0))
            tt(at0.rearrange("p b (h e) -> p (b h) e", h=16), ps[0:S, 6:8, :].rearrange("p k (h e) -> p (k h) e", e=8),
               over(rd0.rearrange("p b h -> p (b h)"), [S, D, 8]), ALU.mult).then_inc(l0_att, 1)
            turned(xT2, 4)
            product_in.next()
            ch.link(tt(y, ps[0:TT, 0, :].rearrange("p (t n) -> p t n", t=NT), spread("L0_db"), ALU.add))
            layernorm(y, y, 1e-6, "L0_g", "L0_b")
            act_in.next()
            residual(0, y)

            layernorm(x, z, 1e-5)
            quantise(z, y, zq, ((2, 0), (3, 1)))
            product_in.next()
            dve.tensor_copy(zqT, ps[0:D, 0, 0:256].bitcast(BF16)[:, 0:N]).then_inc(operand, 1)
            product_in.next()
            for t in range(NT):
                act_in.next()
                ch.step(dve.scalar_tensor_tensor(big2[:, t, :], ps[0:TT, 4 + t, :], acol[:, 3, t:t + 1],
                                                 big[:, t, :], ALU.mult, ALU.mult))
            ch.sync()

            def down(scale_row, bias=None):
                for c in range(4):
                    if c == 0:
                        product_in.next()
                    ins = dve.tensor_copy(hqT[:, c, :], ps[0:D, c // 2, 256 * (c % 2):256 * (c % 2) + 256]
                                          .bitcast(BF16)[:, 0:N])
                    if c < 3:
                        ch.step(ins)
                ins.then_inc(operand, 1)
                product_in.next()
                for t in range(NT):
                    src = ps[0:TT, 2, D * t:D * t + D]
                    if bias:
                        ch.step(dve.scalar_tensor_tensor(y[:, t, :], src, acol[:, scale_row, t:t + 1],
                                                         spread(bias)[:, t, :], ALU.mult, ALU.add))
                    else:
                        ch.step(dve.tensor_scalar(y[:, t, :], src, acol[:, scale_row, t:t + 1], None, ALU.mult))
                ch.sync()

            quantise(big2, big3, hq, ((4, 2),))
            down(4)
            residual(4, y)

            turned(c56T, 0)
            product_in.next()
            dve.tensor_scalar(k1T, ps[0:D, 1, 0:N], w_col1[:, 1:2], None, ALU.add).then_inc(operand, 1)
            layernorm(x, z, 1e-5)
            signal(operand, after=OPERAND["k"])
            product_in.next()
            ch.step(tt(xT3, ps[0:D, 2, 0:N], cs("sink"), ALU.mult))
            ch.step(tt(k1T, k1T, cs("cosk"), ALU.mult))
            ch.step(tt(v1, ps[0:S, 3:5, :].rearrange("p k (b n) -> p (k b) n", b=4), spread("L1_vb", S, B), ALU.add))
            ch.sync()
            ch.step(tt(k1T, k1T, xT3, ALU.add))
            ch.step(dve.memset(qst, 0.0))
            turned(xT, 0)
            product_in.next()
            dve.tensor_scalar(q1T, ps[0:D, 1, 0:N], w_col1[:, 0:1], None, ALU.add).then_inc(operand, 1)
            ch.sync()
            product_in.next()
            ch.step(tt(xT3, ps[0:D, 2, 0:N], cs("sinq"), ALU.mult))
            ch.link(tt(q1T, q1T, cs("cosq"), ALU.mult))
            ch.link(tt(q1T, q1T, xT3, ALU.add))
            with dve.Fori(0, NT) as i, ch.loop(i, 9, NT):
                for e in range(2):
                    ch.step(tt(kblk[:, e], k1T[:, bass.ds((2 * i + e) * S, S)].unsqueeze(1).broadcast_to([D, 16, S]),
                               over(cs("hmask"), [D, 16, S]), ALU.mult))
                ch.step(dve.tensor_copy(qst[:, :, 0:S],
                                        q1T[:, bass.ds(2 * i * S, 2 * S)].rearrange("p (e s) -> p e s", e=2)))
                ch.sync()
                dve.tensor_copy(v1s, v1[:, bass.ds(2 * i, 2), :]).then_inc(l1_kq, 1)
                dve.wait_ge(l1_s, i + 1)
                ch.link(tt(sc1.rearrange("p (k h) s -> p k h s", k=2),
                           ps[:, 0:2, 0:8 * S].rearrange("p k (h s) -> p k h s", h=8),
                           cs("causal").unsqueeze(1).unsqueeze(1).broadcast_to([D, 2, 8, S]), ALU.add))
                ch.link(dve.tensor_reduce(m1[:, 0, :], sc1, AX.X, ALU.max))
                tt(sc1, sc1, over(m1[:, 0, :], [D, 16, S]), ALU.subtract).then_inc(l1_m, 1)
                dve.wait_ge(l1_p, i + 1)
                ch.link(dve.tensor_reduce(m1[:, 1, :], pr1, AX.X, ALU.add))
                ch.link(dve.reciprocal(m1[:, 2, :], m1[:, 1, :]))
                dve.wait_ge(l1_o, i + 1)
                tt(o1.rearrange("p (h d) -> p h d", h=16), ps[:, 6, 0:D].rearrange("p (h d) -> p h d", h=16),
                   over(m1[:, 2, :], [D, 16, 8]), ALU.mult).then_inc(l1_on, 1)
                dve.wait_ge(l1_ot, i + 1)
                ch.link(dve.tensor_copy(xT2[:, bass.ds(2 * i * S, 2 * S)].rearrange("p (e s) -> p e s", e=2),
                                        ps[0:D, 7, 0:D].rearrange("p (e s) -> p e s", e=2)[:, :, 0:S]))
                ch.link(dve.tensor_copy(m1[:, 1, :], m1[:, 2, :]))
            signal(operand)
            product_in.next()
            ch.link(tt(y, ps[0:TT, 0, :].rearrange("p (t n) -> p t n", t=NT), spread("L1_ob"), ALU.add))
            residual(1, y)

            def top2(v, n, low):
                rank = cs("rank", TT)[:, 0:n].unsqueeze(1).broadcast_to([TT, NT, n])
                for k in range(2):
                    src = v[:, k]
                    ch.link(dve.tensor_reduce(acol[:, 0, :], src, AX.X, ALU.max))
                    ch.link(tt(v[:, 2], src, over(acol[:, 0, :], [TT, NT, n]), ALU.is_equal))
                    ch.link(tt(v[:, 2], v[:, 2], rank, ALU.mult))
                    ch.link(dve.tensor_reduce(acol[:, 1, :], v[:, 2], AX.X, ALU.max))
                    ch.link(tt(v[:, 3 + k], v[:, 2], over(acol[:, 1, :], [TT, NT, n]), ALU.is_equal))
                    if k == 0:
                        ch.link(dve.scalar_tensor_tensor(v[:, 1], v[:, 3], low, src, ALU.mult, ALU.add))
                ch.link(tt(v[:, 5], v[:, 3], v[:, 4], ALU.add))

            layernorm(x, z, 1e-5)
            signal(operand)
            turned(xT, 0)
            product_in.next()
            dve.tensor_copy(sm16[:, 0], ps[0:TT, 1, 0:64].rearrange("p (t n) -> p t n", t=NT)).then_inc(to_act, 1)
            dve.wait_ge(to_act, 1)
            top2(sm16, 16, NEG)
            act_in.next()
            ch.step(tt(wts[:, :, 0:16], sm16[:, 5], sm16[:, 6], ALU.mult))
            ch.link(dve.memset(wts[:, :, 16:E1], 1.0))

            def hidden1(e, p):
                dve.wait_ge(ex_act, e + 1)
                tt((xT2, xT3)[p], ps[0:D, 3 + 2 * p, 0:N], exs[p], ALU.mult).then_inc(ex_h, 1)

            def weigh(e, p, weight, first):
                dve.wait_ge(ex_dn, first + e + 1)
                dve.wait_ge(ex_acc, first + e + 1)
                tt(big[:, :, D * p:D * p + D], ps[0:TT, 6 + p, :].rearrange("p (t n) -> p t n", t=NT),
                   weight.broadcast_to([TT, NT, D]), ALU.mult).then_inc(ex_w, 1)

            hidden1(0, 0)
            with dve.Fori(0, E1 // 2 - 1) as i:
                for p in range(2):
                    e = 2 * i + p
                    hidden1(e + 1, 1 - p)
                    weigh(e, p, wts[:, :, bass.ds(e, 1)], 0)
            hidden1(E1 - 1, 1)
            weigh(E1 - 2, 0, wts[:, :, E1 - 2:E1 - 1], 0)
            weigh(E1 - 1, 1, wts[:, :, E1 - 1:E1], 0)
            dve.wait_ge(ex_acc, E1 + 2)
            residual(5, y2)

            layernorm(x, z, 1e-5)
            layernorm(z, y, 1e-5, "L2_lw", "L2_lb")
            dve.nop().then_inc(lat_ready, 1)
            dve.nop().then_inc(operand, 1)
            for p in range(2):
                ch.step(dve.memset(cln_s[p][:, :, D:D + 1], 1.0))
            product_in.next()
            ch.step(dve.tensor_copy(m2.rearrange("p (c r) n -> p r c n", r=2),
                                    ps[0:D, 2:4, :].rearrange("p r (c n) -> p r c n", c=4)))
            dve.tensor_copy(xT, ps[0:D, 0, 0:N]).then_inc(operand, 1)
            ch.sync()
            dve.wait_ge(operand, OPERAND["latentsT"])
            dve.nop().then_inc(lat_ready, 1)
            product_in.next()
            act_in.next(4)
            ch.link(dve.tensor_reduce(qss[:, 0, :], big2.rearrange("p t (h d) -> p (t h) d", h=H8), AX.X, ALU.add))
            dve.tensor_scalar(qss[:, 0, :], qss[:, 0, :], 1e-24, None, ALU.max).then_inc(ln_var, 1)
            rstd_in.next()
            bigf = big.rearrange("p t (h d) -> p (t h) d", h=H8)
            ch.link(tt(bigf, ps[0:TT, 0:4, :].rearrange("p t (h d) -> p (t h) d", h=H8),
                       over(qss[:, 2, :], [TT, NT * H8, HD8]), ALU.mult))
            tt(bigf, bigf, qks[0:TT, 0, :].unsqueeze(1).broadcast_to([TT, NT * H8, HD8]), ALU.mult)\
                .then_inc(operand, 1)
            act_in.next(4)
            ch.link(dve.tensor_reduce(qss[:, 1, :], big3.rearrange("p t (h d) -> p (t h) d", h=H8), AX.X, ALU.add))
            dve.tensor_scalar(qss[:, 1, :], qss[:, 1, :], 1e-24, None, ALU.max).then_inc(ln_var, 1)
            rstd_in.next()
            dve.nop().then_inc(lat_ready, 1)
            product_in.next()
            dve.tensor_copy(qT2, ps[0:D, 0:4, 0:N]).then_inc(operand, 1)
            product_in.next()
            for h in range(1, H8, 2):
                ch.step(dve.tensor_copy(qtT[:, h, :], ps[0:D, (4 + h) % 8, 0:N]))
            act_in.next(4)
            signal(operand)
            dve.wait_ge(ld_m, 5 * 16)
            with dve.Fori(0, B // 2) as i, ch.loop(i, 2 * 3, B // 2):
                for p in range(2):
                    b = 2 * i + p
                    for t in range(KT + 1):
                        n = (KT + 1) * b + t
                        rows = KP if t < KT else S
                        norm = (rn[:, bass.ds(b, 1), t, :] if t < KT else rnl[:, bass.ds(b, 1), :])\
                            .rearrange("p o h -> p (o h)")
                        dve.wait_ge(l2_s, n + 1)
                        dve.wait_ge(l2_p, n + 1)
                        tt(sscl[(t + p) % 2][0:rows].rearrange("p (h q) -> p h q", h=H8),
                           ps[0:rows, (t + p) % 2, 0:N].rearrange("p (h q) -> p h q", h=H8),
                           over(norm, [rows, H8, S]), ALU.mult).then_inc(l2_sc, 1)
                    dve.wait_ge(l2_pv, (KT + 1) * (b + 1) + 2)
                    o012 = ps[0:TT, 4 + 2 * p, 0:387].rearrange("p (c n) -> p c n", c=3)
                    o3 = ps[0:TT, 5 + 2 * p, 0:D + 1]
                    ch.step(dve.reciprocal(rden[:, 0:3], o012[:, :, D]))
                    ch.link(dve.reciprocal(rden[:, 3:4], o3[:, D:D + 1]))
                    ch.step(tt(onrm[:, 0:3, :], o012[:, :, 0:D], over(rden[:, 0:3], [TT, 3, D]), ALU.mult))
                    dve.tensor_scalar(onrm[:, 3, :], o3[:, 0:D], rden[:, 3:4], None, ALU.mult).then_inc(l2_on, 1)
                    dve.wait_ge(l2_t, b + 1)
                    dve.tensor_copy(ctxT[:, :, bass.ds(b * S, S)],
                                    ps[0:D, 2, 0:N].rearrange("p (h q) -> p h q", h=H8)).then_inc(l2_done, 1)
            product_in.next()
            ch.link(dve.tensor_copy(y.rearrange("p t n -> p (t n)"), ps[0:TT, 0, :]))
            for p in range(2):
                ch.step(dve.memset(kst[p], 0.0))
            ch.sync()
            for p in range(2):
                ch.step(dve.memset(kst[p][0:1], 1.0))
            signal(l3_free)
            layernorm(y, y, 1e-5, "L2_ow", "L2_ob")
            residual(2, y)

            layernorm(x, z, 1e-5)
            layernorm(z, z, 1e-5, "L2f_g", "L2f_be")
            quantise(z, y, zq, ((2, 3),))
            product_in.next()
            dve.tensor_copy(zqT, ps[0:D, 0, 0:256].bitcast(BF16)[:, 0:N]).then_inc(operand, 1)
            product_in.next()
            for t in range(NT):
                dve.scalar_tensor_tensor(big[:, t, :], ps[0:TT, t, :], acol[:, 2, t:t + 1], b1v[0:TT, :],
                                         ALU.mult, ALU.add).then_inc(to_act, 1)
            act_in.next(4)
            quantise(big2, big3, hq, ((4, 4),))
            down(4, "L2f_b2")
            residual(6, y)

            layernorm(x, z, 1e-5)
            signal(operand)
            turned(xT, 0)
            product_in.next()
            ch.link(dve.tensor_scalar(xT2, ps[0:D, 1, 0:N], float(D) ** -0.5, None, ALU.mult))
            ch.link(dve.tensor_copy(q_hi, xT2))
            tt(q_lo, xT2, q_hi, ALU.subtract).then_inc(operand, 1)
            product_in.next()
            ch.step(dve.tensor_copy(q3, ps[0:D, 0:4, 0:N]))
            signal(l3_free)

            def maxima(bn, pn):
                for u in range(24):
                    dve.wait_ge(l3_mx, 24 * bn + u + 1)
                    dve.tensor_reduce(mx3[:, u // 3, u % 3:u % 3 + 1], ps[0:TT, 4 + u % 2, 0:500], AX.X, ALU.max)\
                        .then_inc(l3_mxd, 1)
                dve.wait_ge(l3_mxd, 24 * bn + 26)
                ch.link(dve.tensor_reduce(m3, mx3, AX.X, ALU.max, negate=True))
                tt(diag3, ident[0:TT, 0:TT].unsqueeze(1).broadcast_to([TT, 8, TT]), over(m3, [TT, 8, TT]), ALU.mult)\
                    .then_inc(l3_dg, 1)
                for half in range(2):
                    dve.wait_ge(l3_sh, 2 * bn + half + 1)
                    dve.tensor_copy(qst3[pn][0:1, 2 * half:2 * half + 2].rearrange("p g h q -> p (g h q)"),
                                    ps[0:1, 7, 0:4 * TT]).then_inc(l3_row, 1)

            def outputs(b):
                dve.wait_ge(l3_pv, KT * (b + 1) + 2)
                at_b = bass.ds(b, 1)
                ch.link(dve.tensor_copy(oA[:, at_b].rearrange("p o h q -> p (o h q)"), ps[0:D, 6, 0:168]))
                dve.tensor_copy(oB[:, at_b].rearrange("p o h q -> p (o h q)"), ps[0:64, 6, 168:280])\
                    .then_inc(l3_o, 1)

            maxima(0, 0)
            with dve.Fori(0, B // 2 - 1) as i, ch.loop(i, 2 * 2, B // 2 - 1):
                for p in range(2):
                    maxima(2 * i + p + 1, 1 - p)
                    outputs(2 * i + p)
            maxima(B - 1, 1)
            outputs(B - 2)
            outputs(B - 1)
            product_in.next()
            ch.link(dve.reciprocal(xT3, ps[0:D, 1, 0:N]))
            tt(xT2, ps[0:D, 0, 0:N], xT3, ALU.mult).then_inc(operand, 1)
            product_in.next()
            ch.link(tt(y, ps[0:TT, 2, :].rearrange("p (t n) -> p t n", t=NT), spread("L3_bo"), ALU.add))
            residual(3, y)

            layernorm(x, z, 1e-5)
            signal(operand)
            turned(xT, 0)
            product_in.next()
            logits = ps[0:TT, 1, 0:4 * E3].rearrange("p (t n) -> p t n", t=NT)
            ch.link(dve.tensor_reduce(acol[:, 5, :], logits, AX.X, ALU.max))
            tt(sm8[:, 7], logits, over(acol[:, 5, :], [TT, NT, E3]), ALU.subtract).then_inc(to_act, 1)
            act_in.next()
            top2(sm8, E3, -4.0)
            ch.link(tt(sm8[:, 5], sm8[:, 5], sm8[:, 0], ALU.mult))
            ch.link(dve.tensor_reduce(acol[:, 0, :], sm8[:, 5], AX.X, ALU.add))
            ch.link(dve.reciprocal(acol[:, 1, :], acol[:, 0, :]))
            ch.link(tt(wt3, sm8[:, 5], over(acol[:, 1, :], [TT, NT, E3]), ALU.mult))

            def expert3(e, p, first=False):
                for c in range(4):
                    dve.wait_ge(ex_act, E1 + 4 * e + c + 1)
                    tt(h3[p][:, c, :], ps[0:D, 3 + 2 * (c % 2), 0:N], exs[c % 2], ALU.mult).then_inc(ex_h, 1)
                    if c == 1 and not first:
                        weigh(e - 1, 1 - p, wt3[:, :, bass.ds(e - 1, 1)], E1)

            expert3(0, 0, first=True)
            expert3(1, 1)
            with dve.Fori(1, E3 // 2) as i:
                for p in range(2):
                    expert3(2 * i + p, p)
            weigh(E3 - 1, 1, wt3[:, :, E3 - 1:E3], E1)
            dve.wait_ge(ex_acc, E1 + E3 + 2)
            residual(7, y2)
            dve.nop().then_inc(out_ready, 1)


def kernel(**inputs):
    import concourse.bacc as bacc
    from concourse.bass_utils import run_bass_kernel_spmd

    a = {name: np.asarray(v) for name, v in inputs.items()}

    def chunks(w):
        return w.reshape(4, D, -1).transpose(1, 0, 2)

    cst, sel = constants()
    wkv = a["L2_xattn_Wkv"]
    shared_gu = [np.concatenate([a[f"L1_ffn_shared_{m}_w"][D * k:D * k + D].T for m in ("gate", "up")], axis=1)
                 for k in range(2)]
    shared_dn = [a["L1_ffn_shared_down_w"][:, D * k:D * k + D].T for k in range(2)]
    io = {
        "ctx": a["ctx_1024"],
        "cst": cst,
        "sel": sel,
        "vec": np.stack([a[n] for n in (
            "L0_xattn_ln_gamma", "L0_xattn_ln_beta", "L0_xattn_dense_b", "L1_xattn_v_b", "L1_xattn_o_b",
            "L2_xattn_ln_x_w", "L2_xattn_ln_x_b", "L2_xattn_ln_l_w", "L2_xattn_ln_l_b", "L2_xattn_ln_o_w",
            "L2_xattn_ln_o_b", "L2_ffn_b2", "L2_ffn_gamma", "L2_ffn_beta", "L3_xattn_bo")]),
        "wquant": np.stack([a["L0_ffn_w_gate"].T, a["L0_ffn_w_up"].T, chunks(a["L0_ffn_w_down"].T).reshape(D, FF),
                            a["L2_ffn_w1"].T, chunks(a["L2_ffn_w2"].T).reshape(D, FF)], axis=1),
        "L0_wk": a["L0_xattn_wk"],
        "L0_wv": a["L0_xattn_wv"],
        "L0_wq": a["L0_xattn_wq"],
        "L0_wd": a["L0_xattn_dense_w"],
        "L2_wk": wkv[:, :I2],
        "L3_wkT": a["L3_xattn_Wk"].T,
        "L3_wvT": a["L3_xattn_Wv"].T,
        "L3_wqT": a["L3_xattn_Wq"].T,
        "L3_woT": a["L3_xattn_Wo"].T,
        "L3_router": a["L3_ffn_gate_w"].T,
        "mask": a["mask_BxS2_ff1"],
        "kmask": a["mask_BxS2_bk0"],
        "qks": np.stack([a["L2_xattn_q_scale"], a["L2_xattn_k_scale"]]),
        "b1": a["L2_ffn_b1"],
        "gates": np.concatenate([a["g_xattn"], a["g_ffn"]]),
        "x": a["x"].reshape(N, D),
        "L1_w": np.stack([a[f"L1_xattn_{n}_w"].T for n in "qkvo"], axis=1),
        "L1_cols": np.stack([a["L1_xattn_q_b"], a["L1_xattn_k_b"]], axis=1),
        "L1_router": a["L1_ffn_router_w"].T,
        "L1_gu": np.concatenate([a["L1_ffn_gate_up_w"], np.stack(shared_gu)]),
        "L1_dn": np.concatenate([a["L1_ffn_down_w"], np.stack(shared_dn)]),
        "L2_wkT": chunks(wkv[:, :I2].T),
        "L2_wvT": chunks(wkv[:, I2:].T),
        "L2_wo": chunks(a["L2_xattn_Wo"]),
        "L2_wq": a["L2_xattn_Wq"],
        "L3_gu": a["L3_ffn_gate_up_w"].transpose(0, 2, 1),
        "L3_dn": a["L3_ffn_down_w"].transpose(0, 2, 1).reshape(E3, 4, D, D).transpose(0, 2, 1, 3),
    }
    io = {name: np.ascontiguousarray(v) for name, v in io.items()}
    nc = bacc.Bacc("TRN2", target_bir_lowering=False, num_devices=1)
    aps = {name: nc.dram_tensor(f"in_{name}", v.shape, mybir.dt.from_np(v.dtype), kind="ExternalInput").ap()
           for name, v in io.items()}
    out = nc.dram_tensor("out_x", (N, D), F32, kind="ExternalOutput").ap()
    build(nc, aps, out)
    r = run_bass_kernel_spmd(nc, [{f"in_{name}": v for name, v in io.items()}], core_ids=[0])
    return r.results[0]["out_x"].reshape(B, S, D)
```

```python
from contextlib import ExitStack, contextmanager

import numpy as np

import concourse.bass as bass
from concourse import mybir

F32 = mybir.dt.float32
F16 = mybir.dt.float16
BF16 = mybir.dt.bfloat16
U8 = mybir.dt.uint8
ALU = mybir.AluOpType
ACT = mybir.ActivationFunctionType
AX = mybir.AxisListType

D = 128
B = 8
S = 56
N = B * S
NT = 4
TT = N // NT
C = 1500
KT = 12
KP = C // KT
CL = C + S
H16, HD16 = 16, 8
H8, HD8 = 8, 64
I2 = H8 * HD8
FF = 512
E1 = 18
E3 = 8
MAGIC = 12582912.0
NEG = -1e30

CST = {}
_at = 0
for _name, _n in (("ident", D), ("blk", D), ("causal", S), ("cosq", N), ("sinq", N), ("cosk", N), ("sink", N),
                  ("rot", D), ("mean", D), ("hmask", 16), ("numA", 3 * D), ("denA", 3 * D),
                  ("numB", 2 * D), ("denB", 2 * D), ("rank", 16), ("gmask", 4)):
    CST[_name] = (_at, _at + _n)
    _at += _n
CST_N = _at


def constants():
    c = np.zeros((D, CST_N), np.float32)

    def put(name, a):
        a = np.asarray(a, np.float32)
        c[:a.shape[0], CST[name][0]:CST[name][1]] = a.reshape(a.shape[0], -1)

    f = np.arange(D)
    put("ident", np.eye(D))
    put("blk", f[:, None] // HD16 == f[None, :] // HD16)
    causal = np.where(np.arange(S)[None, :] > np.arange(64)[:, None], NEG, 0.0)
    put("causal", np.concatenate([causal, causal]))
    half = HD16 // 2
    freqs = np.float32(1.0) / np.float32(10000.0) ** (np.arange(half, dtype=np.float32) / np.float32(half))
    ang = np.tile(np.arange(S, dtype=np.float32), B)[None, :] * freqs[f % half][:, None]
    cos, sin = np.cos(ang), np.sin(ang)
    put("cosk", cos)
    put("sink", sin)
    put("cosq", cos * np.float32(HD16 ** -0.5))
    put("sinq", sin * np.float32(HD16 ** -0.5))
    rot = np.zeros((D, D))
    for i in f:
        if i % HD16 < half:
            rot[i + half, i] = -1.0
        else:
            rot[i - half, i] = 1.0
    put("rot", rot)
    put("mean", np.ones((D, D)))
    put("hmask", f[:, None] // HD16 == np.arange(16)[None, :])
    num_a, den_a = np.zeros((D, 3, D)), np.zeros((D, 3, D))
    num_b, den_b = np.zeros((D, 2, D)), np.zeros((D, 2, D))
    for g in range(4):
        for h in range(3):
            for d in range(HD16):
                num_a[32 * g + 8 * h + d, h, (3 * g + h) * 8 + d] = 1.0
                den_a[32 * g + 24, h, (3 * g + h) * 8 + d] = 1.0
    for g in range(2):
        for h in range(2):
            for d in range(HD16):
                num_b[32 * g + 8 * h + d, h, (12 + 2 * g + h) * 8 + d] = 1.0
                den_b[32 * g + 16, h, (12 + 2 * g + h) * 8 + d] = 1.0
    put("numA", num_a)
    put("denA", den_a)
    put("numB", num_b)
    put("denB", den_b)
    put("rank", np.tile(16.0 - np.arange(16), (D, 1)))
    put("gmask", f[:, None] // 32 == np.arange(4)[None, :])
    sel = np.zeros((D, 2, 4, D), np.float16)
    for g in range(4):
        for hh in range(4):
            for d in range(HD16):
                src = (4 * g + hh) * 8 + d
                sel[src, 0, g, 32 * hh + 8 + d] = 1.0
                sel[src, 0, g, 32 * hh + 16 + d] = 1.0
                sel[src, 1, g, 32 * hh + 24 + d] = 1.0
    pad = np.zeros((2, 8, C), np.float16)
    pad[0, 0] = 1.0
    return c, sel, pad


N_LOADS = 20
L1_LOADS = 5
G1 = 3
PRODUCT = {"ffn0_in": 10, "latent_q": 23, "latent_k": 24, "latent_qT": 25, "queries2": 26}
RSTD = {"latent_k": 9}
MAX_BANKS = (4, 5, 7)
OPERAND = {"kvt": 2, "k": 13, "latentsT": 21}


V128 = ["L0_g", "L0_b", "L0_db", "L1_vb", "L1_ob", "L2_xw", "L2_xb", "L2_lw", "L2_lb", "L2_ow", "L2_ob",
        "L2f_b2", "L2f_g", "L2f_be", "L3_bo"]
V64 = ["qs", "ks"]



class Chain:

    def __init__(self, eng, sem):
        self.eng, self.sem, self.n, self.turns = eng, sem, 0, None

    def step(self, ins):
        ins.then_inc(self.sem, 1)
        self.n += 1

    def sync(self):
        self.eng.wait_ge(self.sem, self.n if self.turns is None else self.turns + self.n)

    def link(self, ins):
        self.step(ins)
        self.sync()

    @contextmanager
    def loop(self, i, per_turn, turns):
        before = self.n
        self.turns = i * per_turn
        yield
        assert self.n - before == per_turn, self.n - before
        self.turns = None
        self.n = before + per_turn * turns


class Count:

    def __init__(self, eng, sem):
        self.eng, self.sem, self.n = eng, sem, 0

    def next(self, k=1):
        self.n += k
        self.eng.wait_ge(self.sem, self.n)


def build(nc, io, out):
    ctx = ExitStack()
    with ctx:
        def sb(name, shape, dt=F32):
            return ctx.enter_context(nc.sbuf_tensor(name, shape, dt))[tuple(slice(0, n) for n in shape)]

        def sem(name):
            return ctx.enter_context(nc.semaphore(name))

        d_cln = nc.dram_tensor("d_cln", (B, KP, KT * D), F32).ap()
        d_clnT = nc.dram_tensor("d_clnT", (B, D, C), F32).ap()
        d_k3 = nc.dram_tensor("d_k3", (B, 4, 4, 24, C), F16).ap()
        d_v3 = nc.dram_tensor("d_v3", (B, KP, KT * 192), F32).ap()
        d_att = nc.dram_tensor("d_att", (B, H16, S, HD16), F32).ap()
        d_lat = nc.dram_tensor("d_lat", (N, D), F32).ap()
        d_latT = nc.dram_tensor("d_latT", (D, N), F32).ap()
        d_rl = nc.dram_tensor("d_rl", (N, H8), F32).ap()

        ps = ctx.enter_context(nc.psum_tensor("ps", [128, 8, 512], F32))

        cst = sb("cst", [D, CST_N])
        sel = sb("sel", [D, 2, 4, D], F16)
        vec = sb("vec", [D, len(V128), D])
        qks = sb("qks", [D, 2, HD8])
        b1v = sb("b1v", [D, FF])
        gates = sb("gates", [D, 8])
        tg = sb("tg", [D, 8])
        colv = sb("colv", [D, 2])
        ident_h = sb("ident_h", [D, D], BF16)
        em = sb("em", [KP, B, KT])
        em2 = sb("em2", [KP, B, KT])
        kmask = sb("kmask", [KP, B, KT], U8)
        kbias = sb("kbias", [KP, B, KT])
        lbias = sb("lbias", [D, 1])
        w_l0 = sb("w_l0", [D, 2, D])
        w_q0 = sb("w_q0", [D, D])
        w_d0 = sb("w_d0", [D, D])
        w_k2 = sb("w_k2", [D, I2])
        w_k3 = sb("w_k3", [D, D])
        w_v3 = sb("w_v3", [D, D])
        w_q3 = sb("w_q3", [D, D])
        w_o3 = sb("w_o3", [D, D])
        w_r3 = sb("w_r3", [D, E3])
        wquant = sb("wquant", [D, 5, FF], BF16)
        mw = sb("mw", [D, 5])
        wscale = sb("wscale", [D, 5])
        gm4 = sb("gm4", [D, 4], F16)
        x = sb("x", [TT, NT, D])
        kv_all = sb("kv_all", [D, B, D + 2])
        rn = sb("rn", [KP, B, KT, H8])
        wex = [sb(f"wex{i}", [D, 3 * FF]) for i in range(2)]

        def cs(name, rows=D):
            a, b = CST[name]
            return cst[0:rows, a:b]

        def spread(name, rows=TT, n=NT):
            return vec[0:rows, V128.index(name), :].unsqueeze(1).broadcast_to([rows, n, D])

        ARENA = 34500
        arena = sb("arena", [D, ARENA])
        at = [0]

        def carve(shape, dt=F32):
            n = int(np.prod(shape[1:]))
            words = n if dt == F32 else (n + 1) // 2
            a = arena[0:shape[0], at[0]:at[0] + words]
            at[0] += words
            assert at[0] <= ARENA, at[0]
            if dt != F32:
                a = a.bitcast(dt)
            if len(shape) == 2:
                return a
            names = "abcd"[:len(shape) - 1]
            return a.rearrange("p (" + " ".join(names) + ") -> p " + " ".join(names),
                               **dict(zip(names[1:], shape[2:])))

        c_in = [carve([KP, KT, D]) for _ in range(2)]
        cln = [carve([KP, KT, D]) for _ in range(2)]
        cT = [carve([D, KT, KP]) for _ in range(2)]
        clnT = [carve([D, KT, KP]) for _ in range(2)]
        kraw = carve([KP, KT, D])
        sq0 = carve([KP, KT, 2, D])
        kn = carve([KP, KT, D])
        kpr = carve([KP, KT, D])
        rhs0 = carve([KP, KT, D + 2])
        k_hi = [carve([D, C], F16) for _ in range(2)]
        k_lo = [carve([D, C], F16) for _ in range(2)]
        v3 = [carve([KP, KT, 192]) for _ in range(2)]
        sqk = carve([KP, 2, I2])
        stat = carve([KP, KT, 6])
        sm = carve([KP, 16, 24])
        wraw = carve([D, 5, FF])

        at[0] = 0
        z = carve([TT, NT, D])
        y = carve([TT, NT, D])
        y2 = carve([TT, NT, D])
        xT = carve([D, N])
        xT2 = carve([D, N])
        xT3 = carve([D, N])
        big = carve([TT, NT, FF])
        big2 = carve([TT, NT, FF])
        big3 = carve([TT, NT, FF])
        zq = carve([TT, NT, D], BF16)
        zqT = carve([D, N], BF16)
        hq = carve([TT, NT, FF], BF16)
        hqT = carve([D, 4, N], BF16)
        lnst = carve([TT, NT, 6])
        lnmv = carve([TT, NT, 2])
        lnve = carve([TT, NT])
        lnrs = carve([TT, NT])
        nhalf = carve([D, 32])
        acol = carve([TT, 6, NT])
        qss = carve([TT, 3, NT * H8])
        exs = [carve([D, N]) for _ in range(2)]
        core_end = at[0]
        kvm = carve([D, B, D])
        kvt = carve([D, B, D])
        ksm = carve([D, B, 16])
        at0 = carve([S, B, D])
        rd0 = carve([S, B, 16])
        c56 = carve([TT, NT, D])
        c56T = carve([D, N])
        k1T = carve([D, N])
        q1T = carve([D, N])
        v1 = carve([S, B, D])
        w_l1 = carve([D, 4, D])
        w_col1 = carve([D, 2])
        kblk = carve([D, 2, 16, S])
        qst = carve([D, 2, 64])
        v1s = carve([S, 2, D])
        sc1 = carve([D, 16, S])
        pr1 = carve([D, 16, S])
        pT1 = carve([S, 16, D])
        m1 = carve([D, 3, 16])
        o1 = carve([D, D])
        w_r1 = carve([D, 16])
        sm16 = carve([TT, 8, NT, 16])
        wts = carve([TT, NT, E1])
        l1_end = at[0]
        at[0] = core_end
        clnT_s = [carve([D, CL]) for _ in range(2)]
        cln_s = [carve([KP, KT + 1, D + 1]) for _ in range(2)]
        qtT = carve([D, H8, N])
        ctxT = carve([D, H8, N])
        qT2 = ctxT
        sscl = [carve([KP, N]) for _ in range(2)]
        pexp = [carve([KP, N]) for _ in range(2)]
        onrm = carve([TT, 4, D])
        rden = carve([TT, 4])
        rnl = carve([S, B, H8])
        at[0] = max(at[0], l1_end)
        m2 = carve([D, H8, D])
        w_kT2 = carve([D, 4, D])
        w_vT2 = carve([D, 4, D])
        w_o2 = carve([D, 4, D])
        w_q2 = carve([D, I2])
        qk_col = carve([D, 2])
        at[0] = core_end
        kst = [carve([D, 4, C], F16) for _ in range(2)]
        v3s = [carve([KP, KT, 192]) for _ in range(2)]
        q3 = carve([D, 4, N], F16)
        q_hi = carve([D, N], F16)
        q_lo = carve([D, N], F16)
        qst3 = carve([D, B, 4, 4, S], F16)
        ones_h = carve([D, 2], F16)
        p3 = [carve([KP, 16, S]) for _ in range(2)]
        oA = carve([D, B, 3, S])
        oB = carve([64, B, 2, S])
        mx3 = carve([TT, 8, 3])
        m3 = carve([TT, 8])
        diag3 = carve([TT, 8, TT], F16)
        sm8 = carve([TT, 8, NT, 8])
        wt3 = carve([TT, NT, 8])
        at[0] = core_end
        h3 = [carve([D, 4, N]) for _ in range(2)]

        ld_c = [sem(f"context_loaded{i}") for i in range(2)]
        ld_w = sem("weights_loaded")
        ld_x = sem("x_loaded")
        st = [sem(f"context_results_stored{i}") for i in range(2)]
        a_full, a_free = sem("act_banks_full"), sem("act_banks_free")
        d_full, d_free = sem("dve_banks_full"), sem("dve_banks_free")
        wsum_in, wsum = sem("weight_sums_ready"), sem("weight_sums_summed")
        w_ready = sem("weights_ready")
        c_var, c_sd = sem("context_variance"), sem("context_deviation")
        c_hat, c_lned = sem("context_normalised"), sem("context_affine")
        l0_var, l0_sd = sem("l0_variance"), sem("l0_deviation")
        l0_kn, l0_kaff = sem("l0_keys_normalised"), sem("l0_keys_affine")
        l0_w, l0_rhs = sem("l0_value_weights"), sem("l0_rhs_ready")
        l0_kp = sem("l0_kprime_ready")
        k_hi_ready = sem("l3_k_hi_ready")
        sq_used = sem("l2_squares_used")
        acc_full, acc_used = sem("kv_sums_full"), sem("kv_sums_used")
        rn_sq, rn_sd = sem("l2_key_squares"), sem("l2_key_norms")
        dve_s, pool_s, act_s = sem("dve_steps"), sem("pool_steps"), sem("act_steps")
        pe_passed = sem("tensor_waits_passed")
        operand, product = sem("operand_ready"), sem("product_ready")
        to_act, from_act = sem("act_input_ready"), sem("act_output_ready")
        ln_var, ln_rstd = sem("variance_ready"), sem("rstd_ready")
        ctx_done = sem("context_pass_done")
        l0_att = sem("l0_attention_ready")
        l0_st, l0_ld = sem("l0_attention_stored"), sem("l0_attention_loaded")
        l1_ld = sem("l1_loaded")
        l1_kq, l1_s, l1_m = sem("l1_operands"), sem("l1_scores"), sem("l1_shifted")
        l1_p, l1_t, l1_pt = sem("l1_probs"), sem("l1_probs_transposed"), sem("l1_probsT_ready")
        l1_o, l1_on, l1_ot = sem("l1_out"), sem("l1_out_normalised"), sem("l1_out_transposed")
        l1_done = sem("l1_pair_done")
        ex_ld = [sem(f"expert_loaded{i}") for i in range(2)]
        ex_gu, ex_act, ex_h = sem("expert_gate_up"), sem("expert_activated"), sem("expert_hidden")
        ex_dn, ex_w, ex_acc = sem("expert_down"), sem("expert_weighted"), sem("expert_added")
        ld_m = sem("layer_weights_loaded")
        st_m = sem("latents_stored")
        l2_ld = [sem(f"l2_loaded{i}") for i in range(2)]
        l2_s, l2_sc, l2_p, l2_pv = sem("l2_sim"), sem("l2_scaled"), sem("l2_probs"), sem("l2_pv_tile")
        ld_rn = sem("latent_key_norms_loaded")
        l2_zero = sem("l2_queries_zeroed")
        l2_on, l2_t, l2_done = sem("l2_out_normalised"), sem("l2_out_transposed"), sem("l2_batch_done")
        l3_ld = [[sem(f"l3_keys_loaded{i}_{u}") for u in range(3)] for i in range(2)]
        l3_ldv = [sem(f"l3_values_loaded{i}") for i in range(2)]
        l3_pad = sem("l3_pad_loaded")
        l3_q, l3_mx, l3_mxd = sem("l3_queries_ready"), sem("l3_max_sim"), sem("l3_max_done")
        l3_dg, l3_sh, l3_row = sem("l3_diag_ready"), sem("l3_shift_row"), sem("l3_shift_copied")
        l3_s, l3_p, l3_pv, l3_o = sem("l3_sim"), sem("l3_probs"), sem("l3_pv_tile"), sem("l3_out_copied")
        st_out = sem("out_stored")
        lat_ready, l3_free, out_ready = sem("latents_ready"), sem("l2_memory_free"), sem("out_ready")

        block = ctx.enter_context(nc.Block())

        def batch(t, b):
            names = "abcd"[:len(t.shape) - 2]
            return t[bass.ds(b, 1)].rearrange("o p " + " ".join(names) + " -> (o p) " + " ".join(names))

        k3_in = d_k3.rearrange("n g e (s d) c -> n s (g e) d c", s=3)

        @block.sync
        def _(sp):
            def load_context(b, p):
                src = io["ctx"][bass.ds(b, 1)].rearrange("o (p j) d -> (o p) j d", j=KT)
                sp.dma_start(c_in[p][0:112], src[0:112]).then_inc(ld_c[p], 16)
                sp.dma_start(c_in[p][112:KP], src[112:KP]).then_inc(ld_c[p], 16)

            load_context(0, 0)
            loads = [(cst[:, :], io["cst"]), (w_l0[:, 0, :], io["L0_wk"]), (w_l0[:, 1, :], io["L0_wv"]),
                     (vec[:, :, :], io["vec"].unsqueeze(0).broadcast_to([D, len(V128), D])),
                     (wraw, io["wquant"]), (w_k2[:, :], io["L2_wk"]), (w_k3[:, :], io["L3_wkT"]),
                     (w_v3[:, :], io["L3_wvT"]), (sel[:, :, :, :], io["sel"]),
                     (em[:, :, :], io["mask"].rearrange("b (p j) -> p b j", j=KT)),
                     (kmask[:, :, :], io["kmask"].rearrange("b (p j) -> p b j", j=KT)),
                     (w_q0[:, :], io["L0_wq"]), (w_d0[:, :], io["L0_wd"]),
                     (w_r3[:, :], io["L3_router"]), (w_q3[:, :], io["L3_wqT"]), (w_o3[:, :], io["L3_woT"]),
                     (qks[:, :, :], io["qks"].unsqueeze(0).broadcast_to([D, 2, HD8])),
                     (b1v[:, :], io["b1"].unsqueeze(0).broadcast_to([D, FF])),
                     (gates[:, :], io["gates"].unsqueeze(0).broadcast_to([D, 8])),
                     (x[:, :, :], io["x"].rearrange("(t p) d -> p t d", p=TT))]
            for dst, src in loads:
                sp.dma_start(dst, src).then_inc(ld_w, 16)
            load_context(1, 1)

            def store_results(b, p):
                sp.wait_ge(c_lned, b + 1)
                sp.dma_start(batch(d_cln, b), cln[p].rearrange("p j d -> p (j d)")).then_inc(st[p], 16)
                sp.wait_ge(d_free, 9 * b + 3 + 3)
                for s, part in enumerate((k_hi[p], k_lo[p], k_hi[p])):
                    sp.dma_start(k3_in[bass.ds(b, 1), s].rearrange("o h d c -> (o h) d c"), part).then_inc(st[p], 16)
                sp.wait_ge(d_free, 9 * b + 3 + 6)
                sp.dma_start(batch(d_v3, b), v3[p].rearrange("p j d -> p (j d)")).then_inc(st[p], 16)
                sp.wait_ge(d_free, 9 * b + 3 + 9)
                sp.dma_start(batch(d_clnT, b), clnT[p].rearrange("p j d -> p (j d)")).then_inc(st[p], 16)

            with sp.Fori(0, B // 2 - 1) as i:
                for p in range(2):
                    b = 2 * i + p
                    store_results(b, p)
                    sp.wait_ge(d_full, 9 * b + 9)
                    sp.wait_ge(l0_rhs, b + 1)
                    load_context(b + 2, p)
            for b in (B - 2, B - 1):
                store_results(b, b % 2)
            for p in range(2):
                sp.wait_ge(st[p], 96 * (B // 2 + 1))

            sp.wait_ge(ctx_done, 1)
            for e in range(2):
                sp.dma_start(c56[S * e:S * e + S], io["ctx"].rearrange("(t e) s d -> e s t d", e=2)[e, 0:S])\
                    .then_inc(l1_ld, 16)
            sp.dma_start(w_l1, io["L1_w"]).then_inc(l1_ld, 16)
            sp.dma_start(w_col1, io["L1_cols"]).then_inc(l1_ld, 16)
            sp.dma_start(w_r1, io["L1_router"]).then_inc(l1_ld, 16)

            for dst, name in ((w_kT2, "L2_wkT"), (w_vT2, "L2_wvT"), (w_o2, "L2_wo"), (w_q2, "L2_wq"),
                              (qk_col, "qk_cols")):
                sp.dma_start(dst, io[name]).then_inc(ld_m, 16)

            def load_experts1(g, p):
                sp.dma_start(wex[p][:, 0:G1 * 3 * D], batch(io["L1_ex"], g)).then_inc(ex_ld[p], 16)

            load_experts1(0, 0)
            load_experts1(1, 1)

            sp.wait_ge(l0_att, 1)
            sp.dma_start(d_att.rearrange("b h n e -> n (b h) e"), at0.rearrange("n b (h e) -> n (b h) e", h=H16))\
                .then_inc(l0_st, 16)
            sp.wait_ge(l0_st, 16)
            sp.dma_start(y2, d_att.rearrange("b h n e -> (b h n e)").rearrange("(t p d) -> p t d", p=TT, d=D))\
                .then_inc(l0_ld, 16)

            with sp.Fori(0, E1 // G1 // 2 - 1) as i:
                for p in range(2):
                    g = 2 * i + p
                    sp.wait_ge(ex_dn, G1 * (g + 1))
                    load_experts1(g + 2, p)

            sp.wait_ge(lat_ready, 1)
            sp.dma_start(d_lat.rearrange("(t p) d -> p t d", p=TT), y).then_inc(st_m, 16)
            sp.wait_ge(lat_ready, 2)
            sp.dma_start(d_latT, xT).then_inc(st_m, 16)
            sp.wait_ge(st_m, 32)

            def load_keys2(b, p):
                sp.dma_start(clnT_s[p][:, 0:C], batch(d_clnT, b)).then_inc(l2_ld[p], 16)
                sp.dma_start(clnT_s[p][:, C:CL], d_latT[:, bass.ds(b * S, S)]).then_inc(l2_ld[p], 16)
                src = batch(d_cln, b).rearrange("p (j d) -> p j d", j=KT)
                sp.dma_start(cln_s[p][0:112, 0:KT, 0:D], src[0:112]).then_inc(l2_ld[p], 16)
                sp.dma_start(cln_s[p][112:KP, 0:KT, 0:D], src[112:KP]).then_inc(l2_ld[p], 16)
                sp.dma_start(cln_s[p][0:S, KT, 0:D], d_lat[bass.ds(b * S, S), :]).then_inc(l2_ld[p], 16)

            for b in range(2):
                load_keys2(b, b)
            sp.wait_ge(ln_rstd, RSTD["latent_k"])
            sp.dma_start(d_rl.rearrange("(t p) h -> p t h", p=TT), qss[:, 1, :].rearrange("p (t h) -> p t h", t=NT))\
                .then_inc(st_m, 16)
            sp.wait_ge(st_m, 48)
            sp.dma_start(rnl, d_rl.rearrange("(b q) h -> q b h", b=B)).then_inc(ld_rn, 16)
            with sp.Fori(0, B // 2 - 1) as i:
                for p in range(2):
                    b = 2 * i + p
                    sp.wait_ge(l2_pv, (KT + 1) * (b + 1) + 2)
                    load_keys2(b + 2, p)

            def load_keys3(b, p, u):
                src = d_k3[bass.ds(b, 1)].rearrange("o g e r c -> (o e) r g c")
                at = 500 * u
                for hh in range(4):
                    sp.dma_start(kst[p][32 * hh + 8:32 * hh + 32, :, at:at + 500], src[hh, :, :, at:at + 500])\
                        .then_inc(l3_ld[p][u], 16)

            def load_values3(b, p):
                src = batch(d_v3, b).rearrange("p (j d) -> p j d", j=KT)
                sp.dma_start(v3s[p][0:112], src[0:112]).then_inc(l3_ldv[p], 16)
                sp.dma_start(v3s[p][112:KP], src[112:KP]).then_inc(l3_ldv[p], 16)

            sp.wait_ge(l3_free, 1)
            for p in range(2):
                for hh in range(4):
                    sp.dma_start(kst[p][32 * hh:32 * hh + 8],
                                 io["pad"][min(hh, 1)].unsqueeze(1).broadcast_to([8, 4, C])).then_inc(l3_pad, 16)
            for b in range(2):
                for u in range(3):
                    load_keys3(b, b, u)
                load_values3(b, b)
            with sp.Fori(0, B // 2 - 1) as i:
                for p in range(2):
                    b = 2 * i + p
                    for u in range(3):
                        sp.wait_ge(l3_s, KT * b + 4 * (u + 1))
                        load_keys3(b + 2, p, u)
                    sp.wait_ge(l3_pv, KT * (b + 1) + 2)
                    load_values3(b + 2, p)

            def load_expert3(e, p):
                sp.dma_start(wex[p], batch(io["L3_ex"], e)).then_inc(ex_ld[p], 16)

            load_expert3(0, 0)
            load_expert3(1, 1)
            with sp.Fori(0, E3 // 2 - 1) as i:
                for p in range(2):
                    e = 2 * i + p
                    sp.wait_ge(ex_dn, E1 + e + 1)
                    load_expert3(e + 2, p)
            sp.wait_ge(out_ready, 1)
            sp.dma_start(out.rearrange("(t p) d -> p t d", p=TT), x[:, :, :]).then_inc(st_out, 16)
            sp.wait_ge(st_out, 16)


        @block.tensor
        def _(pe):
            op = Count(pe, operand)
            ident = cs("ident")

            def transposes(src, k):
                for t in range(NT):
                    last = pe.transpose(ps[0:D, k, TT * t:TT * t + TT], src[:, t, :], ident[0:TT, 0:TT])
                last.then_inc(product, 1)

            def by_tokens(srcT, w, k, cols=D):
                for t in range(NT):
                    mm = pe.matmul(ps[0:TT, k, cols * t:cols * t + cols], srcT[:, TT * t:TT * t + TT], w,
                                   start=True, stop=True)
                mm.then_inc(product, 1)

            pe.wait_ge(ld_w, N_LOADS * 16)
            pe.wait_ge(wsum_in, 1)
            pe.matmul(ps[0:D, 7, 0:5], cs("mean"), mw[:, :], start=True, stop=True).then_inc(wsum, 1)
            pe.wait_ge(w_ready, 1)

            A, DV = (0, 1, 2), (3, 4, 5)
            with pe.Fori(0, B // 2) as i:
                for p in range(2):
                    b = 2 * i + p
                    use_a, use_d = [0], [0]

                    def bank_a():
                        n = use_a[0]
                        use_a[0] += 1
                        pe.wait_ge(a_free, 21 * b + n + 1)
                        return A[(21 * p + n) % 3]

                    def bank_d():
                        n = use_d[0]
                        use_d[0] += 1
                        pe.wait_ge(d_free, 9 * b + n + 1)
                        return DV[n % 3]

                    pe.wait_ge(ld_c[p], 32 * (i + 1))
                    for u in range(3):
                        k = bank_a()
                        for j in range(4):
                            mm = pe.transpose(ps[0:D, k, KP * j:KP * j + KP], c_in[p][:, 4 * u + j, :],
                                              ident[0:KP, 0:KP])
                        mm.then_inc(a_full, 1)
                    for u in range(6):
                        if u % 2 == 0:
                            pe.wait_ge(a_free, 21 * b + 3 + u // 2 + 1)
                        k = bank_a()
                        for j in range(2):
                            mm = pe.matmul(ps[0:KP, k, 256 * j:256 * j + 256], cT[p][:, 2 * u + j, :],
                                           w_l0[:, :, :].rearrange("p a n -> p (a n)"), start=True, stop=True)
                        mm.then_inc(a_full, 1)
                    for u in range(3):
                        k = bank_d()
                        pe.matmul(ps[0:D, k, 0:4 * KP], w_k3[:, :],
                                  cT[p][:, 4 * u:4 * u + 4, :].rearrange("p j n -> p (j n)"),
                                  start=True, stop=True).then_inc(d_full, 1)
                    for u in range(3):
                        k = bank_d()
                        for j in range(4):
                            mm = pe.matmul(ps[0:KP, k, D * j:D * j + D], cT[p][:, 4 * u + j, :], w_v3[:, :],
                                           start=True, stop=True)
                        mm.then_inc(d_full, 1)
                    pe.wait_ge(c_lned, b + 1)
                    for u in range(3):
                        k = bank_d()
                        for j in range(4):
                            mm = pe.transpose(ps[0:D, k, KP * j:KP * j + KP], cln[p][:, 4 * u + j, :],
                                              ident[0:KP, 0:KP])
                        mm.then_inc(d_full, 1)
                    for j in range(KT):
                        if j % 4 == 0:
                            pe.wait_ge(d_free, 9 * b + 3 + 6 + j // 4 + 1)
                        k = bank_a()
                        pe.matmul(ps[0:KP, k, :], clnT[p][:, j, :], w_k2[:, :], start=True, stop=True)\
                            .then_inc(a_full, 1)
                    pe.wait_ge(l0_kp, b + 1)
                    pe.wait_ge(l0_rhs, b + 1)
                    pe.wait_ge(acc_used, b + 1)
                    for j in range(KT):
                        mm = pe.matmul(ps[0:D, 6 + p, 0:D + 2], kpr[:, j, :], rhs0[:, j, :],
                                       start=(j == 0), stop=(j == KT - 1))
                    mm.then_inc(acc_full, 1)

            op.next()
            for b in range(B):
                mm = pe.transpose(ps[0:D, b // 4, D * (b % 4):D * (b % 4) + D], kv_all[:, b, 0:D], ident)
            mm.then_inc(product, 1)
            op.next()
            for b in range(B):
                mm = pe.matmul(ps[0:D, 2 + b // 4, D * (b % 4):D * (b % 4) + D], kvt[:, b, :], w_l0[:, 1, :],
                               start=True, stop=True)
            mm.then_inc(product, 1)
            op.next()
            transposes(z, 4)
            op.next()
            by_tokens(xT, w_q0[:, :], 5)
            op.next()
            transposes(y2, 4)
            op.next()
            for b in range(B):
                pe.matmul(ps[0:S, 6 + b // 4, D * (b % 4):D * (b % 4) + D], xT[:, S * b:S * b + S], kvm[:, b, :],
                          start=True, stop=True)
                mm = pe.matmul(ps[0:S, 5, 16 * b:16 * b + 16], xT[:, S * b:S * b + S], ksm[:, b, :],
                               start=True, stop=True)
            mm.then_inc(product, 1)
            pe.wait_ge(l0_ld, 16)
            transposes(y2, 4)
            op.next()
            by_tokens(xT2, w_d0[:, :], 0)

            def quantised_ffn(first, n_first, second):
                op.next()
                zps = ps[0:D, 0, 0:256].bitcast(BF16)
                for t in range(NT):
                    mm = pe.transpose(zps[:, TT * t:TT * t + TT], zq[:, t, :], ident_h[0:TT, 0:TT])
                mm.then_inc(product, 1)
                op.next()
                for t in range(NT):
                    for m in range(n_first):
                        mm = pe.matmul(ps[0:TT, t + 4 * m, :], zqT[:, TT * t:TT * t + TT], wquant[:, first + m, :],
                                       start=True, stop=True)
                mm.then_inc(product, 1)
                op.next()
                for c in range(4):
                    hps = ps[0:D, c // 2, 256 * (c % 2):256 * (c % 2) + 256].bitcast(BF16)
                    for t in range(NT):
                        mm = pe.transpose(hps[:, TT * t:TT * t + TT], hq[:, t, D * c:D * c + D],
                                          ident_h[0:TT, 0:TT])
                mm.then_inc(product, 1)
                op.next()
                for t in range(NT):
                    for c in range(4):
                        mm = pe.matmul(ps[0:TT, 2, D * t:D * t + D], hqT[:, c, TT * t:TT * t + TT],
                                       wquant[:, second, D * c:D * c + D], start=(c == 0), stop=(c == 3))
                mm.then_inc(product, 1)

            quantised_ffn(0, 2, 2)

            pe.wait_ge(l1_ld, L1_LOADS * 16)
            transposes(c56, 0)
            op.next()
            pe.matmul(ps[0:D, 1, 0:N], w_l1[:, 1, :], c56T, start=True, stop=True).then_inc(product, 1)
            op.next()
            pe.matmul(ps[0:D, 2, 0:N], cs("rot"), k1T, start=True, stop=True)
            for b in range(B):
                mm = pe.matmul(ps[0:S, 3 + b // 4, D * (b % 4):D * (b % 4) + D], c56T[:, S * b:S * b + S],
                               w_l1[:, 2, :], start=True, stop=True)
            mm.then_inc(product, 1)
            op.next()
            transposes(z, 0)
            op.next()
            pe.matmul(ps[0:D, 1, 0:N], w_l1[:, 0, :], xT, start=True, stop=True).then_inc(product, 1)
            op.next()
            pe.matmul(ps[0:D, 2, 0:N], cs("rot"), q1T, start=True, stop=True).then_inc(product, 1)
            with pe.Fori(0, NT) as i:
                pe.wait_ge(l1_kq, i + 1)
                for e in range(2):
                    for half in range(2):
                        mm = pe.matmul(ps[64 * e:64 * e + 64, half, 0:8 * S], qst[:, e, :],
                                       kblk[:, e, 8 * half:8 * half + 8, :].rearrange("p h s -> p (h s)"),
                                       start=True, stop=True)
                mm.then_inc(l1_s, 1)
                pe.wait_ge(l1_p, i + 1)
                pe.nop().then_inc(pe_passed, 1)
                for h in range(16):
                    mm = pe.transpose(ps[0:S, 2 + h // 4, D * (h % 4):D * (h % 4) + D], pr1[:, h, :], ident)
                mm.then_inc(l1_t, 1)
                pe.wait_ge(l1_pt, i + 1)
                pe.nop().then_inc(pe_passed, 1)
                for e in range(2):
                    for h in range(16):
                        mm = pe.matmul(ps[64 * e:64 * e + 64, 6, 8 * h:8 * h + 8], pT1[:, h, 64 * e:64 * e + 64],
                                       v1s[:, e, 8 * h:8 * h + 8], start=True, stop=True)
                mm.then_inc(l1_o, 1)
                pe.wait_ge(l1_on, i + 1)
                pe.transpose(ps[0:D, 7, 0:D], o1, ident).then_inc(l1_ot, 1)
            op.next()
            by_tokens(xT2, w_l1[:, 3, :], 0)

            pe.wait_ge(ld_m, 5 * 16)
            for h in range(H8):
                r, c = 64 * (h % 2), h // 2
                pe.matmul(ps[0:D, 6 + h % 2, D * c:D * c + D], w_vT2[r:r + 64, c, :], w_o2[r:r + 64, c, :],
                          start=True, stop=True)
            op.next()
            transposes(z, 0)
            op.next()
            by_tokens(xT, w_r1, 1, cols=16)

            def w1(k, group, col):
                return wex[group][:, D * (3 * k + col):D * (3 * k + col) + D]

            def gate_up1(s, loads):
                if s % G1 == 0:
                    pe.wait_ge(ex_ld[s // G1 % 2], 16 * loads)
                for m in range(2):
                    mm = pe.matmul(ps[0:D, 2 + 2 * (s % 2) + m, 0:N], w1(s % G1, s // G1 % 2, m), xT,
                                   start=True, stop=True)
                mm.then_inc(ex_gu, 1)

            def expert1(turn, s, more=True):
                e = 2 * G1 * turn + s
                if more:
                    pe.wait_ge(ex_h, e + 1)
                    gate_up1(s + 1, turn + 1 + (s + 1) // (2 * G1))
                pe.wait_ge(ex_w, e + 1)
                pe.wait_ge(ex_h, e + 2)
                for t in range(NT):
                    mm = pe.matmul(ps[0:TT, 6 + s % 2, D * t:D * t + D],
                                   (xT2, xT3)[s % 2][:, TT * t:TT * t + TT], w1(s % G1, s // G1 % 2, 2),
                                   start=True, stop=True)
                mm.then_inc(ex_dn, 1)

            gate_up1(0, 1)
            with pe.Fori(0, E1 // (2 * G1) - 1) as i:
                for s in range(2 * G1):
                    expert1(i, s)
            for s in range(2 * G1):
                expert1(E1 // (2 * G1) - 1, s, more=s < 2 * G1 - 1)

            op.next()
            transposes(y, 0)
            op.next()
            for w in (w_q2, w_k2):
                for t in range(NT):
                    mm = pe.matmul(ps[0:TT, t if w is w_q2 else 4 + t, :], xT[:, TT * t:TT * t + TT], w,
                                   start=True, stop=True)
                mm.then_inc(product, 1)
            op.next()
            for c in range(4):
                for t in range(NT):
                    mm = pe.transpose(ps[0:D, c, TT * t:TT * t + TT], big[:, t, D * c:D * c + D],
                                      ident[0:TT, 0:TT])
            mm.then_inc(product, 1)
            op.next()
            for h in range(H8):
                mm = pe.matmul(ps[0:D, (4 + h) % 8, 0:N], w_kT2[:, h // 2, :], qT2[:, h, :], start=True, stop=True)
                if h % 4 == 3:
                    mm.then_inc(product, 1)
            op.next()

            def sim2(b, p, t):
                rows, cols = (KP, KP * t) if t < KT else (S, C)
                pe.wait_ge(l2_sc, (KT + 1) * b + t + 1)
                if t == KT:
                    pe.nop().then_inc(pe_passed, 1)
                pe.matmul(ps[0:rows, (t + p) % 2, 0:N].rearrange("p (h q) -> p h q", h=H8),
                          clnT_s[p][:, cols:cols + rows], qtT[:, :, bass.ds(b * S, S)],
                          start=True, stop=True).then_inc(l2_s, 1)

            def pv2(b, p, t):
                rows = KP if t < KT else S
                pe.wait_ge(l2_p, (KT + 1) * b + t + 3)
                for c in range(4):
                    dst = ps[0:TT, 4 + 2 * p, 129 * c:129 * c + 129] if c < 3 else ps[0:TT, 5 + 2 * p, 0:129]
                    mm = pe.matmul(dst, pexp[(t + p) % 2][0:rows, TT * c:TT * c + TT], cln_s[p][0:rows, t, :],
                                   start=(t == 0 and c in (0, 3)), stop=(t == KT), skip_group_check=True)
                mm.then_inc(l2_pv, 1)

            def turn2(b):
                pe.wait_ge(l2_on, b)
                pe.wait_ge(l2_done, b)
                for c in range(4):
                    mm = pe.transpose(ps[0:D, 2, TT * c:TT * c + TT], onrm[:, c, :], ident[0:TT, 0:TT])
                mm.then_inc(l2_t, 1)

            def batch2(b, p, loads, first=False):
                pe.wait_ge(l2_ld[p], 80 * loads)
                sim2(b, p, 0)
                sim2(b, p, 1)
                for t in range(KT + 1):
                    if t + 2 <= KT:
                        sim2(b, p, t + 2)
                    pv2(b, p, t)
                    if t == 4 and not first:
                        turn2(b)

            batch2(0, 0, 1, first=True)
            batch2(1, 1, 1)
            with pe.Fori(1, B // 2) as i:
                for p in range(2):
                    batch2(2 * i + p, p, i + 1)
            turn2(B)
            pe.wait_ge(l2_done, B + 1)
            for t in range(NT):
                for h in range(H8):
                    mm = pe.matmul(ps[0:TT, 0, D * t:D * t + D], ctxT[:, h, TT * t:TT * t + TT], m2[:, h, :],
                                   start=(h == 0), stop=(h == H8 - 1))
            mm.then_inc(product, 1)

            quantised_ffn(3, 1, 4)

            op.next()
            transposes(z, 0)
            op.next()
            pe.matmul(ps[0:D, 1, 0:N], w_q3[:, :], xT, start=True, stop=True).then_inc(product, 1)
            op.next()
            for g in range(4):
                pe.matmul(ps[0:D, g, 0:N], sel[:, 0, g, :], q_hi, start=True, stop=False)
                mm = pe.matmul(ps[0:D, g, 0:N], sel[:, 1, g, :], q_lo, start=False, stop=True)
            mm.then_inc(product, 1)

            def max_sim(bn, pn, u, loads):
                third, pair = u // 8, u % 8
                if pair == 0:
                    pe.wait_ge(l3_ld[pn][third], 64 * loads)
                pe.wait_ge(l3_mxd, 24 * bn + u + 1)
                q = qst3[:, bass.ds(bn, 1), pair // 2, 2 * (pair % 2):2 * (pair % 2) + 2, :]
                pe.matmul(ps[0:TT, MAX_BANKS[u % 3], 0:500], q.rearrange("p o h q -> p (o h q)"),
                          kst[pn][:, pair // 2, 500 * third:500 * third + 500],
                          start=True, stop=True).then_inc(l3_mx, 1)

            def shift_row(bn):
                pe.wait_ge(l3_dg, bn + 1)
                for half in range(2):
                    mm = pe.matmul(ps[32 * half:32 * half + 1, MAX_BANKS[0], 0:4 * TT], ones_h[0:TT, 0:1],
                                   diag3[:, 4 * half:4 * half + 4, :].rearrange("p a n -> p (a n)"),
                                   start=True, stop=True)
                mm.then_inc(l3_sh, 1)

            def sim3(b, p, t):
                pe.wait_ge(l3_p, KT * b + t + 1)
                for g in range(4):
                    mm = pe.matmul(ps[0:KP, 2 * (t % 2) + g // 2, 224 * (g % 2):224 * (g % 2) + 224],
                                   kst[p][:, g, KP * t:KP * t + KP],
                                   qst3[:, bass.ds(b, 1), g, :, :].rearrange("p o h q -> p (o h q)"),
                                   start=True, stop=True)
                mm.then_inc(l3_s, 1)

            def pv3(b, p, t):
                pe.wait_ge(l3_p, KT * b + t + 3)
                for g in range(4):
                    pe.matmul(ps[32 * g:32 * g + 32, 6, 0:168], v3s[p][:, t, 32 * g:32 * g + 32],
                              p3[t % 2][:, 3 * g:3 * g + 3, :].rearrange("p h q -> p (h q)"),
                              start=(t == 0), stop=(t == KT - 1), skip_group_check=True)
                for g in range(2):
                    mm = pe.matmul(ps[32 * g:32 * g + 32, 6, 168:280], v3s[p][:, t, 128 + 32 * g:160 + 32 * g],
                                   p3[t % 2][:, 12 + 2 * g:14 + 2 * g, :].rearrange("p h q -> p (h q)"),
                                   start=False, stop=(t == KT - 1), skip_group_check=True)
                mm.then_inc(l3_pv, 1)

            UNITS = (3, 3, 2, 3, 3, 2, 3, 3, 2, 0, 0, 0)

            def batch3(b, p, loads, more=True):
                pe.wait_ge(l3_row, 2 * b + 2)
                if more:
                    pe.wait_ge(l3_q, b + 2)
                sim3(b, p, 0)
                u = 0
                for t in range(KT):
                    if t + 1 < KT:
                        sim3(b, p, t + 1)
                    for _ in range(UNITS[t] if more else 0):
                        max_sim(b + 1, 1 - p, u, loads + p)
                        u += 1
                    if t == 0:
                        pe.wait_ge(l3_ldv[p], 32 * loads)
                        pe.wait_ge(l3_o, b + 1)
                    if more and t == KT - 1:
                        shift_row(b + 1)
                    pv3(b, p, t)

            pe.wait_ge(l3_pad, 8 * 16)
            pe.wait_ge(l3_q, 1)
            for u in range(24):
                max_sim(0, 0, u, 1)
            shift_row(0)
            with pe.Fori(0, B // 2 - 1) as i:
                for p in range(2):
                    batch3(2 * i + p, p, i + 1)
            batch3(B - 2, 0, B // 2)
            batch3(B - 1, 1, B // 2, more=False)
            pe.wait_ge(l3_o, B + 1)
            for k, names in enumerate((("numA", "numB"), ("denA", "denB"))):
                parts = [(cs(names[0])[:, D * h:D * h + D], oA[:, :, h, :]) for h in range(3)]
                parts += [(cs(names[1], 64)[:, D * h:D * h + D], oB[:, :, h, :]) for h in range(2)]
                for n, (w, o) in enumerate(parts):
                    mm = pe.matmul(ps[0:D, k, 0:N].rearrange("p (b q) -> p b q", b=B), w, o,
                                   start=(n == 0), stop=(n == 4))
            mm.then_inc(product, 1)
            op.next()
            by_tokens(xT2, w_o3[:, :], 2)

            op.next()
            transposes(z, 0)
            op.next()
            by_tokens(xT, w_r3[:, :], 1, cols=E3)

            def gate_up3(e, p, c):
                for m in range(2):
                    mm = pe.matmul(ps[0:D, 2 + 2 * (c % 2) + m, 0:N], wex[p][:, FF * m + D * c:FF * m + D * c + D],
                                   xT, start=True, stop=True)
                mm.then_inc(ex_gu, 1)

            def down3(e, p):
                pe.wait_ge(ex_h, E1 + 4 * e + 5)
                pe.wait_ge(ex_w, E1 + e + 1)
                for t in range(NT):
                    for c in range(4):
                        mm = pe.matmul(ps[0:TT, 6 + p, D * t:D * t + D], h3[p][:, c, TT * t:TT * t + TT],
                                       wex[p][:, 2 * FF + D * c:2 * FF + D * c + D], start=(c == 0), stop=(c == 3))
                mm.then_inc(ex_dn, 1)

            def expert3(e, p, i, first=False):
                pe.wait_ge(ex_ld[p], 16 * (E1 // G1 // 2) + 16 * (i + 1))
                for c in range(4):
                    pe.wait_ge(ex_h, E1 + 4 * e + c)
                    gate_up3(e, p, c)
                    if c == 1 and not first:
                        down3(e - 1, 1 - p)

            expert3(0, 0, 0, first=True)
            expert3(1, 1, 0)
            with pe.Fori(1, E3 // 2) as i:
                for p in range(2):
                    expert3(2 * i + p, p, i)
            down3(E3 - 1, 1)

        @block.scalar
        def _(act):
            act.nop().then_inc(a_free, 3)
            act.nop().then_inc(l2_p, 2)
            act.nop().then_inc(l3_p, 2)
            act.wait_ge(ld_w, N_LOADS * 16)
            act.activation(tg[:, :], gates[:, :], ACT.Tanh).then_inc(from_act, 1)

            with act.Fori(0, B // 2) as i:
                for p in range(2):
                    b = 2 * i + p
                    use = [0]

                    def bank_a():
                        n = use[0]
                        use[0] += 1
                        act.wait_ge(a_full, 21 * b + n + 1)
                        return (21 * p + n) % 3

                    for u in range(3):
                        k = bank_a()
                        act.copy(cT[p][:, 4 * u:4 * u + 4, :].rearrange("p j n -> p (j n)"), ps[0:D, k, 0:4 * KP])\
                            .then_inc(a_free, 1)
                    act.wait_ge(l0_kn, b + 1)
                    for u in range(6):
                        k = bank_a()
                        src = ps[0:KP, k, :].rearrange("p (j a n) -> p j a n", j=2, a=2)
                        act.activation(sq0[:, 2 * u:2 * u + 2].rearrange("p j a n -> p (j a n)"), ps[0:KP, k, :],
                                       ACT.Square)
                        act.copy(kraw[:, 2 * u:2 * u + 2, :], src[:, :, 0, :]).then_inc(a_free, 1)
                        if u == 1:
                            act.wait_ge(c_var, b + 1)
                            act.activation(sm[:, 5, 0:KT], sm[:, 4, 0:KT], ACT.Sqrt).then_inc(c_sd, 1)
                    act.wait_ge(st[p], 96 * (i + 1))
                    for u in range(3):
                        act.wait_ge(d_full, 9 * b + u + 1)
                        act.copy(k_hi[p][:, 500 * u:500 * u + 500], ps[0:D, 3 + u, 0:500]).then_inc(k_hi_ready, 1)
                    act.wait_ge(l0_var, b + 1)
                    act.activation(sm[:, 8, :], sm[:, 7, :], ACT.Sqrt).then_inc(l0_sd, 1)
                    for j in range(KT):
                        k = bank_a()
                        act.wait_ge(sq_used, KT * b + j + 1)
                        act.activation(sqk[:, j % 2, :], ps[0:KP, k, :], ACT.Square).then_inc(a_free, 1)
            act.wait_ge(rn_sq, 1)
            rn_flat = rn[:, :, :, :].rearrange("p b t h -> p (b t h)")
            act.activation(rn_flat, rn_flat, ACT.Sqrt).then_inc(rn_sd, 1)

            act.wait_ge(product, PRODUCT["ffn0_in"])
            for t in range(NT):
                act.activation(big[:, t, :], ps[0:TT, t, :], ACT.Silu, scale=acol[:, 2, t:t + 1]).then_inc(from_act, 1)

            with act.Fori(0, NT) as i:
                act.wait_ge(l1_m, i + 1)
                act.activation(pr1, sc1, ACT.Exp).then_inc(l1_p, 1)
                act.wait_ge(l1_t, i + 1)
                act.copy(pT1.rearrange("p (k h) n -> p k (h n)", k=4), ps[0:S, 2:6, :]).then_inc(l1_pt, 1)
            act.wait_ge(to_act, 1)
            act.activation(sm16[:, 6], sm16[:, 0], ACT.Sigmoid).then_inc(from_act, 1)
            with act.Fori(0, E1 // 2) as i:
                for p in range(2):
                    act.wait_ge(ex_gu, 2 * i + p + 1)
                    act.activation(exs[p], ps[0:D, 2 + 2 * p, 0:N], ACT.Silu).then_inc(ex_act, 1)

            act.wait_ge(product, PRODUCT["latent_q"])
            for t in range(NT):
                act.activation(big2[:, t, :], ps[0:TT, t, :], ACT.Square).then_inc(from_act, 1)
            act.wait_ge(to_act, 2)
            act.activation(qss[:, 2, :], qss[:, 0, :], ACT.Sqrt).then_inc(from_act, 1)
            act.wait_ge(product, PRODUCT["latent_k"])
            for t in range(NT):
                act.activation(big3[:, t, :], ps[0:TT, 4 + t, :], ACT.Square).then_inc(from_act, 1)
            act.wait_ge(product, PRODUCT["latent_qT"])
            act.wait_ge(l2_zero, 1)
            act.copy(qT2[64:D, 1::2, :], ps[64:D, 0:4, 0:N]).then_inc(from_act, 1)
            for half in range(2):
                act.wait_ge(product, PRODUCT["queries2"] + half)
                for h in (4 * half, 4 * half + 2):
                    act.copy(qtT[:, h, :], ps[0:D, (4 + h) % 8, 0:N]).then_inc(from_act, 1)
            with act.Fori(0, B // 2) as i:
                for p in range(2):
                    b = 2 * i + p
                    for t in range(KT + 1):
                        n = (KT + 1) * b + t
                        rows = KP if t < KT else S
                        act.wait_ge(l2_sc, n + 3)
                        act.wait_ge(l2_pv, n + 1)
                        bias = kbias[:, bass.ds(b, 1), t] if t < KT else lbias[0:S, :]
                        act.activation(pexp[(t + p) % 2][0:rows], sscl[(t + p) % 2][0:rows], ACT.Exp, bias=bias)\
                            .then_inc(l2_p, 1)

            for t in range(NT):
                act.wait_ge(to_act, 3 + t)
                act.activation(big2[:, t, :], big[:, t, :], ACT.Gelu).then_inc(from_act, 1)

            with act.Fori(0, B // 2) as i:
                for p in range(2):
                    b = 2 * i + p
                    for t in range(KT):
                        n = KT * b + t
                        act.wait_ge(l3_s, n + 1)
                        act.wait_ge(l3_pv, n + 1)
                        act.activation(p3[t % 2].rearrange("p (k h) q -> p k (h q)", k=2),
                                       ps[0:KP, 2 * (t % 2):2 * (t % 2) + 2, 0:8 * S], ACT.Exp).then_inc(l3_p, 1)
            act.wait_ge(to_act, 7)
            act.activation(sm8[:, 0], sm8[:, 7], ACT.Exp).then_inc(from_act, 1)
            with act.Fori(0, E3 // 2) as i:
                for p in range(2):
                    for c in range(4):
                        act.wait_ge(ex_gu, E1 + 8 * i + 4 * p + c + 1)
                        act.activation(exs[c % 2], ps[0:D, 2 + 2 * (c % 2), 0:N], ACT.Gelu).then_inc(ex_act, 1)

        @block.gpsimd
        def _(pool):
            for p in range(2):
                pool.nop().then_inc(st[p], 96)
            pool.nop().then_inc(ex_acc, 2)
            ch = Chain(pool, pool_s)
            pool.wait_ge(ld_w, N_LOADS * 16)

            with pool.Fori(0, B // 2) as i, ch.loop(i, 2 * 4, B // 2):
                for p in range(2):
                    b = 2 * i + p
                    pool.wait_ge(c_hat, b + 1)
                    ch.link(pool.tensor_tensor(cln[p], cln[p], spread("L2_xw", KP, KT), ALU.mult))
                    pool.tensor_tensor(cln[p], cln[p], spread("L2_xb", KP, KT), ALU.add).then_inc(c_lned, 1)
                    pool.wait_ge(l0_w, b + 1)
                    pool.wait_ge(acc_used, b + 2)
                    ch.step(pool.tensor_copy(rhs0[:, :, D:D + 1], em[:, bass.ds(b, 1), :].rearrange("p o j -> p (o j)")
                                             .unsqueeze(2)))
                    ch.step(pool.tensor_copy(rhs0[:, :, D + 1:D + 2], em2[:, bass.ds(b, 1), :]
                                             .rearrange("p o j -> p (o j)").unsqueeze(2)))
                    pool.tensor_tensor(rhs0[:, :, 0:D], c_in[p], sm[:, 11, 0:KT].unsqueeze(2)
                                       .broadcast_to([KP, KT, D]), ALU.mult).then_inc(l0_rhs, 1)
                    pool.wait_ge(l0_kn, b + 2)
                    ch.link(pool.tensor_tensor(kn, kn, spread("L0_g", KP, KT), ALU.mult))
                    pool.tensor_tensor(kn, kn, spread("L0_b", KP, KT), ALU.add).then_inc(l0_kaff, 1)

            rs = [0]

            def rsqrt(n=1):
                for _ in range(n):
                    rs[0] += 1
                    pool.wait_ge(ln_var, rs[0])
                    pool.tensor_tensor(lnrs, lnve, nhalf[0:TT, 0:NT], ALU.pow).then_inc(ln_rstd, 1)

            rsqrt(3)
            rsqrt()
            rsqrt()

            def add_expert(e, p):
                pool.wait_ge(ex_w, e + 3)
                pool.tensor_tensor(y2, y2, big[:, :, D * p:D * p + D], ALU.add).then_inc(ex_acc, 1)

            rsqrt()
            ch.link(pool.memset(y2, 0.0))
            with pool.Fori(0, E1 // 2) as i:
                for p in range(2):
                    e = 2 * i + p
                    pool.wait_ge(ex_acc, e + 2)
                    add_expert(e, p)
            rsqrt(2)
            pool.memset(qT2, 0.0).then_inc(l2_zero, 1)
            rs[0] += 1
            pool.wait_ge(ln_var, rs[0])
            pool.tensor_tensor(qss[:, 1, :], qss[:, 1, :], nhalf[0:TT, :], ALU.pow).then_inc(ln_rstd, 1)
            rsqrt()
            rsqrt(2)
            rsqrt()

            pool.wait_ge(l3_free, 2)
            with pool.Fori(0, B) as b:
                pool.tensor_tensor(qst3[:, bass.ds(b, 1)].rearrange("p o g h q -> p (o g) h q"),
                                   q3[:, :, bass.ds(b * S, S)].unsqueeze(2).broadcast_to([D, 4, 4, S]),
                                   gm4.unsqueeze(1).unsqueeze(3).broadcast_to([D, 4, 4, S]), ALU.mult)\
                    .then_inc(l3_q, 1)

            rsqrt()
            ch.link(pool.memset(y2, 0.0))
            with pool.Fori(0, E3 // 2) as i:
                for p in range(2):
                    e = E1 + 2 * i + p
                    pool.wait_ge(ex_acc, e + 2)
                    add_expert(e, p)

        @block.vector
        def _(dve):
            ch = Chain(dve, dve_s)
            product_in, act_in = Count(dve, product), Count(dve, from_act)
            rstd_in = Count(dve, ln_rstd)
            ident = cs("ident")

            def tt(out, a, b, op):
                return dve.tensor_tensor(out, a, b, op)

            def over(col, shape):
                return col.unsqueeze(2).broadcast_to(shape)

            def signal(s, after=None):
                ch.sync()
                if after:
                    dve.wait_ge(operand, after)
                dve.nop().then_inc(s, 1)

            def layernorm(src, dst, eps, gain=None, bias=None):
                for t in range(NT):
                    ch.step(dve.bn_stats(lnst[:, t, :], src[:, t, :]))
                ch.sync()
                for t in range(NT):
                    ch.step(dve.bn_aggr(lnmv[:, t, :], lnst[:, t, :]))
                ch.sync()
                dve.tensor_scalar(lnve, lnmv[:, :, 1], eps, None, ALU.add).then_inc(ln_var, 1)
                rstd_in.next()
                for t in range(NT):
                    ch.step(dve.tensor_scalar(dst[:, t, :], src[:, t, :], lnmv[:, t, 0:1], lnrs[:, t:t + 1],
                                              ALU.subtract, ALU.mult))
                ch.sync()
                if gain:
                    ch.link(tt(dst, dst, spread(gain), ALU.mult))
                    ch.link(tt(dst, dst, spread(bias), ALU.add))

            def residual(k, src):
                ch.link(dve.scalar_tensor_tensor(x[:, :, :], src, tg[0:TT, k:k + 1], x[:, :, :],
                                                 ALU.mult, ALU.add))

            def turned(dst, k):
                product_in.next()
                dve.tensor_copy(dst, ps[0:D, k, 0:N]).then_inc(operand, 1)

            def quantise(src, tmp, dst, scales):
                width = src.shape[2]
                ch.link(dve.tensor_reduce(acol[:, 0, :], src, AX.X, ALU.max, apply_absolute_value=True))
                ch.link(dve.tensor_scalar(acol[:, 0, :], acol[:, 0, :], 1e-5, None, ALU.max))
                ch.link(dve.reciprocal(acol[:, 1, :], acol[:, 0, :]))
                ch.link(dve.tensor_scalar(acol[:, 1, :], acol[:, 1, :], 127.0, None, ALU.mult))
                for row, m in scales:
                    ch.step(dve.tensor_scalar(acol[:, row, :], acol[:, 0, :], 1.0 / 127.0, mw[0:TT, m:m + 1],
                                              ALU.mult, ALU.mult))
                ch.link(tt(tmp, src, over(acol[:, 1, :], [TT, NT, width]), ALU.mult))
                ch.link(dve.tensor_scalar(tmp, tmp, MAGIC, MAGIC, ALU.add, ALU.subtract))
                dve.tensor_scalar(dst, tmp, -128.0, 127.0, ALU.max, ALU.min).then_inc(operand, 1)

            dve.nop().then_inc(d_free, 3)
            dve.nop().then_inc(sq_used, 2)
            dve.nop().then_inc(acc_used, 2)
            dve.nop().then_inc(l0_kn, 1)
            dve.nop().then_inc(l2_sc, 2)
            dve.nop().then_inc(l2_done, 1)
            dve.nop().then_inc(l2_pv, 2)
            dve.nop().then_inc(l3_mxd, 3)
            dve.nop().then_inc(l3_pv, 2)
            dve.nop().then_inc(l3_o, 1)
            dve.nop().then_inc(ex_h, 1)
            dve.nop().then_inc(ex_w, 2)
            for p in range(2):
                ch.step(dve.memset(v3[p], 0.0))
            ch.sync()
            for p in range(2):
                blocks = v3[p].rearrange("p j (g c) -> p j g c", c=32)
                ch.step(dve.memset(blocks[:, :, 0:4, 24:25], 1.0))
                ch.step(dve.memset(blocks[:, :, 4:6, 16:17], 1.0))
            dve.wait_ge(ld_w, N_LOADS * 16)
            dve.tensor_reduce(mw[:, :], wraw, AX.X, ALU.add, apply_absolute_value=True).then_inc(wsum_in, 1)
            ch.link(dve.tensor_reduce(colv[:, :], w_l0[:, :, :], AX.X, ALU.add))
            ch.link(dve.tensor_scalar(colv[:, :], colv[:, :], 1.0 / D, None, ALU.mult))
            ch.step(tt(w_l0[:, :, :], w_l0[:, :, :], over(colv[:, :], [D, 2, D]), ALU.subtract))
            ch.step(dve.tensor_copy(ident_h[:, :], ident))
            ch.step(dve.tensor_copy(gm4[:, :], cs("gmask")))
            ch.step(tt(em2, em, em, ALU.mult))
            ch.link(tt(qks[:, 0, :], qks[:, 0, :], qks[:, 1, :], ALU.mult))
            ch.link(dve.tensor_scalar(qks[:, 0, :], qks[:, 0, :], 8.0, None, ALU.mult))
            ch.link(dve.tensor_reduce(lbias[:, :], qks[:, 0, :], AX.X, ALU.max, apply_absolute_value=True))
            ch.link(dve.tensor_scalar(lbias[:, :], lbias[:, :], -1.0, None, ALU.mult))
            ch.link(dve.tensor_copy(kbias[:, :, :], kmask[:, :, :]))
            ch.link(dve.tensor_scalar(kbias[:, :, :], kbias[:, :, :], -1.0, -NEG, ALU.add, ALU.mult))
            ch.link(dve.tensor_scalar(kbias[:, :, :], kbias[:, :, :], lbias[0:KP, 0:1], None, ALU.add))
            dve.wait_ge(wsum, 1)
            ch.link(dve.tensor_scalar(mw[:, :], ps[0:D, 7, 0:5], 1.0 / (D * FF), 1e-5, ALU.mult, ALU.max))
            ch.link(dve.reciprocal(wscale[:, :], mw[:, :]))
            for m in range(5):
                ch.step(dve.tensor_scalar(wraw[:, m, :], wraw[:, m, :], wscale[:, m:m + 1], MAGIC,
                                          ALU.mult, ALU.add))
            ch.sync()
            ch.link(dve.tensor_scalar(wraw, wraw, MAGIC, -1.0, ALU.subtract, ALU.max))
            dve.tensor_scalar(wquant[:, :, :], wraw, 1.0, None, ALU.min).then_inc(w_ready, 1)

            with dve.Fori(0, B // 2) as i, ch.loop(i, 2 * 32, B // 2):
                for p in range(2):
                    b = 2 * i + p
                    dve.wait_ge(ld_c[p], 32 * (i + 1))
                    for j in range(KT):
                        ch.step(dve.bn_stats(stat[:, j, :], c_in[p][:, j, :]))
                    ch.sync()
                    n = KT
                    ch.step(tt(sm[:, 0, 0:n], stat[:, :, 1], stat[:, :, 4], ALU.add))
                    ch.step(tt(sm[:, 1, 0:n], stat[:, :, 1], stat[:, :, 4], ALU.subtract))
                    ch.link(tt(sm[:, 2, 0:n], stat[:, :, 2], stat[:, :, 5], ALU.add))
                    ch.step(dve.tensor_scalar(sm[:, 2, 0:n], sm[:, 2, 0:n], 1.0 / D, 1e-5, ALU.mult, ALU.add))
                    ch.step(dve.tensor_scalar(sm[:, 3, 0:n], sm[:, 0, 0:n], 0.5, None, ALU.mult))
                    ch.link(tt(sm[:, 1, 0:n], sm[:, 1, 0:n], sm[:, 1, 0:n], ALU.mult))
                    dve.scalar_tensor_tensor(sm[:, 4, 0:n], sm[:, 1, 0:n], 0.25, sm[:, 2, 0:n],
                                             ALU.mult, ALU.add).then_inc(c_var, 1)
                    dve.wait_ge(c_sd, b + 1)
                    ch.link(dve.reciprocal(sm[:, 6, 0:n], sm[:, 5, 0:n]))
                    dve.wait_ge(st[p], 96 * (i + 1))
                    for j in range(KT):
                        ins = dve.tensor_scalar(cln[p][:, j, :], c_in[p][:, j, :], sm[:, 3, j:j + 1],
                                                sm[:, 6, j:j + 1], ALU.subtract, ALU.mult)
                        if j < KT - 1:
                            ch.step(ins)
                    ins.then_inc(c_hat, 1)
                    dve.wait_ge(a_free, 21 * b + 3 + 9)
                    ch.link(dve.tensor_reduce(sm[:, 10, :].rearrange("p (j a) -> p j a", a=2), sq0, AX.X, ALU.add))
                    dve.tensor_scalar(sm[:, 7, :], sm[:, 10, :], 1.0 / D, 1e-6, ALU.mult, ALU.add)\
                        .then_inc(l0_var, 1)
                    for u in range(3):
                        dve.wait_ge(k_hi_ready, 3 * b + u + 1)
                        tt(k_lo[p][:, 500 * u:500 * u + 500], ps[0:D, 3 + u, 0:500],
                           k_hi[p][:, 500 * u:500 * u + 500], ALU.subtract).then_inc(d_free, 1)
                    dve.wait_ge(l0_sd, b + 1)
                    ch.link(dve.reciprocal(sm[:, 9, :], sm[:, 8, :]))
                    r = sm[:, 9, :].rearrange("p (j a) -> p j a", a=2)
                    tt(sm[:, 11, 0:n], r[:, :, 1], em2[:, bass.ds(b, 1), :].rearrange("p o j -> p (o j)"), ALU.mult)\
                        .then_inc(l0_w, 1)
                    tt(kn, kraw, r[:, :, 0:1].broadcast_to([KP, KT, D]), ALU.mult).then_inc(l0_kn, 1)
                    for u in range(3):
                        dve.wait_ge(d_full, 9 * b + 3 + u + 1)
                        src = ps[0:KP, 3 + u, :].rearrange("p (j n) -> p j n", j=4)
                        dst = v3[p][:, 4 * u:4 * u + 4, :]
                        dve.tensor_copy(dst[:, :, 0:128].rearrange("p j (g c) -> p j g c", c=32)[:, :, :, 0:24],
                                        src[:, :, 0:96].rearrange("p j (g c) -> p j g c", c=24))
                        dve.tensor_copy(dst[:, :, 128:192].rearrange("p j (g c) -> p j g c", c=32)[:, :, :, 0:16],
                                        src[:, :, 96:128].rearrange("p j (g c) -> p j g c", c=16))\
                            .then_inc(d_free, 1)
                    for u in range(3):
                        dve.wait_ge(d_full, 9 * b + 6 + u + 1)
                        dve.tensor_copy(clnT[p][:, 4 * u:4 * u + 4, :].rearrange("p j n -> p (j n)"),
                                        ps[0:D, 3 + u, 0:4 * KP]).then_inc(d_free, 1)
                    for j in range(KT):
                        if j == 2:
                            dve.wait_ge(l0_kaff, b + 1)
                            dve.tensor_scalar(kpr, kn, 0.0, 1e-6, ALU.max, ALU.add).then_inc(l0_kp, 1)
                        dve.wait_ge(a_free, 21 * b + 3 + 9 + j + 1)
                        dve.tensor_reduce(rn[:, bass.ds(b, 1), j, :].rearrange("p o h -> p (o h)"),
                                          sqk[:, j % 2, :].rearrange("p (h d) -> p h d", h=H8), AX.X, ALU.add)\
                            .then_inc(sq_used, 1)
                    dve.wait_ge(acc_full, b + 1)
                    dve.tensor_copy(kv_all[:, bass.ds(b, 1), :].rearrange("p o n -> p (o n)"),
                                    ps[0:D, 6 + p, 0:D + 2]).then_inc(acc_used, 1)
            dve.wait_ge(acc_used, B + 2)
            dve.wait_ge(sq_used, KT * B + 2)
            rn_flat = rn[:, :, :, :].rearrange("p b t h -> p (b t h)")
            dve.tensor_scalar(rn_flat, rn_flat, 1e-24, None, ALU.max).then_inc(rn_sq, 1)
            dve.nop().then_inc(ctx_done, 1)
            dve.nop().then_inc(operand, 1)

            for p in range(2):
                dve.wait_ge(st[p], 96 * (B // 2 + 1))
            ch.link(dve.memset(nhalf, -0.5))
            layernorm(x, z, 1e-5)
            product_in.next()
            dve.tensor_copy(kvt.rearrange("p b n -> p (b n)"), ps[0:D, 0:2, :].rearrange("p k n -> p (k n)"))\
                .then_inc(operand, 1)
            signal(operand, after=OPERAND["kvt"])
            dve.wait_ge(rn_sd, 1)
            ch.link(dve.reciprocal(rn_flat, rn_flat))
            product_in.next()
            ch.link(tt(kvm, ps[0:D, 2:4, :].rearrange("p k (b n) -> p (k b) n", b=4), spread("L0_g", D, B), ALU.mult))
            for b in range(B):
                ch.step(dve.scalar_tensor_tensor(kvm[:, b, :], spread("L0_b", D, 1)[:, 0, :], kv_all[:, b, D + 1:D + 2],
                                                 kvm[:, b, :], ALU.mult, ALU.add))
            ch.sync()
            blk = cs("blk").unsqueeze(1).broadcast_to([D, B, D])
            ch.step(tt(kvm, kvm, blk, ALU.mult))
            ch.step(tt(ksm, cs("hmask").unsqueeze(1).broadcast_to([D, B, 16]),
                       kv_all[:, :, D:D + 1].broadcast_to([D, B, 16]), ALU.mult))
            turned(xT, 4)
            product_in.next()
            ch.link(dve.tensor_copy(y.rearrange("p t n -> p (t n)"), ps[0:TT, 5, :]))
            layernorm(y, y2, 1e-6, "L0_g", "L0_b")
            dve.tensor_scalar(y2, y2, 0.0, 1e-6, ALU.max, ALU.add).then_inc(operand, 1)
            turned(xT, 4)
            product_in.next()
            ch.link(dve.tensor_scalar(rd0, ps[0:S, 5, 0:D].rearrange("p (b h) -> p b h", b=B), 1e-6, None, ALU.add))
            ch.link(dve.reciprocal(rd0, rd0))
            tt(at0.rearrange("p b (h e) -> p (b h) e", h=16), ps[0:S, 6:8, :].rearrange("p k (h e) -> p (k h) e", e=8),
               over(rd0.rearrange("p b h -> p (b h)"), [S, D, 8]), ALU.mult).then_inc(l0_att, 1)
            turned(xT2, 4)
            product_in.next()
            ch.link(tt(y, ps[0:TT, 0, :].rearrange("p (t n) -> p t n", t=NT), spread("L0_db"), ALU.add))
            layernorm(y, y, 1e-6, "L0_g", "L0_b")
            act_in.next()
            residual(0, y)

            layernorm(x, z, 1e-5)
            quantise(z, y, zq, ((2, 0), (3, 1)))
            product_in.next()
            dve.tensor_copy(zqT, ps[0:D, 0, 0:256].bitcast(BF16)[:, 0:N]).then_inc(operand, 1)
            product_in.next()
            for t in range(NT):
                act_in.next()
                ch.step(dve.scalar_tensor_tensor(big2[:, t, :], ps[0:TT, 4 + t, :], acol[:, 3, t:t + 1],
                                                 big[:, t, :], ALU.mult, ALU.mult))
            ch.sync()

            def down(scale_row, bias=None):
                for c in range(4):
                    if c == 0:
                        product_in.next()
                    ins = dve.tensor_copy(hqT[:, c, :], ps[0:D, c // 2, 256 * (c % 2):256 * (c % 2) + 256]
                                          .bitcast(BF16)[:, 0:N])
                    if c < 3:
                        ch.step(ins)
                ins.then_inc(operand, 1)
                product_in.next()
                for t in range(NT):
                    src = ps[0:TT, 2, D * t:D * t + D]
                    if bias:
                        ch.step(dve.scalar_tensor_tensor(y[:, t, :], src, acol[:, scale_row, t:t + 1],
                                                         spread(bias)[:, t, :], ALU.mult, ALU.add))
                    else:
                        ch.step(dve.tensor_scalar(y[:, t, :], src, acol[:, scale_row, t:t + 1], None, ALU.mult))
                ch.sync()

            quantise(big2, big3, hq, ((4, 2),))
            down(4)
            residual(4, y)

            turned(c56T, 0)
            product_in.next()
            dve.tensor_scalar(k1T, ps[0:D, 1, 0:N], w_col1[:, 1:2], None, ALU.add).then_inc(operand, 1)
            layernorm(x, z, 1e-5)
            signal(operand, after=OPERAND["k"])
            product_in.next()
            ch.step(tt(xT3, ps[0:D, 2, 0:N], cs("sink"), ALU.mult))
            ch.step(tt(k1T, k1T, cs("cosk"), ALU.mult))
            ch.step(tt(v1, ps[0:S, 3:5, :].rearrange("p k (b n) -> p (k b) n", b=4), spread("L1_vb", S, B), ALU.add))
            ch.sync()
            ch.step(tt(k1T, k1T, xT3, ALU.add))
            ch.step(dve.memset(qst, 0.0))
            turned(xT, 0)
            product_in.next()
            dve.tensor_scalar(q1T, ps[0:D, 1, 0:N], w_col1[:, 0:1], None, ALU.add).then_inc(operand, 1)
            ch.sync()
            product_in.next()
            ch.step(tt(xT3, ps[0:D, 2, 0:N], cs("sinq"), ALU.mult))
            ch.link(tt(q1T, q1T, cs("cosq"), ALU.mult))
            ch.link(tt(q1T, q1T, xT3, ALU.add))
            with dve.Fori(0, NT) as i, ch.loop(i, 9, NT):
                for e in range(2):
                    ch.step(tt(kblk[:, e], k1T[:, bass.ds((2 * i + e) * S, S)].unsqueeze(1).broadcast_to([D, 16, S]),
                               over(cs("hmask"), [D, 16, S]), ALU.mult))
                ch.step(dve.tensor_copy(qst[:, :, 0:S],
                                        q1T[:, bass.ds(2 * i * S, 2 * S)].rearrange("p (e s) -> p e s", e=2)))
                ch.sync()
                dve.tensor_copy(v1s, v1[:, bass.ds(2 * i, 2), :]).then_inc(l1_kq, 1)
                dve.wait_ge(l1_s, i + 1)
                ch.link(tt(sc1.rearrange("p (k h) s -> p k h s", k=2),
                           ps[:, 0:2, 0:8 * S].rearrange("p k (h s) -> p k h s", h=8),
                           cs("causal").unsqueeze(1).unsqueeze(1).broadcast_to([D, 2, 8, S]), ALU.add))
                ch.link(dve.tensor_reduce(m1[:, 0, :], sc1, AX.X, ALU.max))
                tt(sc1, sc1, over(m1[:, 0, :], [D, 16, S]), ALU.subtract).then_inc(l1_m, 1)
                dve.wait_ge(l1_p, i + 1)
                ch.link(dve.tensor_reduce(m1[:, 1, :], pr1, AX.X, ALU.add))
                ch.link(dve.reciprocal(m1[:, 2, :], m1[:, 1, :]))
                dve.wait_ge(l1_o, i + 1)
                tt(o1.rearrange("p (h d) -> p h d", h=16), ps[:, 6, 0:D].rearrange("p (h d) -> p h d", h=16),
                   over(m1[:, 2, :], [D, 16, 8]), ALU.mult).then_inc(l1_on, 1)
                dve.wait_ge(l1_ot, i + 1)
                ch.link(dve.tensor_copy(xT2[:, bass.ds(2 * i * S, 2 * S)].rearrange("p (e s) -> p e s", e=2),
                                        ps[0:D, 7, 0:D].rearrange("p (e s) -> p e s", e=2)[:, :, 0:S]))
                ch.link(dve.tensor_copy(m1[:, 1, :], m1[:, 2, :]))
            signal(operand)
            product_in.next()
            ch.link(tt(y, ps[0:TT, 0, :].rearrange("p (t n) -> p t n", t=NT), spread("L1_ob"), ALU.add))
            residual(1, y)

            def top2(v, n, low):
                rank = cs("rank", TT)[:, 0:n].unsqueeze(1).broadcast_to([TT, NT, n])
                for k in range(2):
                    src = v[:, k]
                    ch.link(dve.tensor_reduce(acol[:, 0, :], src, AX.X, ALU.max))
                    ch.link(tt(v[:, 2], src, over(acol[:, 0, :], [TT, NT, n]), ALU.is_equal))
                    ch.link(tt(v[:, 2], v[:, 2], rank, ALU.mult))
                    ch.link(dve.tensor_reduce(acol[:, 1, :], v[:, 2], AX.X, ALU.max))
                    ch.link(tt(v[:, 3 + k], v[:, 2], over(acol[:, 1, :], [TT, NT, n]), ALU.is_equal))
                    if k == 0:
                        ch.link(dve.scalar_tensor_tensor(v[:, 1], v[:, 3], low, src, ALU.mult, ALU.add))
                ch.link(tt(v[:, 5], v[:, 3], v[:, 4], ALU.add))

            layernorm(x, z, 1e-5)
            signal(operand)
            turned(xT, 0)
            product_in.next()
            dve.tensor_copy(sm16[:, 0], ps[0:TT, 1, 0:64].rearrange("p (t n) -> p t n", t=NT)).then_inc(to_act, 1)
            dve.wait_ge(to_act, 1)
            top2(sm16, 16, NEG)
            ch.step(dve.tensor_copy(m2.rearrange("p (c r) n -> p r c n", r=2),
                                    ps[0:D, 6:8, :].rearrange("p r (c n) -> p r c n", c=4)))
            dve.wait_ge(ld_m, 5 * 16)
            ch.link(tt(qk_col[:, 0:1], qk_col[:, 0:1], qk_col[:, 1:2], ALU.mult))
            ch.step(dve.tensor_scalar(w_kT2, w_kT2, qk_col[:, 0:1], 8.0, ALU.mult, ALU.mult))
            act_in.next()
            ch.step(tt(wts[:, :, 0:16], sm16[:, 5], sm16[:, 6], ALU.mult))
            ch.link(dve.memset(wts[:, :, 16:E1], 1.0))

            def hidden1(e, p):
                dve.wait_ge(ex_act, e + 1)
                tt((xT2, xT3)[p], ps[0:D, 3 + 2 * p, 0:N], exs[p], ALU.mult).then_inc(ex_h, 1)

            def weigh(e, p, weight, first):
                dve.wait_ge(ex_dn, first + e + 1)
                dve.wait_ge(ex_acc, first + e + 1)
                tt(big[:, :, D * p:D * p + D], ps[0:TT, 6 + p, :].rearrange("p (t n) -> p t n", t=NT),
                   weight.broadcast_to([TT, NT, D]), ALU.mult).then_inc(ex_w, 1)

            hidden1(0, 0)
            with dve.Fori(0, E1 // 2 - 1) as i:
                for p in range(2):
                    e = 2 * i + p
                    hidden1(e + 1, 1 - p)
                    weigh(e, p, wts[:, :, bass.ds(e, 1)], 0)
            hidden1(E1 - 1, 1)
            weigh(E1 - 2, 0, wts[:, :, E1 - 2:E1 - 1], 0)
            weigh(E1 - 1, 1, wts[:, :, E1 - 1:E1], 0)
            dve.wait_ge(ex_acc, E1 + 2)
            residual(5, y2)

            layernorm(x, z, 1e-5)
            layernorm(z, y, 1e-5, "L2_lw", "L2_lb")
            dve.nop().then_inc(lat_ready, 1)
            dve.nop().then_inc(operand, 1)
            for p in range(2):
                ch.step(dve.memset(cln_s[p][:, :, D:D + 1], 1.0))
            product_in.next()
            dve.tensor_copy(xT, ps[0:D, 0, 0:N]).then_inc(operand, 1)
            ch.sync()
            dve.wait_ge(operand, OPERAND["latentsT"])
            dve.nop().then_inc(lat_ready, 1)
            product_in.next()
            act_in.next(4)
            ch.link(dve.tensor_reduce(qss[:, 0, :], big2.rearrange("p t (h d) -> p (t h) d", h=H8), AX.X, ALU.add))
            dve.tensor_scalar(qss[:, 0, :], qss[:, 0, :], 1e-24, None, ALU.max).then_inc(to_act, 1)
            act_in.next()
            ch.link(dve.reciprocal(qss[:, 2, :], qss[:, 2, :]))
            bigf = big.rearrange("p t (h d) -> p (t h) d", h=H8)
            tt(bigf, ps[0:TT, 0:4, :].rearrange("p t (h d) -> p (t h) d", h=H8),
               over(qss[:, 2, :], [TT, NT * H8, HD8]), ALU.mult).then_inc(operand, 1)
            product_in.next(2)
            dve.wait_ge(l2_zero, 1)
            ch.step(dve.tensor_copy(qT2[0:64, 0::2, :], ps[0:64, 0:4, 0:N]))
            act_in.next(5)
            signal(operand)
            for half in range(2):
                product_in.next()
                for h in (4 * half + 1, 4 * half + 3):
                    ch.step(dve.tensor_copy(qtT[:, h, :], ps[0:D, (4 + h) % 8, 0:N]))
            act_in.next(4)
            signal(operand)
            ch.link(dve.tensor_reduce(qss[:, 1, :], big3.rearrange("p t (h d) -> p (t h) d", h=H8), AX.X, ALU.add))
            dve.tensor_scalar(qss[:, 1, :], qss[:, 1, :], 1e-24, None, ALU.max).then_inc(ln_var, 1)

            def scale2(b, p, t):
                n = (KT + 1) * b + t
                rows = KP if t < KT else S
                norm = (rn[:, bass.ds(b, 1), t, :] if t < KT else rnl[:, bass.ds(b, 1), :])\
                    .rearrange("p o h -> p (o h)")
                dve.wait_ge(l2_s, n + 1)
                dve.wait_ge(l2_p, n + 1)
                tt(sscl[(t + p) % 2][0:rows].rearrange("p (h q) -> p h q", h=H8),
                   ps[0:rows, (t + p) % 2, 0:N].rearrange("p (h q) -> p h q", h=H8),
                   over(norm, [rows, H8, S]), ALU.mult).then_inc(l2_sc, 1)

            def normalise2(b, p):
                dve.wait_ge(l2_pv, (KT + 1) * (b + 1) + 2)
                o012 = ps[0:TT, 4 + 2 * p, 0:387].rearrange("p (c n) -> p c n", c=3)
                o3 = ps[0:TT, 5 + 2 * p, 0:D + 1]
                ch.step(dve.reciprocal(rden[:, 0:3], o012[:, :, D]))
                ch.link(dve.reciprocal(rden[:, 3:4], o3[:, D:D + 1]))
                ch.step(tt(onrm[:, 0:3, :], o012[:, :, 0:D], over(rden[:, 0:3], [TT, 3, D]), ALU.mult))
                ch.sync()
                dve.tensor_scalar(onrm[:, 3, :], o3[:, 0:D], rden[:, 3:4], None, ALU.mult).then_inc(l2_on, 1)

            def features2(b):
                dve.wait_ge(l2_t, b + 1)
                dve.tensor_copy(ctxT[:, :, bass.ds(b * S, S)],
                                ps[0:D, 2, 0:N].rearrange("p (h q) -> p h q", h=H8)).then_inc(l2_done, 1)

            def batch2(b, p, first=False):
                for t in range(KT + 1):
                    if t == KT and first:
                        dve.wait_ge(ld_rn, 16)
                    scale2(b, p, t)
                    if not first and t == 3:
                        normalise2(b - 1, 1 - p)
                    if not first and t == 6:
                        features2(b - 1)

            batch2(0, 0, first=True)
            rstd_in.next()
            batch2(1, 1)
            with dve.Fori(0, B // 2 - 1) as i, ch.loop(i, 2 * 3, B // 2 - 1):
                for p in range(2):
                    batch2(2 * i + 2 + p, p)
            normalise2(B - 1, 1)
            features2(B - 1)
            product_in.next()
            ch.link(dve.tensor_copy(y.rearrange("p t n -> p (t n)"), ps[0:TT, 0, :]))
            ch.step(dve.memset(ones_h, 1.0))
            signal(l3_free)
            layernorm(y, y, 1e-5, "L2_ow", "L2_ob")
            residual(2, y)

            layernorm(x, z, 1e-5)
            layernorm(z, z, 1e-5, "L2f_g", "L2f_be")
            quantise(z, y, zq, ((2, 3),))
            product_in.next()
            dve.tensor_copy(zqT, ps[0:D, 0, 0:256].bitcast(BF16)[:, 0:N]).then_inc(operand, 1)
            product_in.next()
            for t in range(NT):
                dve.scalar_tensor_tensor(big[:, t, :], ps[0:TT, t, :], acol[:, 2, t:t + 1], b1v[0:TT, :],
                                         ALU.mult, ALU.add).then_inc(to_act, 1)
            act_in.next(4)
            quantise(big2, big3, hq, ((4, 4),))
            down(4, "L2f_b2")
            residual(6, y)

            layernorm(x, z, 1e-5)
            signal(operand)
            turned(xT, 0)
            product_in.next()
            ch.link(dve.tensor_scalar(xT2, ps[0:D, 1, 0:N], float(D) ** -0.5, None, ALU.mult))
            ch.link(dve.tensor_copy(q_hi, xT2))
            tt(q_lo, xT2, q_hi, ALU.subtract).then_inc(operand, 1)
            product_in.next()
            ch.step(dve.tensor_copy(q3, ps[0:D, 0:4, 0:N]))
            signal(l3_free)

            def maxima(bn):
                for u in range(24):
                    dve.wait_ge(l3_mx, 24 * bn + u + 1)
                    dve.tensor_reduce(mx3[:, u % 8, u // 8:u // 8 + 1], ps[0:TT, MAX_BANKS[u % 3], 0:500], AX.X, ALU.max)\
                        .then_inc(l3_mxd, 1)
                dve.wait_ge(l3_mxd, 24 * bn + 27)
                ch.link(dve.tensor_reduce(m3, mx3, AX.X, ALU.max, negate=True))
                tt(diag3, ident[0:TT, 0:TT].unsqueeze(1).broadcast_to([TT, 8, TT]), over(m3, [TT, 8, TT]), ALU.mult)\
                    .then_inc(l3_dg, 1)
                dve.wait_ge(l3_sh, bn + 1)
                for half in range(2):
                    dve.tensor_copy(qst3[0:1, bass.ds(bn, 1), 2 * half:2 * half + 2]
                                    .rearrange("p o g h q -> p (o g h q)"),
                                    ps[32 * half:32 * half + 1, MAX_BANKS[0], 0:4 * TT]).then_inc(l3_row, 1)

            def outputs(b):
                dve.wait_ge(l3_pv, KT * (b + 1) + 2)
                at_b = bass.ds(b, 1)
                ch.link(dve.tensor_copy(oA[:, at_b].rearrange("p o h q -> p (o h q)"), ps[0:D, 6, 0:168]))
                dve.tensor_copy(oB[:, at_b].rearrange("p o h q -> p (o h q)"), ps[0:64, 6, 168:280])\
                    .then_inc(l3_o, 1)

            maxima(0)
            with dve.Fori(0, B // 2 - 1) as i, ch.loop(i, 2 * 2, B // 2 - 1):
                for p in range(2):
                    maxima(2 * i + p + 1)
                    outputs(2 * i + p)
            maxima(B - 1)
            outputs(B - 2)
            outputs(B - 1)
            product_in.next()
            ch.link(dve.reciprocal(xT3, ps[0:D, 1, 0:N]))
            tt(xT2, ps[0:D, 0, 0:N], xT3, ALU.mult).then_inc(operand, 1)
            product_in.next()
            ch.link(tt(y, ps[0:TT, 2, :].rearrange("p (t n) -> p t n", t=NT), spread("L3_bo"), ALU.add))
            residual(3, y)

            layernorm(x, z, 1e-5)
            signal(operand)
            turned(xT, 0)
            product_in.next()
            logits = ps[0:TT, 1, 0:4 * E3].rearrange("p (t n) -> p t n", t=NT)
            ch.link(dve.tensor_reduce(acol[:, 5, :], logits, AX.X, ALU.max))
            tt(sm8[:, 7], logits, over(acol[:, 5, :], [TT, NT, E3]), ALU.subtract).then_inc(to_act, 1)
            act_in.next()
            top2(sm8, E3, -4.0)
            ch.link(tt(sm8[:, 5], sm8[:, 5], sm8[:, 0], ALU.mult))
            ch.link(dve.tensor_reduce(acol[:, 0, :], sm8[:, 5], AX.X, ALU.add))
            ch.link(dve.reciprocal(acol[:, 1, :], acol[:, 0, :]))
            ch.link(tt(wt3, sm8[:, 5], over(acol[:, 1, :], [TT, NT, E3]), ALU.mult))

            def expert3(e, p, first=False):
                for c in range(4):
                    dve.wait_ge(ex_act, E1 + 4 * e + c + 1)
                    tt(h3[p][:, c, :], ps[0:D, 3 + 2 * (c % 2), 0:N], exs[c % 2], ALU.mult).then_inc(ex_h, 1)
                    if c == 1 and not first:
                        weigh(e - 1, 1 - p, wt3[:, :, bass.ds(e - 1, 1)], E1)

            expert3(0, 0, first=True)
            expert3(1, 1)
            with dve.Fori(1, E3 // 2) as i:
                for p in range(2):
                    expert3(2 * i + p, p)
            weigh(E3 - 1, 1, wt3[:, :, E3 - 1:E3], E1)
            dve.wait_ge(ex_acc, E1 + E3 + 2)
            residual(7, y2)
            dve.nop().then_inc(out_ready, 1)


def kernel(**inputs):
    import concourse.bacc as bacc
    from concourse.bass_utils import run_bass_kernel_spmd

    a = {name: np.asarray(v) for name, v in inputs.items()}

    def chunks(w):
        return w.reshape(4, D, -1).transpose(1, 0, 2)

    cst, sel, pad = constants()
    wkv = a["L2_xattn_Wkv"]
    experts1 = np.concatenate([a["L1_ffn_gate_up_w"], a["L1_ffn_down_w"]], axis=2)
    shared1 = [np.concatenate([a["L1_ffn_shared_gate_w"][D * k:D * k + D].T,
                               a["L1_ffn_shared_up_w"][D * k:D * k + D].T,
                               a["L1_ffn_shared_down_w"][:, D * k:D * k + D].T], axis=1) for k in range(2)]
    io = {
        "ctx": a["ctx_1024"],
        "cst": cst,
        "sel": sel,
        "pad": pad,
        "vec": np.stack([a[n] for n in (
            "L0_xattn_ln_gamma", "L0_xattn_ln_beta", "L0_xattn_dense_b", "L1_xattn_v_b", "L1_xattn_o_b",
            "L2_xattn_ln_x_w", "L2_xattn_ln_x_b", "L2_xattn_ln_l_w", "L2_xattn_ln_l_b", "L2_xattn_ln_o_w",
            "L2_xattn_ln_o_b", "L2_ffn_b2", "L2_ffn_gamma", "L2_ffn_beta", "L3_xattn_bo")]),
        "wquant": np.stack([a["L0_ffn_w_gate"].T, a["L0_ffn_w_up"].T, chunks(a["L0_ffn_w_down"].T).reshape(D, FF),
                            a["L2_ffn_w1"].T, chunks(a["L2_ffn_w2"].T).reshape(D, FF)], axis=1),
        "L0_wk": a["L0_xattn_wk"],
        "L0_wv": a["L0_xattn_wv"],
        "L0_wq": a["L0_xattn_wq"],
        "L0_wd": a["L0_xattn_dense_w"],
        "L2_wk": wkv[:, :I2],
        "L3_wkT": a["L3_xattn_Wk"].T,
        "L3_wvT": a["L3_xattn_Wv"].T,
        "L3_wqT": a["L3_xattn_Wq"].T,
        "L3_woT": a["L3_xattn_Wo"].T,
        "L3_router": a["L3_ffn_gate_w"].T,
        "mask": a["mask_BxS2_ff1"],
        "kmask": a["mask_BxS2_bk0"],
        "qks": np.stack([a["L2_xattn_q_scale"], a["L2_xattn_k_scale"]]),
        "qk_cols": np.stack([np.tile(a["L2_xattn_q_scale"], 2), np.tile(a["L2_xattn_k_scale"], 2)], axis=1),
        "b1": a["L2_ffn_b1"],
        "gates": np.concatenate([a["g_xattn"], a["g_ffn"]]),
        "x": a["x"].reshape(N, D),
        "L1_w": np.stack([a[f"L1_xattn_{n}_w"].T for n in "qkvo"], axis=1),
        "L1_cols": np.stack([a["L1_xattn_q_b"], a["L1_xattn_k_b"]], axis=1),
        "L1_router": a["L1_ffn_router_w"].T,
        "L1_ex": np.concatenate([experts1, np.stack(shared1)]).reshape(-1, G1, D, 3 * D).transpose(0, 2, 1, 3)
        .reshape(-1, D, G1 * 3 * D),
        "L2_wkT": chunks(wkv[:, :I2].T),
        "L2_wvT": chunks(wkv[:, I2:].T),
        "L2_wo": chunks(a["L2_xattn_Wo"]),
        "L2_wq": a["L2_xattn_Wq"],
        "L3_ex": np.concatenate([
            a["L3_ffn_gate_up_w"].transpose(0, 2, 1),
            a["L3_ffn_down_w"].transpose(0, 2, 1).reshape(E3, 4, D, D).transpose(0, 2, 1, 3).reshape(E3, D, FF)],
            axis=2),
    }
    io = {name: np.ascontiguousarray(v) for name, v in io.items()}
    nc = bacc.Bacc("TRN2", target_bir_lowering=False, num_devices=1)
    aps = {name: nc.dram_tensor(f"in_{name}", v.shape, mybir.dt.from_np(v.dtype), kind="ExternalInput").ap()
           for name, v in io.items()}
    out = nc.dram_tensor("out_x", (N, D), F32, kind="ExternalOutput").ap()
    build(nc, aps, out)
    r = run_bass_kernel_spmd(nc, [{f"in_{name}": v for name, v in io.items()}], core_ids=[0])
    return r.results[0]["out_x"].reshape(B, S, D)
```

```python
from contextlib import ExitStack, contextmanager

import numpy as np

import concourse.bass as bass
from concourse import mybir

F32 = mybir.dt.float32
F16 = mybir.dt.float16
BF16 = mybir.dt.bfloat16
U8 = mybir.dt.uint8
ALU = mybir.AluOpType
ACT = mybir.ActivationFunctionType
AX = mybir.AxisListType

D = 128
B = 8
S = 56
N = B * S
NT = 4
TT = N // NT
C = 1500
KT = 12
KP = C // KT
CL = C + S
H16, HD16 = 16, 8
H8, HD8 = 8, 64
I2 = H8 * HD8
FF = 512
E1 = 18
E3 = 8
MAGIC = 12582912.0
NEG = -1e30

CST = {}
_at = 0
for _name, _n in (("ident", D), ("blk", D), ("causal", S), ("cosq", N), ("sinq", N), ("cosk", N), ("sink", N),
                  ("rot", D), ("mean", D), ("hmask", 16), ("numA", 3 * D), ("denA", 3 * D),
                  ("numB", 2 * D), ("denB", 2 * D), ("rank", 16), ("gmask", 4)):
    CST[_name] = (_at, _at + _n)
    _at += _n
CST_N = _at


def constants():
    c = np.zeros((D, CST_N), np.float32)

    def put(name, a):
        a = np.asarray(a, np.float32)
        c[:a.shape[0], CST[name][0]:CST[name][1]] = a.reshape(a.shape[0], -1)

    f = np.arange(D)
    put("ident", np.eye(D))
    put("blk", f[:, None] // HD16 == f[None, :] // HD16)
    causal = np.where(np.arange(S)[None, :] > np.arange(64)[:, None], NEG, 0.0)
    put("causal", np.concatenate([causal, causal]))
    half = HD16 // 2
    freqs = np.float32(1.0) / np.float32(10000.0) ** (np.arange(half, dtype=np.float32) / np.float32(half))
    ang = np.tile(np.arange(S, dtype=np.float32), B)[None, :] * freqs[f % half][:, None]
    cos, sin = np.cos(ang), np.sin(ang)
    put("cosk", cos)
    put("sink", sin)
    put("cosq", cos * np.float32(HD16 ** -0.5))
    put("sinq", sin * np.float32(HD16 ** -0.5))
    rot = np.zeros((D, D))
    for i in f:
        if i % HD16 < half:
            rot[i + half, i] = -1.0
        else:
            rot[i - half, i] = 1.0
    put("rot", rot)
    put("mean", np.ones((D, D)))
    put("hmask", f[:, None] // HD16 == np.arange(16)[None, :])
    num_a, den_a = np.zeros((D, 3, D)), np.zeros((D, 3, D))
    num_b, den_b = np.zeros((D, 2, D)), np.zeros((D, 2, D))
    for g in range(4):
        for h in range(3):
            for d in range(HD16):
                num_a[32 * g + 8 * h + d, h, (3 * g + h) * 8 + d] = 1.0
                den_a[32 * g + 24, h, (3 * g + h) * 8 + d] = 1.0
    for g in range(2):
        for h in range(2):
            for d in range(HD16):
                num_b[32 * g + 8 * h + d, h, (12 + 2 * g + h) * 8 + d] = 1.0
                den_b[32 * g + 16, h, (12 + 2 * g + h) * 8 + d] = 1.0
    put("numA", num_a)
    put("denA", den_a)
    put("numB", num_b)
    put("denB", den_b)
    put("rank", np.tile(16.0 - np.arange(16), (D, 1)))
    put("gmask", f[:, None] // 32 == np.arange(4)[None, :])
    sel = np.zeros((D, 2, 4, D), np.float16)
    for g in range(4):
        for hh in range(4):
            for d in range(HD16):
                src = (4 * g + hh) * 8 + d
                sel[src, 0, g, 32 * hh + 8 + d] = 1.0
                sel[src, 0, g, 32 * hh + 16 + d] = 1.0
                sel[src, 1, g, 32 * hh + 24 + d] = 1.0
    pad = np.zeros((2, 8, C), np.float16)
    pad[0] = 1.0
    return c, sel, pad


A_LOADS = 8
N_LOADS = 14
L1_LOADS = 5
SQ = 6
G1 = 3
PRODUCT = {"ffn0_in": 10, "latent_q": 19, "latent_k": 23, "latent_qT": 24, "queries2": 25}
RSTD = {"latent_k": 9}
MAX_BANKS = (4, 5, 7)
OPERAND = {"kvt": 2, "latentsT": 17, "x3T": 28}


V128 = ["L0_g", "L0_b", "L2_xw", "L2_xb", "L0_db", "L1_vb", "L1_ob", "L2_lw", "L2_lb", "L2_ow", "L2_ob",
        "L2f_b2", "L2f_g", "L2f_be", "L3_bo"]


class Chain:

    def __init__(self, eng, sem):
        self.eng, self.sem, self.n, self.turns = eng, sem, 0, None

    def step(self, ins):
        ins.then_inc(self.sem, 1)
        self.n += 1

    def sync(self):
        self.eng.wait_ge(self.sem, self.n if self.turns is None else self.turns + self.n)

    def link(self, ins):
        self.step(ins)
        self.sync()

    @contextmanager
    def loop(self, i, per_turn, turns):
        before = self.n
        self.turns = i * per_turn
        yield
        assert self.n - before == per_turn, self.n - before
        self.turns = None
        self.n = before + per_turn * turns


class Count:

    def __init__(self, eng, sem):
        self.eng, self.sem, self.n = eng, sem, 0

    def next(self, k=1):
        self.n += k
        self.eng.wait_ge(self.sem, self.n)


def a_uses(b):
    return 0 if isinstance(b, int) and b == 0 else 21 * b - 12


def build(nc, io, out):
    ctx = ExitStack()
    with ctx:
        def sb(name, shape, dt=F32):
            return ctx.enter_context(nc.sbuf_tensor(name, shape, dt))[tuple(slice(0, n) for n in shape)]

        def sem(name):
            return ctx.enter_context(nc.semaphore(name))

        d_cln = nc.dram_tensor("d_cln", (B, KP, KT * D), F32).ap()
        d_clnT = nc.dram_tensor("d_clnT", (B, D, 2, C), F16).ap()
        d_k3 = nc.dram_tensor("d_k3", (B, 4, 4, 24, C), F16).ap()
        d_v3 = nc.dram_tensor("d_v3", (B, KP, KT * 192), F32).ap()
        d_att = nc.dram_tensor("d_att", (B, H16, S, HD16), F32).ap()
        d_lat = nc.dram_tensor("d_lat", (N, D), F32).ap()
        d_latT = nc.dram_tensor("d_latT", (D, 2, N), F16).ap()
        d_rl = nc.dram_tensor("d_rl", (N, H8), F32).ap()

        ps = ctx.enter_context(nc.psum_tensor("ps", [128, 8, 512], F32))

        cst = sb("cst", [D, CST_N])
        sel = sb("sel", [D, 2, 4, D], F16)
        vec = sb("vec", [D, len(V128), D])
        qks = sb("qks", [D, 2, HD8])
        b1v = sb("b1v", [D, FF])
        gates = sb("gates", [D, 8])
        tg = sb("tg", [D, 8])
        colv = sb("colv", [D, 2])
        ident_h = sb("ident_h", [D, D], BF16)
        em = sb("em", [KP, B, KT])
        em2 = sb("em2", [KP, B, KT])
        kmask = sb("kmask", [KP, B, KT], U8)
        kbias = sb("kbias", [KP, B, KT])
        lbias = sb("lbias", [D, 1])
        w_l0 = sb("w_l0", [D, 2, D])
        w_q0 = sb("w_q0", [D, D])
        w_d0 = sb("w_d0", [D, D])
        w_k2 = sb("w_k2", [D, I2])
        w_k2h = sb("w_k2h", [D, 2, I2], F16)
        w_k3 = sb("w_k3", [D, D])
        w_v3 = sb("w_v3", [D, D])
        w_q3 = sb("w_q3", [D, D])
        w_o3 = sb("w_o3", [D, D])
        w_r3 = sb("w_r3", [D, E3])
        wquant = sb("wquant", [D, 5, FF], BF16)
        mw = sb("mw", [D, 5])
        wscale = sb("wscale", [D, 5])
        gm4 = sb("gm4", [D, 4], F16)
        x = sb("x", [TT, NT, D])
        kv_all = sb("kv_all", [D, B, D + 2])
        rn = sb("rn", [KP, B, KT, H8])
        wex = [sb(f"wex{i}", [D, 3 * FF]) for i in range(2)]

        def cs(name, rows=D):
            a, b = CST[name]
            return cst[0:rows, a:b]

        ident = cs("ident")

        def spread(name, rows=TT, n=NT):
            return vec[0:rows, V128.index(name), :].unsqueeze(1).broadcast_to([rows, n, D])

        ARENA = 35100
        arena = sb("arena", [D, ARENA])
        at = [0]

        def carve(shape, dt=F32):
            n = int(np.prod(shape[1:]))
            words = n if dt == F32 else (n + 1) // 2
            a = arena[0:shape[0], at[0]:at[0] + words]
            at[0] += words
            assert at[0] <= ARENA, at[0]
            if dt != F32:
                a = a.bitcast(dt)
            if len(shape) == 2:
                return a
            names = "abcd"[:len(shape) - 1]
            return a.rearrange("p (" + " ".join(names) + ") -> p " + " ".join(names),
                               **dict(zip(names[1:], shape[2:])))

        c_in = [carve([KP, KT, D]) for _ in range(2)]
        cln = [carve([KP, KT, D]) for _ in range(2)]
        cT = [carve([D, KT, KP]) for _ in range(2)]
        clnT = [carve([D, 2, C], F16) for _ in range(2)]
        kraw = carve([KP, KT, D])
        sq0 = carve([KP, KT, 2, D])
        kn = carve([KP, KT, D])
        kpr = carve([KP, KT, D])
        rhs0 = carve([KP, KT, D + 2])
        k_hi = [carve([D, C], F16) for _ in range(2)]
        k_lo = [carve([D, C], F16) for _ in range(2)]
        v3 = [carve([KP, KT, 192]) for _ in range(2)]
        sqk = carve([KP, SQ, I2])
        stat = carve([KP, KT, 6])
        sm = carve([KP, 16, 24])
        wraw = carve([D, 5, FF])

        at[0] = 0
        z = carve([TT, NT, D])
        y = carve([TT, NT, D])
        y2 = carve([TT, NT, D])
        xT = carve([D, N])
        xT2 = carve([D, N])
        xT3 = carve([D, N])
        big = carve([TT, NT, FF])
        big2 = carve([TT, NT, FF])
        big3 = carve([TT, NT, FF])
        zq = carve([TT, NT, D], BF16)
        zqT = carve([D, N], BF16)
        hq = carve([TT, NT, FF], BF16)
        hqT = carve([D, 4, N], BF16)
        lnst = carve([TT, NT, 6])
        lnmv = carve([TT, NT, 2])
        lnve = carve([TT, NT])
        lnrs = carve([TT, NT])
        nhalf = carve([D, 32])
        acol = carve([TT, 6, NT])
        qss = carve([TT, 3, NT * H8])
        exs = [carve([D, N]) for _ in range(2)]
        core_end = at[0]
        kvm = carve([D, B, D])
        kvt = carve([D, B, D])
        ksm = carve([D, B, 16])
        at0 = carve([S, B, D])
        rd0 = carve([S, B, 16])
        c56 = carve([TT, NT, D])
        c56T = carve([D, N])
        k1T = carve([D, N])
        q1T = carve([D, N + 8])
        v1 = carve([S, B, H16, HD16 + 1])
        w_l1 = carve([D, 4, D])
        w_col1 = carve([D, 2])
        kblk = [carve([D, 2, 16, S]) for _ in range(2)]
        sc1 = [carve([D, 16, S]) for _ in range(2)]
        pr1 = [carve([D, 16, S]) for _ in range(2)]
        pT1 = carve([S, 16, D])
        m1 = carve([D, 2, 16])
        o1 = carve([D, D])
        w_r1 = carve([D, 16])
        sm16 = carve([TT, 8, NT, 16])
        wts = carve([TT, NT, E1])
        l1_end = at[0]
        at[0] = core_end
        clnT_s = [carve([D, 2, CL], F16) for _ in range(2)]
        cln_s = [carve([KP, KT + 1, D + 1]) for _ in range(2)]
        qtT = carve([D, 2, H8, N], F16)
        latT = carve([D, 2, N], F16)
        ctxT = carve([D, H8, N])
        qT2 = ctxT
        sscl = [carve([KP, N]) for _ in range(2)]
        pexp = [carve([KP, N]) for _ in range(2)]
        onrm = carve([TT, 4, D])
        rden = carve([TT, 4])
        rnl = carve([S, B, H8])
        at[0] = max(at[0], l1_end)
        m2 = carve([D, H8, D])
        w_kT2 = carve([D, 4, D])
        w_vT2 = carve([D, 4, D])
        w_o2 = carve([D, 4, D])
        w_q2 = carve([D, I2])
        qk_col = carve([D, 2])
        at[0] = core_end
        kst = [carve([D, 4, C], F16) for _ in range(2)]
        v3s = [carve([KP, KT, 192]) for _ in range(2)]
        q3 = carve([D, 4, N], F16)
        q_hi = carve([D, N], F16)
        q_lo = carve([D, N], F16)
        qst3 = carve([D, B, 4, 4, S], F16)
        p3 = [carve([KP, 16, S]) for _ in range(2)]
        oA = carve([D, B, 3, S])
        oB = carve([64, B, 2, S])
        mx3 = carve([TT, 8, 3])
        m3 = carve([TT, 8])
        sm8 = carve([TT, 8, NT, 8])
        wt3 = carve([TT, NT, 8])
        at[0] = core_end
        h3 = [carve([D, 4, N]) for _ in range(2)]
        wh3 = [carve([D, 2, 2 * FF], F16) for _ in range(2)]
        xTh = carve([D, 2, N], F16)

        ld_c = [sem(f"context_loaded{i}") for i in range(2)]
        ld_a, ld_w = sem("first_weights_loaded"), sem("weights_loaded")
        a_ready, v3_ones = sem("first_weights_ready"), sem("l3_value_blocks_set")
        st = [sem(f"context_results_stored{i}") for i in range(2)]
        a_full, a_free = sem("act_banks_full"), sem("act_banks_free")
        d_full, d_free = sem("dve_banks_full"), sem("dve_banks_free")
        v3_free = sem("value_banks_free")
        wsum_in, wsum = sem("weight_sums_ready"), sem("weight_sums_summed")
        w_ready = sem("weights_ready")
        c_var, c_sd = sem("context_variance"), sem("context_deviation")
        c_hat, c_lned = sem("context_normalised"), sem("context_affine")
        l0_var, l0_sd = sem("l0_variance"), sem("l0_deviation")
        l0_kn, l0_kaff = sem("l0_keys_normalised"), sem("l0_keys_affine")
        l0_w, l0_rhs = sem("l0_value_weights"), sem("l0_rhs_ready")
        l0_kp = sem("l0_kprime_ready")
        k_hi_ready, cln_hi = sem("l3_k_hi_ready"), sem("context_hi_ready")
        qt_hi = sem("l2_queries_hi_ready")
        sq_used = sem("l2_squares_used")
        acc_full, acc_used = sem("kv_sums_full"), sem("kv_sums_used")
        rn_sq, rn_sd = sem("l2_key_squares"), sem("l2_key_norms")
        dve_s, pool_s = sem("dve_steps"), sem("pool_steps")
        pe_passed = sem("tensor_waits_passed")
        operand, product = sem("operand_ready"), sem("product_ready")
        to_act, from_act = sem("act_input_ready"), sem("act_output_ready")
        ln_var, ln_rstd = sem("variance_ready"), sem("rstd_ready")
        ctx_done = sem("context_pass_done")
        h_rows, h_turned, h_cols = sem("hidden_tile_ready"), sem("hidden_tile_turned"), sem("hidden_tile_copied")
        l0_att = sem("l0_attention_ready")
        l0_st, l0_ld = sem("l0_attention_stored"), sem("l0_attention_loaded")
        l1_ld = sem("l1_loaded")
        l1_kv, l1_ak = sem("l1_keys_values_products"), sem("l1_keys_values_copied")
        l1_k, l1_sr = sem("l1_keys_ready"), sem("l1_scores_read")
        l1_kq, l1_s, l1_m = sem("l1_key_blocks"), sem("l1_scores"), sem("l1_shifted")
        l1_p, l1_t, l1_pt = sem("l1_probs"), sem("l1_probs_transposed"), sem("l1_probsT_ready")
        l1_o, l1_on, l1_ot = sem("l1_out"), sem("l1_out_normalised"), sem("l1_out_transposed")
        l1_done = sem("l1_pair_done")
        ex_ld = [sem(f"expert_loaded{i}") for i in range(2)]
        ex_ldd = [sem(f"expert_down_loaded{i}") for i in range(2)]
        ex_hi, ex_split = sem("expert_weights_hi_ready"), sem("expert_weights_split")
        ex_gu, ex_act, ex_h = sem("expert_gate_up"), sem("expert_activated"), sem("expert_hidden")
        ex_dn, ex_w, ex_acc = sem("expert_down"), sem("expert_weighted"), sem("expert_added")
        ld_m = sem("layer_weights_loaded")
        st_m = sem("latents_stored")
        l2_ld = [sem(f"l2_loaded{i}") for i in range(2)]
        l2_s, l2_sc, l2_p, l2_pv = sem("l2_sim"), sem("l2_scaled"), sem("l2_probs"), sem("l2_pv_tile")
        l2_m = sem("l2_joined_matrices")
        ld_rn = sem("latent_key_norms_loaded")
        l2_zero = sem("l2_queries_zeroed")
        l2_on, l2_t, l2_done = sem("l2_out_normalised"), sem("l2_out_transposed"), sem("l2_batch_done")
        l3_ld = [[sem(f"l3_keys_loaded{i}_{u}") for u in range(3)] for i in range(2)]
        l3_ldv = [sem(f"l3_values_loaded{i}") for i in range(2)]
        l3_pad = sem("l3_pad_loaded")
        l3_q, l3_mx, l3_mxd = sem("l3_queries_ready"), sem("l3_max_sim"), sem("l3_max_done")
        l3_dg, l3_sh, l3_row = sem("l3_maxima_ready"), sem("l3_maxima_turned"), sem("l3_shift_rows_ready")
        l3_s, l3_p, l3_pv, l3_o = sem("l3_sim"), sem("l3_probs"), sem("l3_pv_tile"), sem("l3_out_copied")
        l3_done = sem("l3_attention_done")
        st_out = sem("out_stored")
        lat_ready, l3_free, out_ready = sem("latents_ready"), sem("l2_memory_free"), sem("out_ready")

        block = ctx.enter_context(nc.Block())

        def batch(t, b):
            names = "abcd"[:len(t.shape) - 2]
            return t[bass.ds(b, 1)].rearrange("o p " + " ".join(names) + " -> (o p) " + " ".join(names))

        k3_in = d_k3.rearrange("n g e (s d) c -> n s (g e) d c", s=3)

        @block.sync
        def _(sp):
            def load_context(b, p):
                src = io["ctx"][bass.ds(b, 1)].rearrange("o (p j) d -> (o p) j d", j=KT)
                sp.dma_start(c_in[p][0:112], src[0:112]).then_inc(ld_c[p], 16)
                sp.dma_start(c_in[p][112:KP], src[112:KP]).then_inc(ld_c[p], 16)

            load_context(0, 0)
            n_first = 4
            first = [(ident, io["cst"][:, 0:D]), (w_l0[:, 0, :], io["L0_wk"]), (w_l0[:, 1, :], io["L0_wv"]),
                     (w_k3, io["L3_wkT"]), (w_v3, io["L3_wvT"]),
                     (em, io["mask"].rearrange("b (p j) -> p b j", j=KT)), (w_k2, io["L2_wk"]),
                     (vec[:, 0:n_first, :], io["vec"][0:n_first].unsqueeze(0).broadcast_to([D, n_first, D]))]
            for dst, src in first:
                sp.dma_start(dst, src).then_inc(ld_a, 16)
            load_context(1, 1)
            rest = [(wraw, io["wquant"]), (cst[:, D:CST_N], io["cst"][:, D:CST_N]),
                    (vec[:, n_first:, :], io["vec"][n_first:].unsqueeze(0)
                     .broadcast_to([D, len(V128) - n_first, D])),
                    (sel, io["sel"]), (kmask, io["kmask"].rearrange("b (p j) -> p b j", j=KT)),
                    (w_q0, io["L0_wq"]), (w_d0, io["L0_wd"]), (w_r3, io["L3_router"]), (w_q3, io["L3_wqT"]),
                    (w_o3, io["L3_woT"]), (qks, io["qks"].unsqueeze(0).broadcast_to([D, 2, HD8])),
                    (b1v, io["b1"].unsqueeze(0).broadcast_to([D, FF])),
                    (gates, io["gates"].unsqueeze(0).broadcast_to([D, 8])),
                    (x, io["x"].rearrange("(t p) d -> p t d", p=TT))]
            for dst, src in rest:
                sp.dma_start(dst, src).then_inc(ld_w, 16)

            def store_results(b, p):
                sp.wait_ge(c_lned, b + 1)
                sp.dma_start(batch(d_cln, b), cln[p].rearrange("p j d -> p (j d)")).then_inc(st[p], 16)
                sp.wait_ge(d_free, 6 * b + 3 + 3)
                for s, part in enumerate((k_hi[p], k_lo[p], k_hi[p])):
                    sp.dma_start(k3_in[bass.ds(b, 1), s].rearrange("o h d c -> (o h) d c"), part).then_inc(st[p], 16)
                sp.wait_ge(v3_free, 3 * b + 3)
                sp.dma_start(batch(d_v3, b), v3[p].rearrange("p j d -> p (j d)")).then_inc(st[p], 16)
                sp.wait_ge(d_free, 6 * b + 3 + 6)
                sp.dma_start(batch(d_clnT, b), clnT[p]).then_inc(st[p], 16)

            with sp.Fori(0, B // 2 - 1) as i:
                for p in range(2):
                    b = 2 * i + p
                    store_results(b, p)
                    sp.wait_ge(l0_rhs, b + 1)
                    load_context(b + 2, p)
            for b in (B - 2, B - 1):
                store_results(b, b % 2)
            for p in range(2):
                sp.wait_ge(st[p], 96 * (B // 2 + 1))

            sp.wait_ge(ctx_done, 1)
            for e in range(2):
                sp.dma_start(c56[S * e:S * e + S], io["ctx"].rearrange("(t e) s d -> e s t d", e=2)[e, 0:S])\
                    .then_inc(l1_ld, 16)
            sp.dma_start(w_l1, io["L1_w"]).then_inc(l1_ld, 16)
            sp.dma_start(w_col1, io["L1_cols"]).then_inc(l1_ld, 16)
            sp.dma_start(w_r1, io["L1_router"]).then_inc(l1_ld, 16)

            for dst, name in ((w_kT2, "L2_wkT"), (w_vT2, "L2_wvT"), (w_o2, "L2_wo"), (w_q2, "L2_wq"),
                              (qk_col, "qk_cols")):
                sp.dma_start(dst, io[name]).then_inc(ld_m, 16)

            def load_experts1(g, p):
                sp.dma_start(wex[p][:, 0:G1 * 3 * D], batch(io["L1_ex"], g)).then_inc(ex_ld[p], 16)

            load_experts1(0, 0)
            load_experts1(1, 1)

            sp.wait_ge(l0_att, 1)
            sp.dma_start(d_att.rearrange("b h n e -> n (b h) e"), at0.rearrange("n b (h e) -> n (b h) e", h=H16))\
                .then_inc(l0_st, 16)
            sp.wait_ge(l0_st, 16)
            sp.dma_start(y2, d_att.rearrange("b h n e -> (b h n e)").rearrange("(t p d) -> p t d", p=TT, d=D))\
                .then_inc(l0_ld, 16)

            with sp.Fori(0, E1 // G1 // 2 - 1) as i:
                for p in range(2):
                    g = 2 * i + p
                    sp.wait_ge(ex_dn, G1 * (g + 1))
                    load_experts1(g + 2, p)

            sp.wait_ge(lat_ready, 1)
            sp.dma_start(d_lat.rearrange("(t p) d -> p t d", p=TT), y).then_inc(st_m, 16)
            sp.wait_ge(lat_ready, 2)
            sp.dma_start(d_latT, latT).then_inc(st_m, 16)
            sp.wait_ge(st_m, 32)

            def load_keys2(b, p):
                sp.dma_start(clnT_s[p][:, :, 0:C], batch(d_clnT, b)).then_inc(l2_ld[p], 16)
                sp.dma_start(clnT_s[p][:, :, C:CL], d_latT[:, :, bass.ds(b * S, S)]).then_inc(l2_ld[p], 16)
                src = batch(d_cln, b).rearrange("p (j d) -> p j d", j=KT)
                sp.dma_start(cln_s[p][0:112, 0:KT, 0:D], src[0:112]).then_inc(l2_ld[p], 16)
                sp.dma_start(cln_s[p][112:KP, 0:KT, 0:D], src[112:KP]).then_inc(l2_ld[p], 16)
                sp.dma_start(cln_s[p][0:S, KT, 0:D], d_lat[bass.ds(b * S, S), :]).then_inc(l2_ld[p], 16)

            for b in range(2):
                load_keys2(b, b)
            sp.wait_ge(ln_rstd, RSTD["latent_k"])
            sp.dma_start(d_rl.rearrange("(t p) h -> p t h", p=TT), qss[:, 1, :].rearrange("p (t h) -> p t h", t=NT))\
                .then_inc(st_m, 16)
            sp.wait_ge(st_m, 48)
            sp.dma_start(rnl, d_rl.rearrange("(b q) h -> q b h", b=B)).then_inc(ld_rn, 16)
            with sp.Fori(0, B // 2 - 1) as i:
                for p in range(2):
                    b = 2 * i + p
                    sp.wait_ge(l2_pv, (KT + 1) * (b + 1) + 2)
                    load_keys2(b + 2, p)

            def load_keys3(b, p, u):
                src = d_k3[bass.ds(b, 1)].rearrange("o g e r c -> (o e) r g c")
                at = 500 * u
                for hh in range(4):
                    sp.dma_start(kst[p][32 * hh + 8:32 * hh + 32, :, at:at + 500], src[hh, :, :, at:at + 500])\
                        .then_inc(l3_ld[p][u], 16)

            def load_values3(b, p):
                src = batch(d_v3, b).rearrange("p (j d) -> p j d", j=KT)
                sp.dma_start(v3s[p][0:112], src[0:112]).then_inc(l3_ldv[p], 16)
                sp.dma_start(v3s[p][112:KP], src[112:KP]).then_inc(l3_ldv[p], 16)

            sp.wait_ge(l3_free, 1)
            for p in range(2):
                for hh in range(4):
                    sp.dma_start(kst[p][32 * hh:32 * hh + 8],
                                 io["pad"][min(hh, 1)].unsqueeze(1).broadcast_to([8, 4, C])).then_inc(l3_pad, 16)
            for b in range(2):
                for u in range(3):
                    load_keys3(b, b, u)
                load_values3(b, b)
            with sp.Fori(0, B // 2 - 1) as i:
                for p in range(2):
                    b = 2 * i + p
                    for u in range(3):
                        sp.wait_ge(l3_s, KT * b + 4 * (u + 1))
                        load_keys3(b + 2, p, u)
                    sp.wait_ge(l3_pv, KT * (b + 1) + 2)
                    load_values3(b + 2, p)

            def load_gate_up3(e, p):
                sp.dma_start(wex[p][:, 0:2 * FF], batch(io["L3_ex"], e)[:, 0:2 * FF]).then_inc(ex_ld[p], 16)

            def load_down3(e, p):
                sp.dma_start(wex[p][:, 2 * FF:], batch(io["L3_ex"], e)[:, 2 * FF:]).then_inc(ex_ldd[p], 16)

            for e in range(2):
                load_gate_up3(e, e)
                load_down3(e, e)
            with sp.Fori(0, E3 // 2 - 1) as i:
                for p in range(2):
                    e = 2 * i + p
                    sp.wait_ge(ex_split, e + 1)
                    load_gate_up3(e + 2, p)
                    sp.wait_ge(ex_dn, E1 + e + 1)
                    load_down3(e + 2, p)
            sp.wait_ge(out_ready, 1)
            sp.dma_start(out.rearrange("(t p) d -> p t d", p=TT), x[:, :, :]).then_inc(st_out, 16)
            sp.wait_ge(st_out, 16)


        @block.tensor
        def _(pe):
            op = Count(pe, operand)

            def transposes(src, k):
                for t in range(NT):
                    last = pe.transpose(ps[0:D, k, TT * t:TT * t + TT], src[:, t, :], ident[0:TT, 0:TT])
                last.then_inc(product, 1)

            def by_tokens(srcT, w, k, cols=D):
                for t in range(NT):
                    mm = pe.matmul(ps[0:TT, k, cols * t:cols * t + cols], srcT[:, TT * t:TT * t + TT], w,
                                   start=True, stop=True)
                mm.then_inc(product, 1)

            DV = (3, 4, 5)

            def bank_a(b, n):
                pe.wait_ge(a_free, a_uses(b) + n + 1)
                return n % 3

            def l0_sums(b, p):
                pe.wait_ge(l0_kp, b + 1)
                pe.wait_ge(l0_rhs, b + 1)
                pe.wait_ge(acc_used, b + 1)
                for j in range(KT):
                    mm = pe.matmul(ps[0:D, 6 + p, 0:D + 2], kpr[:, j, :], rhs0[:, j, :],
                                   start=(j == 0), stop=(j == KT - 1))
                mm.then_inc(acc_full, 1)

            def l2_keys(turn, p, first_use):
                pe.wait_ge(d_free, 6 * turn + 3)
                for j in range(KT):
                    k = bank_a(turn, first_use + j)
                    for n, (a, w) in enumerate(((0, 0), (0, 1), (1, 0))):
                        mm = pe.matmul(ps[0:KP, k, :], clnT[p][:, a, KP * j:KP * j + KP], w_k2h[:, w, :],
                                       start=(n == 0), stop=(n == 2))
                    mm.then_inc(a_full, 1)

            def context(b, p, loads, first=False):
                def bank_d(n):
                    if n < 6:
                        pe.wait_ge(d_free, 6 * b + n + 1)
                    else:
                        pe.wait_ge(v3_free, 3 * b + n - 5)
                    return DV[n % 3]

                pe.wait_ge(ld_c[p], 32 * loads)
                if first:
                    pe.wait_ge(ld_a, A_LOADS * 16)
                for u in range(3):
                    k = bank_a(b, u)
                    for j in range(4):
                        mm = pe.transpose(ps[0:D, k, KP * j:KP * j + KP], c_in[p][:, 4 * u + j, :],
                                          ident[0:KP, 0:KP])
                    mm.then_inc(a_full, 1)
                if first:
                    pe.wait_ge(a_ready, 1)
                else:
                    l0_sums(b - 1, 1 - p)
                for u in range(3):
                    pe.wait_ge(a_free, a_uses(b) + 3 + u + 1)
                    k = bank_d(u)
                    pe.matmul(ps[0:D, k, 0:4 * KP], w_k3,
                              cT[p][:, 4 * u:4 * u + 4, :].rearrange("p j n -> p (j n)"),
                              start=True, stop=True).then_inc(d_full, 1)
                for u in range(6):
                    k = bank_a(b, 3 + u)
                    for j in range(2):
                        mm = pe.matmul(ps[0:KP, k, 256 * j:256 * j + 256], cT[p][:, 2 * u + j, :],
                                       w_l0[:, :, :].rearrange("p a n -> p (a n)"), start=True, stop=True)
                    mm.then_inc(a_full, 1)
                for u in range(3):
                    k = bank_d(3 + u)
                    for j in range(4):
                        mm = pe.matmul(ps[0:KP, k, D * j:D * j + D], cT[p][:, 4 * u + j, :], w_v3,
                                       start=True, stop=True)
                    mm.then_inc(d_full, 1)
                if first:
                    pe.wait_ge(wsum_in, 1)
                    pe.matmul(ps[0:D, 7, 0:5], cs("mean"), mw, start=True, stop=True).then_inc(wsum, 1)
                else:
                    l2_keys(b, 1 - p, 9)
                pe.wait_ge(c_lned, b + 1)
                for u in range(3):
                    k = bank_d(6 + u)
                    for j in range(4):
                        mm = pe.transpose(ps[0:D, k, KP * j:KP * j + KP], cln[p][:, 4 * u + j, :],
                                          ident[0:KP, 0:KP])
                    mm.then_inc(d_full, 1)

            context(0, 0, 1, first=True)
            with pe.Fori(0, B // 2 - 1) as i:
                context(2 * i + 1, 1, i + 1)
                context(2 * i + 2, 0, i + 2)
            context(B - 1, 1, B // 2)
            l0_sums(B - 1, 1)
            l2_keys(B, 1, 0)

            op.next()
            for b in range(B):
                mm = pe.transpose(ps[0:D, b // 4, D * (b % 4):D * (b % 4) + D], kv_all[:, b, 0:D], ident)
            mm.then_inc(product, 1)
            op.next()
            for b in range(B):
                mm = pe.matmul(ps[0:D, 2 + b // 4, D * (b % 4):D * (b % 4) + D], kvt[:, b, :], w_l0[:, 1, :],
                               start=True, stop=True)
            mm.then_inc(product, 1)
            op.next()
            transposes(z, 4)
            pe.wait_ge(l1_ld, L1_LOADS * 16)
            for t in range(NT):
                last = pe.transpose(ps[0:D, 0, TT * t:TT * t + TT], c56[:, t, :], ident[0:TT, 0:TT])
            last.then_inc(l1_kv, 1)
            op.next()
            by_tokens(xT, w_q0[:, :], 5)
            pe.wait_ge(l1_ak, 1)
            pe.matmul(ps[0:D, 1, 0:N], w_l1[:, 1, :], c56T, start=True, stop=True).then_inc(l1_kv, 1)
            op.next()
            transposes(y2, 4)
            op.next()
            for b in range(B):
                pe.matmul(ps[0:S, 6 + b // 4, D * (b % 4):D * (b % 4) + D], xT[:, S * b:S * b + S], kvm[:, b, :],
                          start=True, stop=True)
                mm = pe.matmul(ps[0:S, 5, 16 * b:16 * b + 16], xT[:, S * b:S * b + S], ksm[:, b, :],
                               start=True, stop=True)
            mm.then_inc(product, 1)
            pe.wait_ge(l1_ak, 2)
            pe.matmul(ps[0:D, 0, 0:N], cs("rot"), k1T, start=True, stop=True).then_inc(l1_kv, 1)
            for b in range(B):
                dst = ps[0:S, 2 + b // 4, D * (b % 4):D * (b % 4) + D]
                pe.matmul(dst, c56T[:, S * b:S * b + S], w_l1[:, 2, :], start=True, stop=False)
                mm = pe.matmul(dst, cs("mean", 1)[:, 0:S], vec[0:1, V128.index("L1_vb"), :], start=False, stop=True)
            mm.then_inc(l1_kv, 1)
            pe.wait_ge(l0_ld, 16)
            transposes(y2, 4)
            op.next()
            by_tokens(xT2, w_d0[:, :], 0)

            def quantised_ffn(n, first, n_first, second):
                op.next()
                zps = ps[0:D, 0, 0:256].bitcast(BF16)
                for t in range(NT):
                    mm = pe.transpose(zps[:, TT * t:TT * t + TT], zq[:, t, :], ident_h[0:TT, 0:TT])
                mm.then_inc(product, 1)
                op.next()
                for t in range(NT):
                    for m in range(n_first):
                        mm = pe.matmul(ps[0:TT, t + 4 * m, :], zqT[:, TT * t:TT * t + TT], wquant[:, first + m, :],
                                       start=True, stop=True)
                mm.then_inc(product, 1)

                def turn_hidden(t):
                    pe.wait_ge(h_rows, NT * n + t + 1)
                    hps = ps[0:D, 4 + t, 0:256].bitcast(BF16)
                    for c in range(4):
                        mm = pe.transpose(hps[:, TT * c:TT * c + TT], hq[:, t, D * c:D * c + D],
                                          ident_h[0:TT, 0:TT])
                    mm.then_inc(h_turned, 1)

                turn_hidden(0)
                for t in range(NT):
                    if t + 1 < NT:
                        turn_hidden(t + 1)
                    pe.wait_ge(h_cols, NT * n + t + 1)
                    for c in range(4):
                        mm = pe.matmul(ps[0:TT, 2, D * t:D * t + D], hqT[:, c, TT * t:TT * t + TT],
                                       wquant[:, second, D * c:D * c + D], start=(c == 0), stop=(c == 3))
                mm.then_inc(product, 1)

            pe.wait_ge(w_ready, 1)
            pe.wait_ge(l1_ak, 3)
            quantised_ffn(0, 0, 2, 2)

            op.next()
            transposes(z, 0)
            op.next()
            pe.matmul(ps[0:D, 1, 0:N], w_l1[:, 0, :], xT, start=True, stop=True).then_inc(product, 1)
            op.next()
            pe.matmul(ps[0:D, 2, 0:N], cs("rot"), q1T[:, 0:N], start=True, stop=True).then_inc(product, 1)
            op.next()

            def scores1(i):
                pe.wait_ge(l1_kq, i + 1)
                if i:
                    pe.wait_ge(l1_sr, i)
                for e in range(2):
                    at = (2 * i + e) * S
                    for half in range(2):
                        mm = pe.matmul(ps[64 * e:64 * e + 64, half, 0:8 * S], q1T[:, at:at + 64],
                                       kblk[i % 2][:, e, 8 * half:8 * half + 8, :].rearrange("p h s -> p (h s)"),
                                       start=True, stop=True)
                mm.then_inc(l1_s, 1)

            def turn_probs1(i):
                pe.wait_ge(l1_p, i + 1)
                for h in range(16):
                    mm = pe.transpose(ps[0:S, 2 + h // 4, D * (h % 4):D * (h % 4) + D], pr1[i % 2][:, h, :], ident)
                mm.then_inc(l1_t, 1)

            def out1(i):
                pe.wait_ge(l1_pt, i + 1)
                if i:
                    pe.wait_ge(l1_on, i)
                for e in range(2):
                    for h in range(16):
                        mm = pe.matmul(ps[64 * e:64 * e + 64, 6, 9 * h:9 * h + 9], pT1[:, h, 64 * e:64 * e + 64],
                                       v1[:, 2 * i + e, h, :], start=True, stop=True)
                mm.then_inc(l1_o, 1)

            def turn_out1(i):
                pe.wait_ge(l1_on, i + 1)
                if i:
                    pe.wait_ge(l1_done, i)
                pe.transpose(ps[0:D, 7, 0:D], o1, ident).then_inc(l1_ot, 1)

            scores1(0)
            scores1(1)
            for i in range(NT):
                turn_probs1(i)
                if i + 2 < NT:
                    scores1(i + 2)
                if i:
                    turn_out1(i - 1)
                out1(i)
            turn_out1(NT - 1)
            pe.wait_ge(l1_done, NT)
            by_tokens(xT2, w_l1[:, 3, :], 0)

            pe.wait_ge(ld_m, 5 * 16)
            for h in range(H8):
                r, c = 64 * (h % 2), h // 2
                mm = pe.matmul(ps[0:D, 6 + h % 2, D * c:D * c + D], w_vT2[r:r + 64, c, :], w_o2[r:r + 64, c, :],
                               start=True, stop=True)
            mm.then_inc(l2_m, 1)
            op.next()
            transposes(z, 0)
            op.next()
            by_tokens(xT, w_r1, 1, cols=16)

            def w1(k, group, col):
                return wex[group][:, D * (3 * k + col):D * (3 * k + col) + D]

            def gate_up1(s, loads):
                if s % G1 == 0:
                    pe.wait_ge(ex_ld[s // G1 % 2], 16 * loads)
                for m in range(2):
                    mm = pe.matmul(ps[0:D, 2 + 2 * (s % 2) + m, 0:N], w1(s % G1, s // G1 % 2, m), xT,
                                   start=True, stop=True)
                mm.then_inc(ex_gu, 1)

            def expert1(turn, s, more=True):
                e = 2 * G1 * turn + s
                if more:
                    pe.wait_ge(ex_h, e + 1)
                    gate_up1(s + 1, turn + 1 + (s + 1) // (2 * G1))
                pe.wait_ge(ex_w, e + 1)
                pe.wait_ge(ex_h, e + 2)
                for t in range(NT):
                    mm = pe.matmul(ps[0:TT, 6 + s % 2, D * t:D * t + D],
                                   (xT2, xT3)[s % 2][:, TT * t:TT * t + TT], w1(s % G1, s // G1 % 2, 2),
                                   start=True, stop=True)
                mm.then_inc(ex_dn, 1)

            gate_up1(0, 1)
            pe.wait_ge(l2_m, 2)
            with pe.Fori(0, E1 // (2 * G1) - 1) as i:
                for s in range(2 * G1):
                    expert1(i, s)
            for s in range(2 * G1):
                expert1(E1 // (2 * G1) - 1, s, more=s < 2 * G1 - 1)

            op.next()
            transposes(y, 0)
            op.next()
            for w in (w_q2, w_k2):
                for t in range(NT):
                    mm = pe.matmul(ps[0:TT, t if w is w_q2 else 4 + t, :], xT[:, TT * t:TT * t + TT], w,
                                   start=True, stop=True)
                    if w is w_q2 or t == NT - 1:
                        mm.then_inc(product, 1)
            op.next()
            for c in range(4):
                for t in range(NT):
                    mm = pe.transpose(ps[0:D, c, TT * t:TT * t + TT], big[:, t, D * c:D * c + D],
                                      ident[0:TT, 0:TT])
            mm.then_inc(product, 1)
            op.next()
            for h in range(H8):
                mm = pe.matmul(ps[0:D, (4 + h) % 8, 0:N], w_kT2[:, h // 2, :], qT2[:, h, :], start=True, stop=True)
                if h % 4 == 3:
                    mm.then_inc(product, 1)
            op.next()

            def sim2(b, p, t):
                rows, cols = (KP, KP * t) if t < KT else (S, C)
                pe.wait_ge(l2_sc, (KT + 1) * b + t + 1)
                if t == KT:
                    pe.nop().then_inc(pe_passed, 1)
                for n, (a, q) in enumerate(((0, 0), (0, 1), (1, 0))):
                    mm = pe.matmul(ps[0:rows, (t + p) % 2, 0:N].rearrange("p (h q) -> p h q", h=H8),
                                   clnT_s[p][:, a, cols:cols + rows], qtT[:, q, :, bass.ds(b * S, S)],
                                   start=(n == 0), stop=(n == 2))
                mm.then_inc(l2_s, 1)

            def pv2(b, p, t):
                rows = KP if t < KT else S
                pe.wait_ge(l2_p, (KT + 1) * b + t + 3)
                for c in range(4):
                    dst = ps[0:TT, 4 + 2 * p, 129 * c:129 * c + 129] if c < 3 else ps[0:TT, 5 + 2 * p, 0:129]
                    mm = pe.matmul(dst, pexp[(t + p) % 2][0:rows, TT * c:TT * c + TT], cln_s[p][0:rows, t, :],
                                   start=(t == 0 and c in (0, 3)), stop=(t == KT), skip_group_check=True)
                mm.then_inc(l2_pv, 1)

            def turn2(b):
                pe.wait_ge(l2_on, b)
                pe.wait_ge(l2_done, b)
                for c in range(4):
                    mm = pe.transpose(ps[0:D, 2, TT * c:TT * c + TT], onrm[:, c, :], ident[0:TT, 0:TT])
                mm.then_inc(l2_t, 1)

            def batch2(b, p, loads, first=False, more=True):
                for t in range(KT + 1):
                    if t + 2 <= KT:
                        sim2(b, p, t + 2)
                    elif more:
                        if t + 2 == KT + 1:
                            pe.wait_ge(l2_ld[1 - p], 80 * loads)
                        sim2(b + 1, 1 - p, t + 1 - KT)
                    pv2(b, p, t)
                    if t == 4 and not first:
                        turn2(b)

            pe.wait_ge(l2_ld[0], 80)
            sim2(0, 0, 0)
            sim2(0, 0, 1)
            batch2(0, 0, 1, first=True)
            batch2(1, 1, 2)
            with pe.Fori(1, B // 2 - 1) as i:
                for p in range(2):
                    batch2(2 * i + p, p, i + 1 + p)
            batch2(B - 2, 0, B // 2)
            batch2(B - 1, 1, None, more=False)
            turn2(B)
            pe.wait_ge(l2_done, B + 1)
            for t in range(NT):
                for h in range(H8):
                    mm = pe.matmul(ps[0:TT, 0, D * t:D * t + D], ctxT[:, h, TT * t:TT * t + TT], m2[:, h, :],
                                   start=(h == 0), stop=(h == H8 - 1))
            mm.then_inc(product, 1)

            quantised_ffn(1, 3, 1, 4)

            op.next()
            transposes(z, 0)
            op.next()
            pe.matmul(ps[0:D, 1, 0:N], w_q3[:, :], xT, start=True, stop=True).then_inc(product, 1)
            op.next()
            for g in range(4):
                pe.matmul(ps[0:D, g, 0:N], sel[:, 0, g, :], q_hi, start=True, stop=False)
                mm = pe.matmul(ps[0:D, g, 0:N], sel[:, 1, g, :], q_lo, start=False, stop=True)
            mm.then_inc(product, 1)

            def max_sim(bn, pn, u, loads):
                third, pair = u // 8, u % 8
                if pair == 0:
                    pe.wait_ge(l3_ld[pn][third], 64 * loads)
                pe.wait_ge(l3_mxd, 24 * bn + u + 1)
                q = qst3[:, bass.ds(bn, 1), pair // 2, 2 * (pair % 2):2 * (pair % 2) + 2, :]
                pe.matmul(ps[0:TT, MAX_BANKS[u % 3], 0:500], q.rearrange("p o h q -> p (o h q)"),
                          kst[pn][:, pair // 2, 500 * third:500 * third + 500],
                          start=True, stop=True).then_inc(l3_mx, 1)

            def turn_maxima(bn):
                pe.wait_ge(l3_dg, bn + 1)
                pe.transpose(ps[0:8, MAX_BANKS[0], 0:TT], m3, ident[0:TT, 0:TT]).then_inc(l3_sh, 1)

            def sim3(b, p, t):
                pe.wait_ge(l3_p, KT * b + t + 1)
                for g in range(4):
                    mm = pe.matmul(ps[0:KP, 2 * (t % 2) + g // 2, 224 * (g % 2):224 * (g % 2) + 224],
                                   kst[p][:, g, KP * t:KP * t + KP],
                                   qst3[:, bass.ds(b, 1), g, :, :].rearrange("p o h q -> p (o h q)"),
                                   start=True, stop=True)
                mm.then_inc(l3_s, 1)

            def pv3(b, p, t):
                pe.wait_ge(l3_p, KT * b + t + 3)
                for g in range(4):
                    pe.matmul(ps[32 * g:32 * g + 32, 6, 0:168], v3s[p][:, t, 32 * g:32 * g + 32],
                              p3[t % 2][:, 3 * g:3 * g + 3, :].rearrange("p h q -> p (h q)"),
                              start=(t == 0), stop=(t == KT - 1), skip_group_check=True)
                for g in range(2):
                    mm = pe.matmul(ps[32 * g:32 * g + 32, 6, 168:280], v3s[p][:, t, 128 + 32 * g:160 + 32 * g],
                                   p3[t % 2][:, 12 + 2 * g:14 + 2 * g, :].rearrange("p h q -> p (h q)"),
                                   start=False, stop=(t == KT - 1), skip_group_check=True)
                mm.then_inc(l3_pv, 1)

            UNITS = (3, 2, 3, 2, 2, 3, 2, 3, 2, 2, 0, 0)

            def batch3(b, p, loads, more=True):
                pe.wait_ge(l3_row, b + 1)
                if more:
                    pe.wait_ge(l3_q, b + 2)
                sim3(b, p, 0)
                u = 0
                for t in range(KT):
                    if t + 1 < KT:
                        sim3(b, p, t + 1)
                    for _ in range(UNITS[t] if more else 0):
                        max_sim(b + 1, 1 - p, u, loads + p)
                        u += 1
                    if t == 0:
                        pe.wait_ge(l3_ldv[p], 32 * loads)
                        pe.wait_ge(l3_o, b + 1)
                    if more and t == KT - 1:
                        turn_maxima(b + 1)
                    pv3(b, p, t)

            pe.wait_ge(l3_pad, 8 * 16)
            pe.wait_ge(l3_q, 1)
            for u in range(24):
                max_sim(0, 0, u, 1)
            turn_maxima(0)
            with pe.Fori(0, B // 2 - 1) as i:
                for p in range(2):
                    batch3(2 * i + p, p, i + 1)
            batch3(B - 2, 0, B // 2)
            batch3(B - 1, 1, B // 2, more=False)
            pe.wait_ge(l3_o, B + 1)
            for k, names in enumerate((("numA", "numB"), ("denA", "denB"))):
                parts = [(cs(names[0])[:, D * h:D * h + D], oA[:, :, h, :]) for h in range(3)]
                parts += [(cs(names[1], 64)[:, D * h:D * h + D], oB[:, :, h, :]) for h in range(2)]
                for n, (w, o) in enumerate(parts):
                    mm = pe.matmul(ps[0:D, k, 0:N].rearrange("p (b q) -> p b q", b=B), w, o,
                                   start=(n == 0), stop=(n == 4))
            mm.then_inc(product, 1)
            op.next()
            by_tokens(xT2, w_o3[:, :], 2)

            op.next()
            transposes(z, 0)
            op.next()
            by_tokens(xT, w_r3[:, :], 1, cols=E3)

            def gate_up3(e, p, c):
                for m in range(2):
                    at = FF * m + D * c
                    for n, (a, w) in enumerate(((0, 0), (1, 0), (0, 1))):
                        mm = pe.matmul(ps[0:D, 2 + 2 * (c % 2) + m, 0:N], wh3[p][:, w, at:at + D], xTh[:, a, :],
                                       start=(n == 0), stop=(n == 2))
                mm.then_inc(ex_gu, 1)

            def down3(e, p, loads):
                pe.wait_ge(ex_ldd[p], 16 * loads)
                pe.wait_ge(ex_h, E1 + 4 * e + 5)
                pe.wait_ge(ex_w, E1 + e + 1)
                for t in range(NT):
                    for c in range(4):
                        mm = pe.matmul(ps[0:TT, 6 + p, D * t:D * t + D], h3[p][:, c, TT * t:TT * t + TT],
                                       wex[p][:, 2 * FF + D * c:2 * FF + D * c + D], start=(c == 0), stop=(c == 3))
                mm.then_inc(ex_dn, 1)

            def expert3(e, p, i, first=False):
                pe.wait_ge(ex_split, e + 1)
                for c in range(4):
                    pe.wait_ge(ex_h, E1 + 4 * e + c)
                    gate_up3(e, p, c)
                    if c == 1 and not first:
                        down3(e - 1, 1 - p, i + p)

            expert3(0, 0, 0, first=True)
            expert3(1, 1, 0)
            with pe.Fori(1, E3 // 2) as i:
                for p in range(2):
                    expert3(2 * i + p, p, i)
            down3(E3 - 1, 1, E3 // 2)

        @block.scalar
        def _(act):
            act.nop().then_inc(a_free, 3)
            act.nop().then_inc(l2_p, 2)
            act.nop().then_inc(l3_p, 2)

            def bank_a(b, n):
                act.wait_ge(a_full, a_uses(b) + n + 1)
                return n % 3

            def deviation(b):
                act.wait_ge(c_var, b + 1)
                act.activation(sm[:, 5, 0:KT], sm[:, 4, 0:KT], ACT.Sqrt).then_inc(c_sd, 1)

            def l2_squares(turn, first_use, between=None):
                for j in range(KT):
                    k = bank_a(turn, first_use + j)
                    act.wait_ge(sq_used, KT * (turn - 1) + j + 1)
                    act.activation(sqk[:, j % SQ, :], ps[0:KP, k, :], ACT.Square).then_inc(a_free, 1)
                    if between and j == 2:
                        between()

            def context(b, p, loads, first=False, more=True):
                for u in range(3):
                    k = bank_a(b, u)
                    act.copy(cT[p][:, 4 * u:4 * u + 4, :].rearrange("p j n -> p (j n)"), ps[0:D, k, 0:4 * KP])\
                        .then_inc(a_free, 1)
                if first:
                    deviation(0)
                act.wait_ge(st[p], 96 * loads)
                for u in range(3):
                    act.wait_ge(d_full, 9 * b + u + 1)
                    act.copy(k_hi[p][:, 500 * u:500 * u + 500], ps[0:D, 3 + u, 0:500]).then_inc(k_hi_ready, 1)
                act.wait_ge(l0_kn, b + 1)
                for u in range(6):
                    k = bank_a(b, 3 + u)
                    src = ps[0:KP, k, :].rearrange("p (j a n) -> p j a n", j=2, a=2)
                    act.activation(sq0[:, 2 * u:2 * u + 2].rearrange("p j a n -> p (j a n)"), ps[0:KP, k, :],
                                   ACT.Square)
                    act.copy(kraw[:, 2 * u:2 * u + 2, :], src[:, :, 0, :]).then_inc(a_free, 1)
                if first:
                    act.wait_ge(v3_ones, 4)
                for u in range(3):
                    act.wait_ge(d_full, 9 * b + 3 + u + 1)
                    src = ps[0:KP, 3 + u, :].rearrange("p (j n) -> p j n", j=4)
                    dst = v3[p][:, 4 * u:4 * u + 4, :]
                    act.copy(dst[:, :, 0:128].rearrange("p j (g c) -> p j g c", c=32)[:, :, :, 0:24],
                             src[:, :, 0:96].rearrange("p j (g c) -> p j g c", c=24))
                    act.copy(dst[:, :, 128:192].rearrange("p j (g c) -> p j g c", c=32)[:, :, :, 0:16],
                             src[:, :, 96:128].rearrange("p j (g c) -> p j g c", c=16))\
                        .then_inc(v3_free, 1)

                def deviations():
                    if more:
                        deviation(b + 1)
                    act.wait_ge(l0_var, b + 1)
                    act.activation(sm[:, 8, :], sm[:, 7, :], ACT.Sqrt).then_inc(l0_sd, 1)

                if first:
                    deviations()
                else:
                    l2_squares(b, 9, deviations)
                for u in range(3):
                    act.wait_ge(d_full, 9 * b + 6 + u + 1)
                    act.copy(clnT[p][:, 0, 500 * u:500 * u + 500], ps[0:D, 3 + u, 0:500]).then_inc(cln_hi, 1)

            context(0, 0, 1, first=True)
            with act.Fori(0, B // 2 - 1) as i:
                context(2 * i + 1, 1, i + 1)
                context(2 * i + 2, 0, i + 2)
            context(B - 1, 1, B // 2, more=False)
            l2_squares(B, 0)
            act.wait_ge(rn_sq, 1)
            rn_flat = rn[:, :, :, :].rearrange("p b t h -> p (b t h)")
            act.activation(rn_flat, rn_flat, ACT.Sqrt).then_inc(rn_sd, 1)
            act.wait_ge(ld_w, N_LOADS * 16)
            act.activation(tg[:, :], gates[:, :], ACT.Tanh).then_inc(from_act, 1)

            act.wait_ge(l1_kv, 1)
            act.copy(c56T, ps[0:D, 0, 0:N]).then_inc(l1_ak, 1)
            act.wait_ge(l1_kv, 2)
            act.activation(k1T, ps[0:D, 1, 0:N], ACT.Identity, bias=w_col1[:, 1:2]).then_inc(l1_ak, 1)
            act.wait_ge(l1_kv, 4)
            act.copy(v1[:, :, :, 0:HD16], ps[0:S, 2:4, :].rearrange("p k (b h d) -> p (k b) h d", b=4, h=H16))\
                .then_inc(l1_ak, 1)

            act.wait_ge(product, PRODUCT["ffn0_in"])
            for t in range(NT):
                act.activation(big[:, t, :], ps[0:TT, t, :], ACT.Silu, scale=acol[:, 2, t:t + 1]).then_inc(from_act, 1)

            def heads_joined1(i):
                act.wait_ge(l1_ot, i + 1)
                act.copy(xT2[:, 2 * i * S:2 * (i + 1) * S].rearrange("p (e s) -> p e s", e=2),
                         ps[0:D, 7, 0:D].rearrange("p (e s) -> p e s", e=2)[:, :, 0:S]).then_inc(l1_done, 1)

            def probs1(i):
                act.wait_ge(l1_m, i + 1)
                if i > 1:
                    act.wait_ge(l1_t, i - 1)
                act.activation(pr1[i % 2], sc1[i % 2], ACT.Exp).then_inc(l1_p, 1)

            probs1(0)
            for i in range(NT):
                if i + 1 < NT:
                    probs1(i + 1)
                act.wait_ge(l1_t, i + 1)
                if i:
                    act.wait_ge(l1_o, i)
                act.copy(pT1.rearrange("p (k h) n -> p k (h n)", k=4), ps[0:S, 2:6, :]).then_inc(l1_pt, 1)
                if i:
                    heads_joined1(i - 1)
            heads_joined1(NT - 1)

            act.wait_ge(l2_m, 1)
            act.copy(m2.rearrange("p (c r) n -> p r c n", r=2),
                     ps[0:D, 6:8, :].rearrange("p r (c n) -> p r c n", c=4)).then_inc(l2_m, 1)

            def silu1(e, p):
                act.wait_ge(ex_gu, e + 1)
                act.activation(exs[p], ps[0:D, 2 + 2 * p, 0:N], ACT.Silu).then_inc(ex_act, 1)

            silu1(0, 0)
            silu1(1, 1)
            act.wait_ge(to_act, 1)
            act.activation(sm16[:, 6], sm16[:, 0], ACT.Sigmoid).then_inc(from_act, 1)
            with act.Fori(1, E1 // 2) as i:
                for p in range(2):
                    silu1(2 * i + p, p)

            for t in range(NT):
                act.wait_ge(product, PRODUCT["latent_q"] + t)
                act.activation(big2[:, t, :], ps[0:TT, t, :], ACT.Square).then_inc(from_act, 1)
            act.wait_ge(to_act, 2)
            act.activation(qss[:, 2, :], qss[:, 0, :], ACT.Sqrt).then_inc(from_act, 1)
            act.wait_ge(product, PRODUCT["latent_k"])
            for t in range(NT):
                act.activation(big3[:, t, :], ps[0:TT, 4 + t, :], ACT.Square).then_inc(from_act, 1)
            act.wait_ge(product, PRODUCT["latent_qT"])
            act.wait_ge(l2_zero, 1)
            act.copy(qT2[64:D, 1::2, :], ps[64:D, 0:4, 0:N]).then_inc(from_act, 1)
            for half in range(2):
                act.wait_ge(product, PRODUCT["queries2"] + half)
                for h in range(4 * half, 4 * half + 4):
                    act.copy(qtT[:, 0, h, :], ps[0:D, (4 + h) % 8, 0:N]).then_inc(qt_hi, 1)
            with act.Fori(0, B // 2) as i:
                for p in range(2):
                    b = 2 * i + p
                    for t in range(KT + 1):
                        n = (KT + 1) * b + t
                        rows = KP if t < KT else S
                        act.wait_ge(l2_sc, n + 3)
                        act.wait_ge(l2_pv, n + 1)
                        bias = kbias[:, bass.ds(b, 1), t] if t < KT else lbias[0:S, :]
                        act.activation(pexp[(t + p) % 2][0:rows], sscl[(t + p) % 2][0:rows], ACT.Exp, bias=bias)\
                            .then_inc(l2_p, 1)

            for t in range(NT):
                act.wait_ge(to_act, 3 + t)
                act.activation(big2[:, t, :], big[:, t, :], ACT.Gelu).then_inc(from_act, 1)

            with act.Fori(0, B // 2) as i:
                for p in range(2):
                    b = 2 * i + p
                    for t in range(KT):
                        n = KT * b + t
                        act.wait_ge(l3_s, n + 1)
                        act.wait_ge(l3_pv, n + 1)
                        act.activation(p3[t % 2].rearrange("p (k h) q -> p k (h q)", k=2),
                                       ps[0:KP, 2 * (t % 2):2 * (t % 2) + 2, 0:8 * S], ACT.Exp).then_inc(l3_p, 1)

            act.wait_ge(l3_done, 1)
            act.wait_ge(ex_ld[0], 16 * (E1 // G1 // 2) + 16)
            act.copy(wh3[0][:, 0, :], wex[0][:, 0:2 * FF]).then_inc(ex_hi, 1)

            def split_hi3(e, p, loads):
                act.wait_ge(ex_ld[p], 16 * (E1 // G1 // 2) + 16 * loads)
                if not isinstance(e, int) or e > 1:
                    act.wait_ge(ex_gu, E1 + 4 * (e - 1))
                act.copy(wh3[p][:, 0, :], wex[p][:, 0:2 * FF]).then_inc(ex_hi, 1)

            def gelu3(e, p, loads, more=True):
                for c in range(4):
                    act.wait_ge(ex_gu, E1 + 4 * e + c + 1)
                    act.activation(exs[c % 2], ps[0:D, 2 + 2 * (c % 2), 0:N], ACT.Gelu).then_inc(ex_act, 1)
                    if c == 0 and more:
                        split_hi3(e + 1, 1 - p, loads)

            gelu3(0, 0, 1)
            act.wait_ge(to_act, 7)
            act.activation(sm8[:, 0], sm8[:, 7], ACT.Exp).then_inc(from_act, 1)
            gelu3(1, 1, 2)
            with act.Fori(1, E3 // 2 - 1) as i:
                for p in range(2):
                    gelu3(2 * i + p, p, i + 1 + p)
            gelu3(E3 - 2, 0, E3 // 2)
            gelu3(E3 - 1, 1, None, more=False)


        @block.gpsimd
        def _(pool):
            for p in range(2):
                pool.nop().then_inc(st[p], 96)
            pool.nop().then_inc(ex_acc, 2)
            ch = Chain(pool, pool_s)
            for p in range(2):
                ch.step(pool.memset(v3[p], 0.0))
            ch.sync()
            for p in range(2):
                blocks = v3[p].rearrange("p j (g c) -> p j g c", c=32)
                pool.memset(blocks[:, :, 0:4, 24:25], 1.0).then_inc(v3_ones, 1)
                pool.memset(blocks[:, :, 4:6, 16:17], 1.0).then_inc(v3_ones, 1)
            pool.wait_ge(ld_a, A_LOADS * 16)

            with pool.Fori(0, B // 2) as i, ch.loop(i, 2 * 3, B // 2):
                for p in range(2):
                    b = 2 * i + p
                    pool.wait_ge(c_hat, b + 1)
                    ch.link(pool.tensor_tensor(cln[p], cln[p], spread("L2_xw", KP, KT), ALU.mult))
                    pool.tensor_tensor(cln[p], cln[p], spread("L2_xb", KP, KT), ALU.add).then_inc(c_lned, 1)
                    pool.wait_ge(l0_w, b + 1)
                    pool.wait_ge(acc_full, b + 1)
                    ch.step(pool.tensor_copy(rhs0[:, :, D:D + 1], em[:, bass.ds(b, 1), :].rearrange("p o j -> p (o j)")
                                             .unsqueeze(2)))
                    ch.step(pool.tensor_copy(rhs0[:, :, D + 1:D + 2], em2[:, bass.ds(b, 1), :]
                                             .rearrange("p o j -> p (o j)").unsqueeze(2)))
                    pool.tensor_tensor(rhs0[:, :, 0:D], c_in[p], sm[:, 11, 0:KT].unsqueeze(2)
                                       .broadcast_to([KP, KT, D]), ALU.mult).then_inc(l0_rhs, 1)
                    pool.wait_ge(l0_kn, b + 2)
                    pool.tensor_tensor(kn, kn, spread("L0_b", KP, KT), ALU.add).then_inc(l0_kaff, 1)

            rs = [0]

            def rsqrt(n=1):
                for _ in range(n):
                    rs[0] += 1
                    pool.wait_ge(ln_var, rs[0])
                    pool.tensor_tensor(lnrs, lnve, nhalf[0:TT, 0:NT], ALU.pow).then_inc(ln_rstd, 1)

            rsqrt(2)

            def key_blocks(i):
                for e in range(2):
                    at = (2 * i + e) * S
                    ins = pool.tensor_tensor(kblk[i % 2][:, e], k1T[:, at:at + S].unsqueeze(1)
                                             .broadcast_to([D, 16, S]), cs("hmask").unsqueeze(2)
                                             .broadcast_to([D, 16, S]), ALU.mult)
                    if e == 0:
                        ch.link(ins)
                ins.then_inc(l1_kq, 1)

            pool.wait_ge(l1_k, 1)
            key_blocks(0)
            key_blocks(1)
            rsqrt()
            rsqrt()
            rsqrt()

            for i in range(2, NT):
                pool.wait_ge(l1_s, i - 1)
                key_blocks(i)

            def add_expert(e, p):
                pool.wait_ge(ex_w, e + 3)
                pool.tensor_tensor(y2, y2, big[:, :, D * p:D * p + D], ALU.add).then_inc(ex_acc, 1)

            rsqrt()
            ch.link(pool.memset(y2, 0.0))
            with pool.Fori(0, E1 // 2) as i:
                for p in range(2):
                    e = 2 * i + p
                    pool.wait_ge(ex_acc, e + 2)
                    add_expert(e, p)
            rsqrt(2)
            pool.memset(qT2, 0.0).then_inc(l2_zero, 1)
            rs[0] += 1
            pool.wait_ge(ln_var, rs[0])
            pool.tensor_tensor(qss[:, 1, :], qss[:, 1, :], nhalf[0:TT, :], ALU.pow).then_inc(ln_rstd, 1)
            rsqrt()
            rsqrt(2)
            rsqrt()

            pool.wait_ge(l3_free, 2)
            with pool.Fori(0, B) as b:
                pool.tensor_tensor(qst3[:, bass.ds(b, 1)].rearrange("p o g h q -> p (o g) h q"),
                                   q3[:, :, bass.ds(b * S, S)].unsqueeze(2).broadcast_to([D, 4, 4, S]),
                                   gm4.unsqueeze(1).unsqueeze(3).broadcast_to([D, 4, 4, S]), ALU.mult)\
                    .then_inc(l3_q, 1)

            rsqrt()
            ch.link(pool.memset(y2, 0.0))
            with pool.Fori(0, E3 // 2) as i:
                for p in range(2):
                    e = E1 + 2 * i + p
                    pool.wait_ge(ex_acc, e + 2)
                    add_expert(e, p)

        @block.vector
        def _(dve):
            ch = Chain(dve, dve_s)
            product_in, act_in = Count(dve, product), Count(dve, from_act)
            rstd_in = Count(dve, ln_rstd)

            def tt(out, a, b, op):
                return dve.tensor_tensor(out, a, b, op)

            def over(col, shape):
                return col.unsqueeze(2).broadcast_to(shape)

            def signal(s, after=None):
                ch.sync()
                if after:
                    dve.wait_ge(operand, after)
                dve.nop().then_inc(s, 1)

            def layernorm(src, dst, eps, gain=None, bias=None):
                for t in range(NT):
                    ch.step(dve.bn_stats(lnst[:, t, :], src[:, t, :]))
                ch.sync()
                for t in range(NT):
                    ch.step(dve.bn_aggr(lnmv[:, t, :], lnst[:, t, :]))
                ch.sync()
                dve.tensor_scalar(lnve, lnmv[:, :, 1], eps, None, ALU.add).then_inc(ln_var, 1)
                if gain:
                    for t in range(NT):
                        ch.step(dve.scalar_tensor_tensor(dst[:, t, :], src[:, t, :], lnmv[:, t, 0:1],
                                                         spread(gain)[:, t, :], ALU.subtract, ALU.mult))
                    ch.sync()
                rstd_in.next()
                for t in range(NT):
                    if gain:
                        ch.step(dve.scalar_tensor_tensor(dst[:, t, :], dst[:, t, :], lnrs[:, t:t + 1],
                                                         spread(bias)[:, t, :], ALU.mult, ALU.add))
                    else:
                        ch.step(dve.tensor_scalar(dst[:, t, :], src[:, t, :], lnmv[:, t, 0:1], lnrs[:, t:t + 1],
                                                  ALU.subtract, ALU.mult))
                ch.sync()

            def residual(k, src):
                ch.link(dve.scalar_tensor_tensor(x[:, :, :], src, tg[0:TT, k:k + 1], x[:, :, :],
                                                 ALU.mult, ALU.add))

            def turned(dst, k):
                product_in.next()
                dve.tensor_copy(dst, ps[0:D, k, 0:N]).then_inc(operand, 1)

            def quantise(src, tmp, dst, scales, ffn=None):
                if ffn == 1:
                    for t in range(NT):
                        act_in.next()
                        ch.step(dve.tensor_reduce(acol[:, 0, t:t + 1], src[:, t, :], AX.X, ALU.max,
                                                  apply_absolute_value=True))
                    ch.sync()
                else:
                    ch.link(dve.tensor_reduce(acol[:, 0, :], src, AX.X, ALU.max, apply_absolute_value=True))
                ch.link(dve.tensor_scalar(acol[:, 0, :], acol[:, 0, :], 1e-5, None, ALU.max))
                ch.link(dve.reciprocal(acol[:, 1, :], acol[:, 0, :]))
                ch.link(dve.tensor_scalar(acol[:, 1, :], acol[:, 1, :], 127.0, None, ALU.mult))
                for row, m in scales:
                    ch.step(dve.tensor_scalar(acol[:, row, :], acol[:, 0, :], 1.0 / 127.0, mw[0:TT, m:m + 1],
                                              ALU.mult, ALU.mult))
                for t in range(NT):
                    ch.step(dve.tensor_scalar(tmp[:, t, :], src[:, t, :], acol[:, 1, t:t + 1], MAGIC,
                                              ALU.mult, ALU.add))
                ch.sync()
                ch.link(dve.tensor_scalar(tmp, tmp, MAGIC, -128.0, ALU.subtract, ALU.max))
                if ffn is None:
                    dve.tensor_scalar(dst, tmp, 127.0, None, ALU.min).then_inc(operand, 1)
                    return
                for t in range(NT + 1):
                    if t < NT:
                        dve.tensor_scalar(dst[:, t, :], tmp[:, t, :], 127.0, None, ALU.min).then_inc(h_rows, 1)
                    if t:
                        dve.wait_ge(h_turned, NT * ffn + t)
                        dve.tensor_copy(hqT[:, :, TT * (t - 1):TT * t], ps[0:D, 3 + t, 0:256].bitcast(BF16)[:, 0:N]
                                        .rearrange("p (c n) -> p c n", c=4)).then_inc(h_cols, 1)

            dve.nop().then_inc(d_free, 3)
            dve.nop().then_inc(sq_used, SQ)
            dve.nop().then_inc(acc_used, 2)
            dve.nop().then_inc(l0_kn, 1)
            dve.nop().then_inc(l2_sc, 2)
            dve.nop().then_inc(l2_done, 1)
            dve.nop().then_inc(l2_pv, 2)
            dve.nop().then_inc(l3_mxd, 3)
            dve.nop().then_inc(l3_pv, 2)
            dve.nop().then_inc(l3_o, 1)
            dve.nop().then_inc(ex_h, 1)
            dve.nop().then_inc(ex_w, 2)
            dve.nop().then_inc(acc_full, 1)
            dve.wait_ge(ld_a, A_LOADS * 16)
            ch.step(tt(em2, em, em, ALU.mult))
            ch.link(dve.tensor_reduce(colv, w_l0, AX.X, ALU.add))
            ch.link(dve.tensor_scalar(colv, colv, 1.0 / D, None, ALU.mult))
            ch.step(tt(w_l0, w_l0, over(colv, [D, 2, D]), ALU.subtract))
            ch.link(dve.tensor_copy(w_k2h[:, 0, :], w_k2))
            ch.step(tt(w_k2h[:, 1, :], w_k2, w_k2h[:, 0, :], ALU.subtract))
            signal(a_ready)

            def scales_and_masks():
                dve.wait_ge(ld_w, N_LOADS * 16)
                dve.tensor_reduce(mw, wraw, AX.X, ALU.add, apply_absolute_value=True).then_inc(wsum_in, 1)
                ch.step(dve.tensor_copy(ident_h, ident))
                ch.step(dve.tensor_copy(gm4, cs("gmask")))
                ch.link(tt(qks[:, 0, :], qks[:, 0, :], qks[:, 1, :], ALU.mult))
                ch.link(dve.tensor_reduce(lbias, qks[:, 0, :], AX.X, ALU.max, apply_absolute_value=True))
                ch.link(dve.tensor_scalar(lbias, lbias, -8.0, None, ALU.mult))
                ch.link(dve.tensor_copy(kbias, kmask))
                ch.link(dve.tensor_scalar(kbias, kbias, -1.0, -NEG, ALU.add, ALU.mult))
                ch.link(dve.tensor_scalar(kbias, kbias, lbias[0:KP, 0:1], None, ALU.add))
                dve.wait_ge(wsum, 1)
                ch.link(dve.tensor_scalar(mw, ps[0:D, 7, 0:5], 1.0 / (D * FF), 1e-5, ALU.mult, ALU.max))
                ch.link(dve.reciprocal(wscale, mw))
                for m in range(5):
                    ch.step(dve.tensor_scalar(wraw[:, m, :], wraw[:, m, :], wscale[:, m:m + 1], MAGIC,
                                              ALU.mult, ALU.add))
                ch.sync()
                ch.link(dve.tensor_scalar(wraw, wraw, MAGIC, -1.0, ALU.subtract, ALU.max))
                dve.tensor_scalar(wquant, wraw, 1.0, None, ALU.min).then_inc(w_ready, 1)

            def l0_take(b, p):
                dve.wait_ge(acc_full, b + 2)
                dve.tensor_copy(kv_all[:, bass.ds(b, 1), :].rearrange("p o n -> p (o n)"),
                                ps[0:D, 6 + p, 0:D + 2]).then_inc(acc_used, 1)

            def l2_norms(turn, first_use):
                for j in range(KT):
                    dve.wait_ge(a_free, a_uses(turn) + 3 + first_use + j + 1)
                    dve.tensor_reduce(rn[:, bass.ds(turn - 1, 1), j, :].rearrange("p o h -> p (o h)"),
                                      sqk[:, j % SQ, :].rearrange("p (h d) -> p h d", h=H8), AX.X, ALU.add)\
                        .then_inc(sq_used, 1)

            def statistics(b, p, loads):
                dve.wait_ge(ld_c[p], 32 * loads)
                for j in range(KT):
                    ch.step(dve.bn_stats(stat[:, j, :], c_in[p][:, j, :]))
                ch.sync()
                n = KT
                ch.step(tt(sm[:, 0, 0:n], stat[:, :, 1], stat[:, :, 4], ALU.add))
                ch.step(tt(sm[:, 1, 0:n], stat[:, :, 1], stat[:, :, 4], ALU.subtract))
                ch.link(tt(sm[:, 2, 0:n], stat[:, :, 2], stat[:, :, 5], ALU.add))
                ch.step(dve.tensor_scalar(sm[:, 2, 0:n], sm[:, 2, 0:n], 1.0 / D, 1e-5, ALU.mult, ALU.add))
                ch.step(dve.tensor_scalar(sm[:, 3, 0:n], sm[:, 0, 0:n], 0.5, None, ALU.mult))
                ch.link(tt(sm[:, 1, 0:n], sm[:, 1, 0:n], sm[:, 1, 0:n], ALU.mult))
                dve.scalar_tensor_tensor(sm[:, 4, 0:n], sm[:, 1, 0:n], 0.25, sm[:, 2, 0:n],
                                         ALU.mult, ALU.add).then_inc(c_var, 1)

            def context(b, p, loads, first=False, more=True):
                n = KT
                dve.wait_ge(c_sd, b + 1)
                ch.link(dve.reciprocal(sm[:, 6, 0:n], sm[:, 5, 0:n]))
                dve.wait_ge(st[p], 96 * loads)
                for j in range(KT):
                    ins = dve.tensor_scalar(cln[p][:, j, :], c_in[p][:, j, :], sm[:, 3, j:j + 1],
                                            sm[:, 6, j:j + 1], ALU.subtract, ALU.mult)
                    if j < KT - 1:
                        ch.step(ins)
                ins.then_inc(c_hat, 1)
                if not first:
                    l0_take(b - 1, 1 - p)
                for u in range(3):
                    dve.wait_ge(k_hi_ready, 3 * b + u + 1)
                    tt(k_lo[p][:, 500 * u:500 * u + 500], ps[0:D, 3 + u, 0:500],
                       k_hi[p][:, 500 * u:500 * u + 500], ALU.subtract).then_inc(d_free, 1)
                if more:
                    statistics(b + 1, 1 - p, loads + p)
                dve.wait_ge(a_free, a_uses(b) + 3 + 9)
                ch.link(dve.tensor_reduce(sm[:, 10, :].rearrange("p (j a) -> p j a", a=2), sq0, AX.X, ALU.add))
                dve.tensor_scalar(sm[:, 7, :], sm[:, 10, :], 1.0 / D, 1e-6, ALU.mult, ALU.add)\
                    .then_inc(l0_var, 1)
                dve.wait_ge(l0_sd, b + 1)
                ch.link(dve.reciprocal(sm[:, 9, :], sm[:, 8, :]))
                r = sm[:, 9, :].rearrange("p (j a) -> p j a", a=2)
                tt(sm[:, 11, 0:n], r[:, :, 1], em2[:, bass.ds(b, 1), :].rearrange("p o j -> p (o j)"), ALU.mult)\
                    .then_inc(l0_w, 1)
                for j in range(KT):
                    ins = dve.scalar_tensor_tensor(kn[:, j, :], kraw[:, j, :], r[:, j, 0:1],
                                                   spread("L0_g", KP, 1)[:, 0, :], ALU.mult, ALU.mult)
                    if j < KT - 1:
                        ch.step(ins)
                ins.then_inc(l0_kn, 1)
                if first:
                    scales_and_masks()
                else:
                    l2_norms(b, 9)
                dve.wait_ge(l0_kaff, b + 1)
                dve.tensor_scalar(kpr, kn, 0.0, 1e-6, ALU.max, ALU.add).then_inc(l0_kp, 1)
                for u in range(3):
                    dve.wait_ge(cln_hi, 3 * b + u + 1)
                    tt(clnT[p][:, 1, 500 * u:500 * u + 500], ps[0:D, 3 + u, 0:500],
                       clnT[p][:, 0, 500 * u:500 * u + 500], ALU.subtract).then_inc(d_free, 1)

            statistics(0, 0, 1)
            context(0, 0, 1, first=True)
            with dve.Fori(0, B // 2 - 1) as i, ch.loop(i, 2 * 43, B // 2 - 1):
                context(2 * i + 1, 1, i + 1)
                context(2 * i + 2, 0, i + 2)
            context(B - 1, 1, B // 2, more=False)
            l0_take(B - 1, 1)
            l2_norms(B, 0)
            dve.wait_ge(acc_used, B + 2)
            dve.wait_ge(sq_used, KT * B + SQ)
            rn_flat = rn[:, :, :, :].rearrange("p b t h -> p (b t h)")
            dve.tensor_scalar(rn_flat, rn_flat, 1e-24, None, ALU.max).then_inc(rn_sq, 1)
            dve.nop().then_inc(ctx_done, 1)
            dve.nop().then_inc(operand, 1)

            for p in range(2):
                dve.wait_ge(st[p], 96 * (B // 2 + 1))
            ch.link(dve.memset(nhalf, -0.5))
            layernorm(x, z, 1e-5)
            product_in.next()
            dve.tensor_copy(kvt.rearrange("p b n -> p (b n)"), ps[0:D, 0:2, :].rearrange("p k n -> p (k n)"))\
                .then_inc(operand, 1)
            signal(operand, after=OPERAND["kvt"])
            product_in.next()
            ch.link(tt(kvm, ps[0:D, 2:4, :].rearrange("p k (b n) -> p (k b) n", b=4), spread("L0_g", D, B), ALU.mult))
            for b in range(B):
                ch.step(dve.scalar_tensor_tensor(kvm[:, b, :], spread("L0_b", D, 1)[:, 0, :], kv_all[:, b, D + 1:D + 2],
                                                 kvm[:, b, :], ALU.mult, ALU.add))
            ch.sync()
            blk = cs("blk").unsqueeze(1).broadcast_to([D, B, D])
            ch.step(tt(kvm, kvm, blk, ALU.mult))
            ch.step(tt(ksm, cs("hmask").unsqueeze(1).broadcast_to([D, B, 16]),
                       kv_all[:, :, D:D + 1].broadcast_to([D, B, 16]), ALU.mult))
            turned(xT, 4)
            product_in.next()
            ch.link(dve.tensor_copy(y.rearrange("p t n -> p (t n)"), ps[0:TT, 5, :]))
            layernorm(y, y2, 1e-6, "L0_g", "L0_b")
            dve.tensor_scalar(y2, y2, 0.0, 1e-6, ALU.max, ALU.add).then_inc(operand, 1)
            turned(xT, 4)
            product_in.next()
            ch.link(dve.tensor_scalar(rd0, ps[0:S, 5, 0:D].rearrange("p (b h) -> p b h", b=B), 1e-6, None, ALU.add))
            ch.link(dve.reciprocal(rd0, rd0))
            tt(at0.rearrange("p b (h e) -> p (b h) e", h=16), ps[0:S, 6:8, :].rearrange("p k (h e) -> p (k h) e", e=8),
               over(rd0.rearrange("p b h -> p (b h)"), [S, D, 8]), ALU.mult).then_inc(l0_att, 1)
            dve.wait_ge(l1_kv, 3)
            ch.step(tt(xT3, ps[0:D, 0, 0:N], cs("sink"), ALU.mult))
            ch.link(tt(k1T, k1T, cs("cosk"), ALU.mult))
            tt(k1T, k1T, xT3, ALU.add).then_inc(l1_k, 1)
            ch.step(dve.memset(v1[:, :, :, HD16:HD16 + 1], 1.0))
            ch.step(dve.memset(q1T[:, N:N + 8], 0.0))
            turned(xT2, 4)
            product_in.next()
            ch.link(tt(y, ps[0:TT, 0, :].rearrange("p (t n) -> p t n", t=NT), spread("L0_db"), ALU.add))
            layernorm(y, y, 1e-6, "L0_g", "L0_b")
            act_in.next()
            residual(0, y)

            layernorm(x, z, 1e-5)
            quantise(z, y, zq, ((2, 0), (3, 1)))
            product_in.next()
            dve.tensor_copy(zqT, ps[0:D, 0, 0:256].bitcast(BF16)[:, 0:N]).then_inc(operand, 1)
            product_in.next()
            for t in range(NT):
                act_in.next()
                ch.step(dve.scalar_tensor_tensor(big2[:, t, :], ps[0:TT, 4 + t, :], acol[:, 3, t:t + 1],
                                                 big[:, t, :], ALU.mult, ALU.mult))
            ch.sync()

            def down(scale_row, bias=None):
                product_in.next()
                for t in range(NT):
                    src = ps[0:TT, 2, D * t:D * t + D]
                    if bias:
                        ch.step(dve.scalar_tensor_tensor(y[:, t, :], src, acol[:, scale_row, t:t + 1],
                                                         spread(bias)[:, t, :], ALU.mult, ALU.add))
                    else:
                        ch.step(dve.tensor_scalar(y[:, t, :], src, acol[:, scale_row, t:t + 1], None, ALU.mult))
                ch.sync()

            quantise(big2, big3, hq, ((4, 2),), ffn=0)
            down(4)
            residual(4, y)

            layernorm(x, z, 1e-5)
            signal(operand)
            turned(xT, 0)
            product_in.next()
            q1 = q1T[:, 0:N]
            dve.tensor_scalar(q1, ps[0:D, 1, 0:N], w_col1[:, 0:1], None, ALU.add).then_inc(operand, 1)
            product_in.next()
            ch.step(tt(xT3, ps[0:D, 2, 0:N], cs("sinq"), ALU.mult))
            ch.link(tt(q1, q1, cs("cosq"), ALU.mult))
            tt(q1, q1, xT3, ALU.add).then_inc(operand, 1)

            def shift1(i):
                sc = sc1[i % 2]
                dve.wait_ge(l1_s, i + 1)
                if i > 1:
                    dve.wait_ge(l1_p, i - 1)
                tt(sc.rearrange("p (k h) s -> p k h s", k=2), ps[:, 0:2, 0:8 * S]
                   .rearrange("p k (h s) -> p k h s", h=8),
                   cs("causal").unsqueeze(1).unsqueeze(1).broadcast_to([D, 2, 8, S]), ALU.add).then_inc(l1_sr, 1)
                dve.wait_ge(l1_sr, i + 1)
                ch.link(dve.tensor_reduce(m1[:, 0, :], sc, AX.X, ALU.max))
                tt(sc, sc, over(m1[:, 0, :], [D, 16, S]), ALU.subtract).then_inc(l1_m, 1)

            def normalise1(i):
                dve.wait_ge(l1_o, i + 1)
                if i:
                    dve.wait_ge(l1_ot, i)
                src = ps[:, 6, 0:H16 * (HD16 + 1)].rearrange("p (h d) -> p h d", h=H16)
                ch.link(dve.reciprocal(m1[:, 1, :], src[:, :, HD16]))
                tt(o1.rearrange("p (h d) -> p h d", h=H16), src[:, :, 0:HD16],
                   over(m1[:, 1, :], [D, H16, HD16]), ALU.mult).then_inc(l1_on, 1)

            shift1(0)
            shift1(1)
            for i in range(NT):
                if i + 2 < NT:
                    shift1(i + 2)
                if i == 2:
                    dve.wait_ge(rn_sd, 1)
                    ch.step(dve.reciprocal(rn_flat, rn_flat))
                normalise1(i)
            product_in.next()
            ch.link(tt(y, ps[0:TT, 0, :].rearrange("p (t n) -> p t n", t=NT), spread("L1_ob"), ALU.add))
            residual(1, y)

            def pick(v, n, k, low):
                rank = cs("rank", TT)[:, 0:n].unsqueeze(1).broadcast_to([TT, NT, n])
                src = v[:, k]
                ch.link(dve.tensor_reduce(acol[:, 0, :], src, AX.X, ALU.max))
                ch.link(tt(v[:, 2], src, over(acol[:, 0, :], [TT, NT, n]), ALU.is_equal))
                ch.link(tt(v[:, 2], v[:, 2], rank, ALU.mult))
                ch.link(dve.tensor_reduce(acol[:, 1, :], v[:, 2], AX.X, ALU.max))
                ch.link(tt(v[:, 3 + k], v[:, 2], over(acol[:, 1, :], [TT, NT, n]), ALU.is_equal))
                if k == 0:
                    ch.link(dve.scalar_tensor_tensor(v[:, 1], v[:, 3], low, src, ALU.mult, ALU.add))
                else:
                    ch.link(tt(v[:, 5], v[:, 3], v[:, 4], ALU.add))

            layernorm(x, z, 1e-5)
            signal(operand)
            turned(xT, 0)
            product_in.next()
            dve.tensor_copy(sm16[:, 0], ps[0:TT, 1, 0:64].rearrange("p (t n) -> p t n", t=NT)).then_inc(to_act, 1)

            def hidden1(e, p):
                dve.wait_ge(ex_act, e + 1)
                tt((xT2, xT3)[p], ps[0:D, 3 + 2 * p, 0:N], exs[p], ALU.mult).then_inc(ex_h, 1)

            def weigh(e, p, weight, first):
                dve.wait_ge(ex_dn, first + e + 1)
                dve.wait_ge(ex_acc, first + e + 1)
                tt(big[:, :, D * p:D * p + D], ps[0:TT, 6 + p, :].rearrange("p (t n) -> p t n", t=NT),
                   weight.broadcast_to([TT, NT, D]), ALU.mult).then_inc(ex_w, 1)

            hidden1(0, 0)
            dve.wait_ge(to_act, 1)
            pick(sm16, 16, 0, NEG)
            hidden1(1, 1)
            pick(sm16, 16, 1, NEG)
            dve.wait_ge(ld_m, 5 * 16)
            ch.link(tt(qk_col[:, 0:1], qk_col[:, 0:1], qk_col[:, 1:2], ALU.mult))
            ch.step(dve.tensor_scalar(w_kT2, w_kT2, qk_col[:, 0:1], 8.0, ALU.mult, ALU.mult))
            act_in.next()
            ch.step(tt(wts[:, :, 0:16], sm16[:, 5], sm16[:, 6], ALU.mult))
            ch.link(dve.memset(wts[:, :, 16:E1], 1.0))

            weigh(0, 0, wts[:, :, 0:1], 0)
            hidden1(2, 0)
            weigh(1, 1, wts[:, :, 1:2], 0)
            with dve.Fori(1, E1 // 2 - 1) as i:
                for p in range(2):
                    e = 2 * i + p
                    hidden1(e + 1, 1 - p)
                    weigh(e, p, wts[:, :, bass.ds(e, 1)], 0)
            hidden1(E1 - 1, 1)
            weigh(E1 - 2, 0, wts[:, :, E1 - 2:E1 - 1], 0)
            weigh(E1 - 1, 1, wts[:, :, E1 - 1:E1], 0)
            dve.wait_ge(ex_acc, E1 + 2)
            residual(5, y2)

            layernorm(x, z, 1e-5)
            layernorm(z, y, 1e-5, "L2_lw", "L2_lb")
            dve.nop().then_inc(lat_ready, 1)
            dve.nop().then_inc(operand, 1)
            for p in range(2):
                ch.step(dve.memset(cln_s[p][:, :, D:D + 1], 1.0))
            product_in.next()
            dve.tensor_copy(xT, ps[0:D, 0, 0:N]).then_inc(operand, 1)
            dve.wait_ge(operand, OPERAND["latentsT"])
            ch.link(dve.tensor_copy(latT[:, 0, :], xT))
            ch.step(tt(latT[:, 1, :], xT, latT[:, 0, :], ALU.subtract))
            signal(lat_ready)
            product_in.next(4)
            for t in range(NT):
                act_in.next()
                ch.step(dve.tensor_reduce(qss[:, 0, H8 * t:H8 * t + H8],
                                          big2[:, t, :].rearrange("p (h d) -> p h d", h=H8), AX.X, ALU.add))
            ch.sync()
            dve.tensor_scalar(qss[:, 0, :], qss[:, 0, :], 1e-24, None, ALU.max).then_inc(to_act, 1)
            act_in.next()
            ch.link(dve.reciprocal(qss[:, 2, :], qss[:, 2, :]))
            bigf = big.rearrange("p t (h d) -> p (t h) d", h=H8)
            tt(bigf, ps[0:TT, 0:4, :].rearrange("p t (h d) -> p (t h) d", h=H8),
               over(qss[:, 2, :], [TT, NT * H8, HD8]), ALU.mult).then_inc(operand, 1)
            product_in.next(2)
            dve.wait_ge(l2_zero, 1)
            ch.step(dve.tensor_copy(qT2[0:64, 0::2, :], ps[0:64, 0:4, 0:N]))
            act_in.next(5)
            signal(operand)
            for h in range(H8):
                if h % 4 == 0:
                    product_in.next()
                dve.wait_ge(qt_hi, h + 1)
                ch.step(tt(qtT[:, 1, h, :], ps[0:D, (4 + h) % 8, 0:N], qtT[:, 0, h, :], ALU.subtract))
            signal(operand)

            def scale2(b, p, t):
                n = (KT + 1) * b + t
                rows = KP if t < KT else S
                norm = (rn[:, bass.ds(b, 1), t, :] if t < KT else rnl[:, bass.ds(b, 1), :])\
                    .rearrange("p o h -> p (o h)")
                dve.wait_ge(l2_s, n + 1)
                dve.wait_ge(l2_p, n + 1)
                tt(sscl[(t + p) % 2][0:rows].rearrange("p (h q) -> p h q", h=H8),
                   ps[0:rows, (t + p) % 2, 0:N].rearrange("p (h q) -> p h q", h=H8),
                   over(norm, [rows, H8, S]), ALU.mult).then_inc(l2_sc, 1)

            def normalise2(b, p):
                dve.wait_ge(l2_pv, (KT + 1) * (b + 1) + 2)
                o012 = ps[0:TT, 4 + 2 * p, 0:387].rearrange("p (c n) -> p c n", c=3)
                o3 = ps[0:TT, 5 + 2 * p, 0:D + 1]
                ch.step(dve.reciprocal(rden[:, 0:3], o012[:, :, D]))
                ch.link(dve.reciprocal(rden[:, 3:4], o3[:, D:D + 1]))
                ch.step(tt(onrm[:, 0:3, :], o012[:, :, 0:D], over(rden[:, 0:3], [TT, 3, D]), ALU.mult))
                ch.sync()
                dve.tensor_scalar(onrm[:, 3, :], o3[:, 0:D], rden[:, 3:4], None, ALU.mult).then_inc(l2_on, 1)

            def features2(b):
                dve.wait_ge(l2_t, b + 1)
                dve.tensor_copy(ctxT[:, :, bass.ds(b * S, S)],
                                ps[0:D, 2, 0:N].rearrange("p (h q) -> p h q", h=H8)).then_inc(l2_done, 1)

            def batch2(b, p, first=False):
                for t in range(KT + 1):
                    if t == KT and first:
                        dve.wait_ge(ld_rn, 16)
                    scale2(b, p, t)
                    if first and t == 1:
                        ch.link(dve.tensor_reduce(qss[:, 1, :], big3.rearrange("p t (h d) -> p (t h) d", h=H8),
                                                  AX.X, ALU.add))
                        dve.tensor_scalar(qss[:, 1, :], qss[:, 1, :], 1e-24, None, ALU.max).then_inc(ln_var, 1)
                    if not first and t == 3:
                        normalise2(b - 1, 1 - p)
                    if not first and t == 6:
                        features2(b - 1)

            batch2(0, 0, first=True)
            rstd_in.next()
            batch2(1, 1)
            with dve.Fori(0, B // 2 - 1) as i, ch.loop(i, 2 * 3, B // 2 - 1):
                for p in range(2):
                    batch2(2 * i + 2 + p, p)
            normalise2(B - 1, 1)
            features2(B - 1)
            product_in.next()
            ch.link(dve.tensor_copy(y.rearrange("p t n -> p (t n)"), ps[0:TT, 0, :]))
            signal(l3_free)
            layernorm(y, y, 1e-5, "L2_ow", "L2_ob")
            residual(2, y)

            layernorm(x, z, 1e-5)
            layernorm(z, z, 1e-5, "L2f_g", "L2f_be")
            quantise(z, y, zq, ((2, 3),))
            product_in.next()
            dve.tensor_copy(zqT, ps[0:D, 0, 0:256].bitcast(BF16)[:, 0:N]).then_inc(operand, 1)
            product_in.next()
            for t in range(NT):
                dve.scalar_tensor_tensor(big[:, t, :], ps[0:TT, t, :], acol[:, 2, t:t + 1], b1v[0:TT, :],
                                         ALU.mult, ALU.add).then_inc(to_act, 1)
            quantise(big2, big3, hq, ((4, 4),), ffn=1)
            down(4, "L2f_b2")
            residual(6, y)

            layernorm(x, z, 1e-5)
            signal(operand)
            turned(xT, 0)
            product_in.next()
            ch.link(dve.tensor_scalar(xT2, ps[0:D, 1, 0:N], float(D) ** -0.5, None, ALU.mult))
            ch.link(dve.tensor_copy(q_hi, xT2))
            tt(q_lo, xT2, q_hi, ALU.subtract).then_inc(operand, 1)
            product_in.next()
            ch.step(dve.tensor_copy(q3, ps[0:D, 0:4, 0:N]))
            signal(l3_free)

            def maxima(bn):
                for u in range(24):
                    dve.wait_ge(l3_mx, 24 * bn + u + 1)
                    dve.tensor_reduce(mx3[:, u % 8, u // 8:u // 8 + 1], ps[0:TT, MAX_BANKS[u % 3], 0:500], AX.X, ALU.max)\
                        .then_inc(l3_mxd, 1)
                dve.wait_ge(l3_mxd, 24 * bn + 27)
                dve.tensor_reduce(m3, mx3, AX.X, ALU.max, negate=True).then_inc(l3_dg, 1)
                dve.wait_ge(l3_sh, bn + 1)
                tt(qst3[0:8, bass.ds(bn, 1)].rearrange("p o g (a h) q -> p (o g a) (h q)", a=2),
                   ps[0:8, MAX_BANKS[0], 0:TT].unsqueeze(1).broadcast_to([8, 8, TT]),
                   over(ident[0:8, 0:8], [8, 8, TT]), ALU.mult).then_inc(l3_row, 1)

            def outputs(b):
                dve.wait_ge(l3_pv, KT * (b + 1) + 2)
                at_b = bass.ds(b, 1)
                ch.link(dve.tensor_copy(oA[:, at_b].rearrange("p o h q -> p (o h q)"), ps[0:D, 6, 0:168]))
                dve.tensor_copy(oB[:, at_b].rearrange("p o h q -> p (o h q)"), ps[0:64, 6, 168:280])\
                    .then_inc(l3_o, 1)

            maxima(0)
            with dve.Fori(0, B // 2 - 1) as i, ch.loop(i, 2 * 1, B // 2 - 1):
                for p in range(2):
                    maxima(2 * i + p + 1)
                    outputs(2 * i + p)
            maxima(B - 1)
            outputs(B - 2)
            outputs(B - 1)
            product_in.next()
            ch.link(dve.reciprocal(xT3, ps[0:D, 1, 0:N]))
            tt(xT2, ps[0:D, 0, 0:N], xT3, ALU.mult).then_inc(operand, 1)
            product_in.next()
            ch.link(tt(y, ps[0:TT, 2, :].rearrange("p (t n) -> p t n", t=NT), spread("L3_bo"), ALU.add))
            residual(3, y)

            dve.nop().then_inc(l3_done, 1)
            layernorm(x, z, 1e-5)
            signal(operand)

            def split_lo3(e, p):
                dve.wait_ge(ex_hi, e + 1)
                tt(wh3[p][:, 1, :], wex[p][:, 0:2 * FF], wh3[p][:, 0, :], ALU.subtract).then_inc(ex_split, 1)

            product_in.next()
            ch.step(dve.tensor_copy(xTh[:, 0, :], ps[0:D, 0, 0:N]))
            dve.tensor_copy(xT, ps[0:D, 0, 0:N]).then_inc(operand, 1)
            ch.sync()
            dve.wait_ge(operand, OPERAND["x3T"])
            ch.link(tt(xTh[:, 1, :], xT, xTh[:, 0, :], ALU.subtract))
            split_lo3(0, 0)
            product_in.next()
            logits = ps[0:TT, 1, 0:4 * E3].rearrange("p (t n) -> p t n", t=NT)
            ch.link(dve.tensor_reduce(acol[:, 5, :], logits, AX.X, ALU.max))
            tt(sm8[:, 7], logits, over(acol[:, 5, :], [TT, NT, E3]), ALU.subtract).then_inc(to_act, 1)

            def expert3(e, p, first=False, more=True, between=None):
                for c in range(4):
                    dve.wait_ge(ex_act, E1 + 4 * e + c + 1)
                    tt(h3[p][:, c, :], ps[0:D, 3 + 2 * (c % 2), 0:N], exs[c % 2], ALU.mult).then_inc(ex_h, 1)
                    if c == 0 and more:
                        split_lo3(e + 1, 1 - p)
                    if between and c in between:
                        between[c]()
                    if c == (3 if between else 1) and not first:
                        weigh(e - 1, 1 - p, wt3[:, :, bass.ds(e - 1, 1)], E1)

            expert3(0, 0, first=True)
            dve.wait_ge(to_act, 7)
            act_in.next()

            def weights3():
                pick(sm8, E3, 1, None)
                ch.link(tt(sm8[:, 5], sm8[:, 5], sm8[:, 0], ALU.mult))
                ch.link(dve.tensor_reduce(acol[:, 0, :], sm8[:, 5], AX.X, ALU.add))
                ch.link(dve.reciprocal(acol[:, 1, :], acol[:, 0, :]))
                ch.link(tt(wt3, sm8[:, 5], over(acol[:, 1, :], [TT, NT, E3]), ALU.mult))

            expert3(1, 1, between={1: lambda: pick(sm8, E3, 0, -4.0), 2: weights3})
            with dve.Fori(1, E3 // 2 - 1) as i:
                for p in range(2):
                    expert3(2 * i + p, p)
            expert3(E3 - 2, 0)
            expert3(E3 - 1, 1, more=False)
            weigh(E3 - 1, 1, wt3[:, :, E3 - 1:E3], E1)
            dve.wait_ge(ex_acc, E1 + E3 + 2)
            residual(7, y2)
            dve.nop().then_inc(out_ready, 1)


def kernel(**inputs):
    import concourse.bacc as bacc
    from concourse.bass_utils import run_bass_kernel_spmd

    a = {name: np.asarray(v) for name, v in inputs.items()}

    def chunks(w):
        return w.reshape(4, D, -1).transpose(1, 0, 2)

    cst, sel, pad = constants()
    wkv = a["L2_xattn_Wkv"]
    experts1 = np.concatenate([a["L1_ffn_gate_up_w"], a["L1_ffn_down_w"]], axis=2)
    shared1 = [np.concatenate([a["L1_ffn_shared_gate_w"][D * k:D * k + D].T,
                               a["L1_ffn_shared_up_w"][D * k:D * k + D].T,
                               a["L1_ffn_shared_down_w"][:, D * k:D * k + D].T], axis=1) for k in range(2)]
    io = {
        "ctx": a["ctx_1024"],
        "cst": cst,
        "sel": sel,
        "pad": pad,
        "vec": np.stack([a[n] for n in (
            "L0_xattn_ln_gamma", "L0_xattn_ln_beta", "L2_xattn_ln_x_w", "L2_xattn_ln_x_b", "L0_xattn_dense_b",
            "L1_xattn_v_b", "L1_xattn_o_b", "L2_xattn_ln_l_w", "L2_xattn_ln_l_b", "L2_xattn_ln_o_w",
            "L2_xattn_ln_o_b", "L2_ffn_b2", "L2_ffn_gamma", "L2_ffn_beta", "L3_xattn_bo")]),
        "wquant": np.stack([a["L0_ffn_w_gate"].T, a["L0_ffn_w_up"].T, chunks(a["L0_ffn_w_down"].T).reshape(D, FF),
                            a["L2_ffn_w1"].T, chunks(a["L2_ffn_w2"].T).reshape(D, FF)], axis=1),
        "L0_wk": a["L0_xattn_wk"],
        "L0_wv": a["L0_xattn_wv"],
        "L0_wq": a["L0_xattn_wq"],
        "L0_wd": a["L0_xattn_dense_w"],
        "L2_wk": wkv[:, :I2],
        "L3_wkT": a["L3_xattn_Wk"].T,
        "L3_wvT": a["L3_xattn_Wv"].T,
        "L3_wqT": a["L3_xattn_Wq"].T,
        "L3_woT": a["L3_xattn_Wo"].T,
        "L3_router": a["L3_ffn_gate_w"].T,
        "mask": a["mask_BxS2_ff1"],
        "kmask": a["mask_BxS2_bk0"],
        "qks": np.stack([a["L2_xattn_q_scale"], a["L2_xattn_k_scale"]]),
        "qk_cols": np.stack([np.tile(a["L2_xattn_q_scale"], 2), np.tile(a["L2_xattn_k_scale"], 2)], axis=1),
        "b1": a["L2_ffn_b1"],
        "gates": np.concatenate([a["g_xattn"], a["g_ffn"]]),
        "x": a["x"].reshape(N, D),
        "L1_w": np.stack([a[f"L1_xattn_{n}_w"].T for n in "qkvo"], axis=1),
        "L1_cols": np.stack([a["L1_xattn_q_b"], a["L1_xattn_k_b"]], axis=1),
        "L1_router": a["L1_ffn_router_w"].T,
        "L1_ex": np.concatenate([experts1, np.stack(shared1)]).reshape(-1, G1, D, 3 * D).transpose(0, 2, 1, 3)
        .reshape(-1, D, G1 * 3 * D),
        "L2_wkT": chunks(wkv[:, :I2].T),
        "L2_wvT": chunks(wkv[:, I2:].T),
        "L2_wo": chunks(a["L2_xattn_Wo"]),
        "L2_wq": a["L2_xattn_Wq"],
        "L3_ex": np.concatenate([
            a["L3_ffn_gate_up_w"].transpose(0, 2, 1),
            a["L3_ffn_down_w"].transpose(0, 2, 1).reshape(E3, 4, D, D).transpose(0, 2, 1, 3).reshape(E3, D, FF)],
            axis=2),
    }
    io = {name: np.ascontiguousarray(v) for name, v in io.items()}
    nc = bacc.Bacc("TRN2", target_bir_lowering=False, num_devices=1)
    aps = {name: nc.dram_tensor(f"in_{name}", v.shape, mybir.dt.from_np(v.dtype), kind="ExternalInput").ap()
           for name, v in io.items()}
    out = nc.dram_tensor("out_x", (N, D), F32, kind="ExternalOutput").ap()
    build(nc, aps, out)
    r = run_bass_kernel_spmd(nc, [{f"in_{name}": v for name, v in io.items()}], core_ids=[0])
    return r.results[0]["out_x"].reshape(B, S, D)
```
